# Optimizing a Trainium2 kernel written in Bass

```python
import numpy as np
import jax
import jax.numpy as jnp

def _softmax(x, axis=-1):
    return jax.nn.softmax(x, axis=axis)

def _gelu(x):
    return jax.nn.gelu(x, approximate=True)

def _silu(x):
    return jax.nn.silu(x)

def _sigmoid(x):
    return jax.nn.sigmoid(x)

def _layernorm(x, axis=-1, eps=1e-05):
    m = jnp.mean(x, axis=axis, keepdims=True)
    v = jnp.var(x, axis=axis, keepdims=True)
    return (x - m) / jnp.sqrt(v + eps)

def _scatter_add(tgt, idx, src, axis=0):
    return tgt.at[idx].add(src)

def _segment_sum(src, seg, n):
    return jax.ops.segment_sum(src, seg, n)
kernel_name = 'mk_xattn_seq_d2_seqx_r8_9627bb'

def setup_inputs(seed: int=0):
    np.random.seed(seed)
    _w = jnp.asarray

    def _rec_inputs():
        import jax
        import jax.numpy as jnp
        _rk = jax.random.key(seed)
        x = -0.0002928 + 1 * jax.random.normal(jax.random.fold_in(_rk, 1), (64, 64, 256), jnp.float32)
        _lenS = 64 - jax.random.randint(jax.random.fold_in(_rk, 7), (64,), 0, max(1, 64 // 4) + 1, jnp.int32)
        _lenS2 = 64 - jax.random.randint(jax.random.fold_in(_rk, 8), (64,), 0, max(1, 64 // 4) + 1, jnp.int32)
        _ctx_2048P = jax.random.normal(jax.random.fold_in(_rk, 11), (64, 16, 256), jnp.float32)
        _ctx_2048c = jax.random.dirichlet(jax.random.fold_in(_rk, 511), 0.3 * jnp.ones((16,), jnp.float32), (64, 64))
        _ctx_2048t = jnp.einsum('bsk,bkd->bsd', _ctx_2048c, _ctx_2048P)
        _ctx_2048t = _ctx_2048t * jax.lax.rsqrt(jnp.mean(jnp.square(_ctx_2048t)) + 1e-12) * 0.953939
        ctx_2048 = -1.39393e-06 + 0.999914 * (_ctx_2048t + 0.3 * jax.random.normal(jax.random.fold_in(_rk, 611), (64, 64, 256), jnp.float32))
        return (x, ctx_2048)
    x, ctx_2048 = _rec_inputs()

    def _L0_xattn_setup():
        import jax, jax.numpy as jnp
        import numpy as np
        EPS = 1e-05

        def _inorm(x):
            m = jnp.mean(x, axis=-1, keepdims=True)
            v = jnp.var(x, axis=-1, keepdims=True)
            return (x - m) * jax.lax.rsqrt(v + EPS)

        def _conv1x1(W, b, x):
            return jnp.einsum('oc,bct->bot', W, x) + b[None, :, None]
        key = jax.random.key(seed)
        ks = jax.random.split(key, 10)
        B, C, T = (4, 64, 256)
        s = 1.0 / np.sqrt(C)
        return {'x_c': jax.random.normal(ks[0], (B, C, T), jnp.float32), 'x_s': jax.random.normal(ks[1], (B, C, T), jnp.float32), 'Wn': jax.random.normal(ks[2], (C, C), jnp.float32) * s, 'bn': jax.random.normal(ks[3], (C,), jnp.float32) * s, 'Wm': jax.random.normal(ks[4], (C, C), jnp.float32) * s, 'bm': jax.random.normal(ks[5], (C,), jnp.float32) * s, 'Wl': jax.random.normal(ks[6], (C, C), jnp.float32) * s, 'bl': jax.random.normal(ks[7], (C,), jnp.float32) * s, 'Wo': jax.random.normal(ks[8], (C, C), jnp.float32) * s, 'bo': jax.random.normal(ks[9], (C,), jnp.float32) * s}
    _L0_xattn_all = _L0_xattn_setup()
    _L0_xattn_in = {k: v for k, v in _L0_xattn_all.items() if k in ('Wn', 'bn', 'Wm', 'bm', 'Wl', 'bl', 'Wo', 'bo')}
    del _L0_xattn_all

    def _L1_xattn_setup():
        import jax, jax.numpy as jnp
        import numpy as np
        B, Q, S1, S2 = (4, 32, 256, 256)
        D, H, K, F = (256, 16, 128, 1024)
        LN_EPS = 1e-05

        def _layer_norm(x, scale, offset):
            mu = jnp.mean(x, axis=-1, keepdims=True)
            var = jnp.var(x, axis=-1, keepdims=True)
            return (x - mu) * jax.lax.rsqrt(var + LN_EPS) * scale + offset

        def _cross_attention(q_in, kv_in, wq, bq, wk, bk, wv, bv, wo, bo, bias_k, bias_v):
            b, q_len, _ = q_in.shape
            t = kv_in.shape[1]
            qh = (q_in @ wq + bq).reshape(b, q_len, H, K)
            kh = (kv_in @ wk + bk).reshape(b, t, H, K)
            vh = (kv_in @ wv + bv).reshape(b, t, H, K)
            kh = jnp.concatenate([kh, jnp.broadcast_to(bias_k, (b, 1, H, K))], axis=1)
            vh = jnp.concatenate([vh, jnp.broadcast_to(bias_v, (b, 1, H, K))], axis=1)
            scale = jnp.sqrt(jnp.asarray(K, q_in.dtype))
            logits = jnp.einsum('bqhk,bthk->bhqt', qh, kh) / scale
            weights = jax.nn.softmax(logits, axis=-1)
            ctx = jnp.einsum('bhqt,bthk->bqhk', weights, vh).reshape(b, q_len, H * K)
            return ctx @ wo + bo

        def _forward(x, xf_1, xf_2, ln1_scale, ln1_offset, wq1, bq1, wk1, bk1, wv1, bv1, wo1, bo1, bias_k1, bias_v1, ln2_scale, ln2_offset, wq2, bq2, wk2, bk2, wv2, bv2, wo2, bo2, bias_k2, bias_v2, ln_mlp_scale, ln_mlp_offset, w_fc1, b_fc1, w_fc2, b_fc2):
            res = x
            h = _layer_norm(x, ln1_scale, ln1_offset)
            x = res + _cross_attention(h, xf_1, wq1, bq1, wk1, bk1, wv1, bv1, wo1, bo1, bias_k1, bias_v1)
            res = x
            h = _layer_norm(x, ln2_scale, ln2_offset)
            x = res + _cross_attention(h, xf_2, wq2, bq2, wk2, bk2, wv2, bv2, wo2, bo2, bias_k2, bias_v2)
            h = _layer_norm(x, ln_mlp_scale, ln_mlp_offset)
            h = jax.nn.gelu(h @ w_fc1 + b_fc1, approximate=False) @ w_fc2 + b_fc2
            return x + h
        key = jax.random.key(seed)
        ks = iter(jax.random.split(key, 64))

        def rn(shape, s=0.02):
            return jax.random.normal(next(ks), shape, jnp.float32) * s
        inp = {'x': rn((B, Q, D), 1.0), 'xf_1': rn((B, S1, D), 1.0), 'xf_2': rn((B, S2, D), 1.0)}
        for i in (1, 2):
            inp[f'ln{i}_scale'] = jnp.ones((D,), jnp.float32)
            inp[f'ln{i}_offset'] = jnp.zeros((D,), jnp.float32)
            inp[f'wq{i}'] = rn((D, H * K))
            inp[f'bq{i}'] = jnp.zeros((H * K,), jnp.float32)
            inp[f'wk{i}'] = rn((D, H * K))
            inp[f'bk{i}'] = jnp.zeros((H * K,), jnp.float32)
            inp[f'wv{i}'] = rn((D, H * K))
            inp[f'bv{i}'] = jnp.zeros((H * K,), jnp.float32)
            inp[f'wo{i}'] = rn((H * K, D))
            inp[f'bo{i}'] = jnp.zeros((D,), jnp.float32)
            inp[f'bias_k{i}'] = rn((1, 1, H, K))
            inp[f'bias_v{i}'] = rn((1, 1, H, K))
        inp['ln_mlp_scale'] = jnp.ones((D,), jnp.float32)
        inp['ln_mlp_offset'] = jnp.zeros((D,), jnp.float32)
        inp['w_fc1'] = rn((D, F))
        inp['b_fc1'] = jnp.zeros((F,), jnp.float32)
        inp['w_fc2'] = rn((F, D))
        inp['b_fc2'] = jnp.zeros((D,), jnp.float32)
        return inp
    _L1_xattn_all = _L1_xattn_setup()
    _L1_xattn_in = {k: v for k, v in _L1_xattn_all.items() if k in ('ln1_scale', 'ln1_offset', 'wq1', 'bq1', 'wk1', 'bk1', 'wv1', 'bv1', 'wo1', 'bo1', 'bias_k1', 'bias_v1', 'ln2_scale', 'ln2_offset', 'wq2', 'bq2', 'wk2', 'bk2', 'wv2', 'bv2', 'wo2', 'bo2', 'bias_k2', 'bias_v2', 'ln_mlp_scale', 'ln_mlp_offset', 'w_fc1', 'b_fc1', 'w_fc2', 'b_fc2')}
    del _L1_xattn_all
    return {'x': x, 'ctx_2048': ctx_2048, 'L0_xattn_Wn': _L0_xattn_in['Wn'], 'L0_xattn_bn': _L0_xattn_in['bn'], 'L0_xattn_Wm': _L0_xattn_in['Wm'], 'L0_xattn_bm': _L0_xattn_in['bm'], 'L0_xattn_Wl': _L0_xattn_in['Wl'], 'L0_xattn_bl': _L0_xattn_in['bl'], 'L0_xattn_Wo': _L0_xattn_in['Wo'], 'L0_xattn_bo': _L0_xattn_in['bo'], 'L1_xattn_ln1_scale': _L1_xattn_in['ln1_scale'], 'L1_xattn_ln1_offset': _L1_xattn_in['ln1_offset'], 'L1_xattn_wq1': _L1_xattn_in['wq1'], 'L1_xattn_bq1': _L1_xattn_in['bq1'], 'L1_xattn_wk1': _L1_xattn_in['wk1'], 'L1_xattn_bk1': _L1_xattn_in['bk1'], 'L1_xattn_wv1': _L1_xattn_in['wv1'], 'L1_xattn_bv1': _L1_xattn_in['bv1'], 'L1_xattn_wo1': _L1_xattn_in['wo1'], 'L1_xattn_bo1': _L1_xattn_in['bo1'], 'L1_xattn_bias_k1': _L1_xattn_in['bias_k1'], 'L1_xattn_bias_v1': _L1_xattn_in['bias_v1'], 'L1_xattn_ln2_scale': _L1_xattn_in['ln2_scale'], 'L1_xattn_ln2_offset': _L1_xattn_in['ln2_offset'], 'L1_xattn_wq2': _L1_xattn_in['wq2'], 'L1_xattn_bq2': _L1_xattn_in['bq2'], 'L1_xattn_wk2': _L1_xattn_in['wk2'], 'L1_xattn_bk2': _L1_xattn_in['bk2'], 'L1_xattn_wv2': _L1_xattn_in['wv2'], 'L1_xattn_bv2': _L1_xattn_in['bv2'], 'L1_xattn_wo2': _L1_xattn_in['wo2'], 'L1_xattn_bo2': _L1_xattn_in['bo2'], 'L1_xattn_bias_k2': _L1_xattn_in['bias_k2'], 'L1_xattn_bias_v2': _L1_xattn_in['bias_v2'], 'L1_xattn_ln_mlp_scale': _L1_xattn_in['ln_mlp_scale'], 'L1_xattn_ln_mlp_offset': _L1_xattn_in['ln_mlp_offset'], 'L1_xattn_w_fc1': _L1_xattn_in['w_fc1'], 'L1_xattn_b_fc1': _L1_xattn_in['b_fc1'], 'L1_xattn_w_fc2': _L1_xattn_in['w_fc2'], 'L1_xattn_b_fc2': _L1_xattn_in['b_fc2']}

def reference(x, ctx_2048, L0_xattn_Wn, L0_xattn_bn, L0_xattn_Wm, L0_xattn_bm, L0_xattn_Wl, L0_xattn_bl, L0_xattn_Wo, L0_xattn_bo, L1_xattn_ln1_scale, L1_xattn_ln1_offset, L1_xattn_wq1, L1_xattn_bq1, L1_xattn_wk1, L1_xattn_bk1, L1_xattn_wv1, L1_xattn_bv1, L1_xattn_wo1, L1_xattn_bo1, L1_xattn_bias_k1, L1_xattn_bias_v1, L1_xattn_ln2_scale, L1_xattn_ln2_offset, L1_xattn_wq2, L1_xattn_bq2, L1_xattn_wk2, L1_xattn_bk2, L1_xattn_wv2, L1_xattn_bv2, L1_xattn_wo2, L1_xattn_bo2, L1_xattn_bias_k2, L1_xattn_bias_v2, L1_xattn_ln_mlp_scale, L1_xattn_ln_mlp_offset, L1_xattn_w_fc1, L1_xattn_b_fc1, L1_xattn_w_fc2, L1_xattn_b_fc2):
    import jax
    import jax.numpy as jnp

    def _L0_xattn_ref(x_c, x_s, Wn, bn, Wm, bm, Wl, bl, Wo, bo):
        import jax, jax.numpy as jnp
        import numpy as np
        EPS = 1e-05

        def _inorm(x):
            m = jnp.mean(x, axis=-1, keepdims=True)
            v = jnp.var(x, axis=-1, keepdims=True)
            return (x - m) * jax.lax.rsqrt(v + EPS)

        def _conv1x1(W, b, x):
            return jnp.einsum('oc,bct->bot', W, x) + b[None, :, None]
        Mn = _conv1x1(Wn, bn, _inorm(x_c))
        Mm = _conv1x1(Wm, bm, _inorm(x_s))
        A = jax.nn.softmax(jnp.einsum('bct,bcs->bts', Mn, Mm), axis=-1)
        Ml = _conv1x1(Wl, bl, x_s)
        Mo = jnp.einsum('bcs,bts->bct', Ml, A)
        return _conv1x1(Wo, bo, Mo) + x_c

    def _L1_xattn_ref(x, xf_1, xf_2, ln1_scale, ln1_offset, wq1, bq1, wk1, bk1, wv1, bv1, wo1, bo1, bias_k1, bias_v1, ln2_scale, ln2_offset, wq2, bq2, wk2, bk2, wv2, bv2, wo2, bo2, bias_k2, bias_v2, ln_mlp_scale, ln_mlp_offset, w_fc1, b_fc1, w_fc2, b_fc2):
        import jax, jax.numpy as jnp
        import numpy as np
        B, Q, S1, S2 = (4, 32, 256, 256)
        D, H, K, F = (256, 16, 128, 1024)
        LN_EPS = 1e-05

        def _layer_norm(x, scale, offset):
            mu = jnp.mean(x, axis=-1, keepdims=True)
            var = jnp.var(x, axis=-1, keepdims=True)
            return (x - mu) * jax.lax.rsqrt(var + LN_EPS) * scale + offset

        def _cross_attention(q_in, kv_in, wq, bq, wk, bk, wv, bv, wo, bo, bias_k, bias_v):
            b, q_len, _ = q_in.shape
            t = kv_in.shape[1]
            qh = (q_in @ wq + bq).reshape(b, q_len, H, K)
            kh = (kv_in @ wk + bk).reshape(b, t, H, K)
            vh = (kv_in @ wv + bv).reshape(b, t, H, K)
            kh = jnp.concatenate([kh, jnp.broadcast_to(bias_k, (b, 1, H, K))], axis=1)
            vh = jnp.concatenate([vh, jnp.broadcast_to(bias_v, (b, 1, H, K))], axis=1)
            scale = jnp.sqrt(jnp.asarray(K, q_in.dtype))
            logits = jnp.einsum('bqhk,bthk->bhqt', qh, kh) / scale
            weights = jax.nn.softmax(logits, axis=-1)
            ctx = jnp.einsum('bhqt,bthk->bqhk', weights, vh).reshape(b, q_len, H * K)
            return ctx @ wo + bo

        def _forward(x, xf_1, xf_2, ln1_scale, ln1_offset, wq1, bq1, wk1, bk1, wv1, bv1, wo1, bo1, bias_k1, bias_v1, ln2_scale, ln2_offset, wq2, bq2, wk2, bk2, wv2, bv2, wo2, bo2, bias_k2, bias_v2, ln_mlp_scale, ln_mlp_offset, w_fc1, b_fc1, w_fc2, b_fc2):
            res = x
            h = _layer_norm(x, ln1_scale, ln1_offset)
            x = res + _cross_attention(h, xf_1, wq1, bq1, wk1, bk1, wv1, bv1, wo1, bo1, bias_k1, bias_v1)
            res = x
            h = _layer_norm(x, ln2_scale, ln2_offset)
            x = res + _cross_attention(h, xf_2, wq2, bq2, wk2, bk2, wv2, bv2, wo2, bo2, bias_k2, bias_v2)
            h = _layer_norm(x, ln_mlp_scale, ln_mlp_offset)
            h = jax.nn.gelu(h @ w_fc1 + b_fc1, approximate=False) @ w_fc2 + b_fc2
            return x + h
        return _forward(x, xf_1, xf_2, ln1_scale, ln1_offset, wq1, bq1, wk1, bk1, wv1, bv1, wo1, bo1, bias_k1, bias_v1, ln2_scale, ln2_offset, wq2, bq2, wk2, bk2, wv2, bv2, wo2, bo2, bias_k2, bias_v2, ln_mlp_scale, ln_mlp_offset, w_fc1, b_fc1, w_fc2, b_fc2)
    x = _L0_xattn_ref(x, ctx_2048, L0_xattn_Wn, L0_xattn_bn, L0_xattn_Wm, L0_xattn_bm, L0_xattn_Wl, L0_xattn_bl, L0_xattn_Wo, L0_xattn_bo)
    x = _L1_xattn_ref(x, ctx_2048, ctx_2048, L1_xattn_ln1_scale, L1_xattn_ln1_offset, L1_xattn_wq1, L1_xattn_bq1, L1_xattn_wk1, L1_xattn_bk1, L1_xattn_wv1, L1_xattn_bv1, L1_xattn_wo1, L1_xattn_bo1, L1_xattn_bias_k1, L1_xattn_bias_v1, L1_xattn_ln2_scale, L1_xattn_ln2_offset, L1_xattn_wq2, L1_xattn_bq2, L1_xattn_wk2, L1_xattn_bk2, L1_xattn_wv2, L1_xattn_bv2, L1_xattn_wo2, L1_xattn_bo2, L1_xattn_bias_k2, L1_xattn_bias_v2, L1_xattn_ln_mlp_scale, L1_xattn_ln_mlp_offset, L1_xattn_w_fc1, L1_xattn_b_fc1, L1_xattn_w_fc2, L1_xattn_b_fc2)
    return x

_drawn_inputs = setup_inputs


def setup_inputs(seed=0):
    import zlib

    import numpy as np

    out = dict(_drawn_inputs(seed))
    spreads = {'L1_xattn_ln1_scale': (1.0, 0.6),
     'L1_xattn_ln1_offset': (0.0, 0.8),
     'L1_xattn_bq1': (0.0, 0.8),
     'L1_xattn_bk1': (0.0, 2.0),
     'L1_xattn_bv1': (0.0, 0.1),
     'L1_xattn_bo1': (0.0, 0.1),
     'L1_xattn_ln2_scale': (1.0, 0.6),
     'L1_xattn_ln2_offset': (0.0, 0.8),
     'L1_xattn_bq2': (0.0, 0.8),
     'L1_xattn_bk2': (0.0, 2.0),
     'L1_xattn_bv2': (0.0, 0.1),
     'L1_xattn_bo2': (0.0, 0.1),
     'L1_xattn_ln_mlp_scale': (1.0, 0.6),
     'L1_xattn_ln_mlp_offset': (0.0, 0.8),
     'L1_xattn_b_fc1': (0.0, 0.349),
     'L1_xattn_b_fc2': (0.0, 0.1)}
    factors = {'L0_xattn_bm': 64.0,
     'L1_xattn_wq1': 8.0,
     'L1_xattn_wk1': 8.0,
     'L1_xattn_bias_k1': 64.0,
     'L1_xattn_bias_v1': 64.0,
     'L1_xattn_wq2': 8.0,
     'L1_xattn_wk2': 8.0,
     'L1_xattn_bias_k2': 64.0,
     'L1_xattn_bias_v2': 64.0}
    for name, (base, spread) in spreads.items():
        noise = np.random.default_rng([zlib.crc32(name.encode()), seed]).standard_normal(out[name].shape)
        drawn = base * np.exp(spread * noise) if base else spread * noise
        out[name] = jnp.asarray(drawn.astype(out[name].dtype))
    for name, factor in factors.items():
        out[name] = (out[name] * factor).astype(out[name].dtype)
    return out
```

```python
import concourse.bass as bass
from concourse import mybir

F32 = mybir.dt.float32
F32R = mybir.dt.float32r
ACT = mybir.ActivationFunctionType
ALU = mybir.AluOpType
AX = mybir.AxisListType

P = 128
BATCH, Q, D = 64, 64, 256
H, K, F = 16, 128, 1024
LAYERS = 2
TOK = 512
BLOCKS = BATCH * Q // TOK
PAIRS = TOK // P
DC = D // P
HG = 4
GROUPS = H // HG
SLOTS = GROUPS * PAIRS
KEYS = Q + 1
FT = F // P
EPS = 1e-5
SCALE = float(K) ** -0.5
ZPAIRS = BATCH // 2
ZUN = 4



def projections(slot, last):
    if slot < 12:
        uses = ([("Q", slot + 4, 0)], [("K", slot + 4, 0)], [("V", slot + 3, 0)])
    elif slot == 12:
        uses = ([], [("X", 0, 1), ("X", 1, 1)], [("V", 15, 0), ("X", 2, 1), ("X", 3, 1)])
    elif slot == 13:
        uses = ([("Q", 0, 1), ("K", 0, 1)], [("Q", 1, 1)], [("V", 0, 1)])
    elif slot == 14:
        uses = ([("K", 1, 1), ("Q", 2, 1)], [("K", 2, 1)], [("V", 1, 1)])
    else:
        uses = ([("Q", 3, 1)], [("K", 3, 1)], [("V", 2, 1)])
    return [[u for u in part if not (last and u[2])] for part in uses]


PROLOGUE = [("X", 0, 0), ("X", 1, 0), ("X", 2, 0), ("X", 3, 0), ("Q", 0, 0), ("K", 0, 0), ("Q", 1, 0), ("V", 0, 0),
            ("K", 1, 0), ("Q", 2, 0), ("K", 2, 0), ("V", 1, 0), ("Q", 3, 0), ("K", 3, 0), ("V", 2, 0)]


def bank_plan(uses, first_bank, before):
    seq = list(before)
    plan = {}
    for n, use in enumerate(uses):
        plan[use] = ((first_bank + n) % 2, seq[-2] if len(seq) > 1 else None)
        seq.append(use)
    return plan


def block_plan(last):
    uses = [u for s in range(SLOTS) for part in projections(s, last) for u in part]
    return bank_plan(uses, len(PROLOGUE) % 2, [("K", 3, 0), ("V", 2, 0)])


def ge(engine, sem, value):
    if isinstance(value, int) and value <= 0:
        return
    engine.wait_ge(sem, value)


def ge_apart(engine, sem, value, apart):
    engine.wait_ge(sem, value)
    engine.sem_inc(apart, 1)


class Space:

    def __init__(self, nc, at):
        self.nc, self.at = nc, at

    def put(self, name, shape, dtype=F32, at=None):
        size = 4
        for n in shape[1:]:
            size *= n
        if at is None:
            at = self.at
            self.at += (size + 31) // 32 * 32
        t = self.nc.alloc_sbuf_tensor_at(name, shape, dtype, offset=at)
        t_at = at
        return t, t_at


def build(nc, x, ctx, zw, zb, wq, wk, wv, wo, rows, ln, bo, w1, w2, b1, b2, out):
    base = (nc.sbuf_base + 31) // 32 * 32
    sp = Space(nc, base)
    WSZ = DC * H * K * 4
    w_hi, w_lo, w_raw = {}, {}, {}
    w_at = {}
    for n, shape in (("q", [P, DC, H * K]), ("k", [P, DC, H * K]), ("v", [P, DC, H * K]), ("o", [P, H, D])):
        w_hi[n], w_at[n] = sp.put("w_hi_" + n, shape, F32R)
        w_lo[n], lo_at = sp.put("w_lo_" + n, shape, F32R)
        w_raw[n], _ = sp.put("w_raw_" + n, shape, F32, lo_at)
    q_sb, shared_at = sp.put("q_sb", [P, 2, HG, TOK])
    k_sb, _ = sp.put("k_sb", [P, 2, HG, 2 * PAIRS, KEYS])
    v_sb, _ = sp.put("v_sb", [P, PAIRS, HG * K])
    h_hi, _ = sp.put("h_hi", [P, DC, TOK], F32R)
    h_lo, _ = sp.put("h_lo", [P, DC, TOK], F32R)
    c_hi, _ = sp.put("c_hi", [P, DC, TOK], F32R)
    c_lo, shared_end = sp.put("c_lo", [P, DC, TOK], F32R)
    shared_end += DC * TOK * 4
    x_st, _ = sp.put("x_st", [P, PAIRS, D])
    kv_st, _ = sp.put("kv_st", [P, PAIRS, D])
    ln_bc, _ = sp.put("ln_bc", [P, 2, D])
    s_sb, s_at = sp.put("s_sb", [P, HG, KEYS])
    bo_row, _ = sp.put("bo_row", [1, D], F32, s_at)
    p_sb, _ = sp.put("p_sb", [P, HG, P])
    pt_sb, pt_at = sp.put("pt_sb", [P, HG * P])
    rows_sb, _ = sp.put("rows_sb", [P, K], F32, pt_at)
    lmat, _ = sp.put("lmat", [P, H, H + 1], F32, pt_at + K * 4)
    cx_hi, _ = sp.put("cx_hi", [P, HG * P], F32R)
    cx_lo, _ = sp.put("cx_lo", [P, HG * P], F32R)
    ident, _ = sp.put("ident", [P, P])
    pbt_sb, _ = sp.put("pbt_sb", [P, TOK])
    bw_sb, _ = sp.put("bw_sb", [P, D])
    pb_sb, _ = sp.put("pb_sb", [P, PAIRS, H + 1])
    prm, _ = sp.put("prm", [P, 5 * H])
    onehot, _ = sp.put("onehot", [1, H + 1])
    small, _ = sp.put("small", [P, 3, HG])
    mx, sm, rc = small[:, 0, :], small[:, 1, :], small[:, 2, :]
    st6, _ = sp.put("st6", [P, PAIRS, 6])
    mv, _ = sp.put("mv", [P, PAIRS, 2])
    rstd, _ = sp.put("rstd", [P, PAIRS])
    mhalf, _ = sp.put("mhalf", [P, PAIRS])
    assert sp.at <= nc.sbuf_usable_end, (sp.at, nc.sbuf_usable_end)
    bq_c, bk_c, bkey_c = prm[:, 0:H], prm[:, H:2 * H], prm[:, 2 * H:3 * H]

    zs = Space(nc, shared_at)
    z_x, _ = zs.put("z_x", [P, ZUN, D])
    z_s, _ = zs.put("z_s", [P, ZUN, D])
    z_o, _ = zs.put("z_o", [P, 2, D])
    z_v, _ = zs.put("z_v", [P, ZUN, 2, P])
    z_xn, _ = zs.put("z_xn", [P, D])
    z_sn, _ = zs.put("z_sn", [P, D])
    z_mn, _ = zs.put("z_mn", [P, 2, D])
    z_mm, _ = zs.put("z_mm", [P, D])
    z_p, _ = zs.put("z_p", [P, 2, 2, 2, D])
    z_pt, _ = zs.put("z_pt", [P, 2, 2, D])
    z_w, _ = zs.put("z_w", [P, 4, P])
    z_wt, _ = zs.put("z_wt", [P, 4, P])
    z_b, _ = zs.put("z_b", [P, 4])
    z_c, _ = zs.put("z_c", [P, 1])
    z_st6, _ = zs.put("z_st6", [P, 2, 6])
    z_mv, _ = zs.put("z_mv", [P, 2, 2, 2])
    z_rs, _ = zs.put("z_rs", [P, 2, 2])
    z_nmx, _ = zs.put("z_nmx", [P, 2, 2])
    z_mxv, _ = zs.put("z_mxv", [P, 2, 2])
    z_sum, _ = zs.put("z_sum", [P, 2, 2])
    z_rc, _ = zs.put("z_rc", [P, 2, 2])
    assert zs.at <= shared_end

    w1_hi, _ = sp.put("w1_hi", [P, DC, F], F32R, w_at["q"])
    w1_lo, _ = sp.put("w1_lo", [P, DC, F], F32R, w_at["q"] + 8192)
    w1_raw, _ = sp.put("w1_raw", [P, DC, F], F32, w_at["q"] + 8192)
    w2_hi, _ = sp.put("w2_hi", [P, FT, D], F32R, w_at["q"] + 16384)
    w2_lo, _ = sp.put("w2_lo", [P, FT, D], F32R, w_at["q"] + 24576)
    w2_raw, _ = sp.put("w2_raw", [P, FT, D], F32, w_at["q"] + 24576)
    g_hi, _ = sp.put("g_hi", [P, FT, TOK], F32R, w_at["k"])
    g_lo, _ = sp.put("g_lo", [P, FT, TOK], F32R, w_at["k"] + 16384)
    g_raw, _ = sp.put("g_raw", [P, 2, TOK], F32, w_at["v"])
    b1_rows, _ = sp.put("b1_rows", [FT, P], F32, w_at["v"] + 4096)
    b1_c, _ = sp.put("b1_c", [P, FT], F32, w_at["v"] + 8192)
    b2_bc, _ = sp.put("b2_bc", [P, D], F32, w_at["v"] + 12288)
    mln_bc, _ = sp.put("mln_bc", [P, 2, D], F32, w_at["v"] + 16384)

    ps_pr = [nc.alloc_psum_tensor(f"ps_pr{i}", [P, 512], F32) for i in range(2)]
    ps_l = nc.alloc_psum_tensor("ps_l", [P, 2, 512], F32)
    ps_t = nc.alloc_psum_tensor("ps_t", [P, 512], F32)
    ps_c = nc.alloc_psum_tensor("ps_c", [P, 512], F32)
    ps_o = [nc.alloc_psum_tensor(f"ps_o{i}", [P, 512], F32) for i in range(2)]

    scr = nc.dram_tensor("x_scratch", (3 * BLOCKS, TOK, D), F32, kind="Internal").ap()

    names = """apart_dve apart_pool ident_ok consts_ok
    z_wld z_wt_mm z_wt_ev z_wl_mm z_wl_ev z_bias z_zero z_ld0 z_ld1 z_ld2 z_ld3 z_so0 z_so1
    z_st z_mvd z_eps z_rsd z_norm_x z_s1 z_vmm z_m_ev z_v_ev z_l z_max z_nmx_ok z_exp z_rec z_normd z_t z_pt_ev0 z_pt_ev1 z_pv z_outd z_end
    wq_ld wk_ld wv_ld wo_ld wq_hi wk_hi wv_hi wo_hi wq_ok wk_ok wv_ok wo_ok rows_ld rows_t prm_ok l_zero lmat_ok bo_ld bw_mm bw_ok lnb_ld
    x_ld kv_ld res_ld x_st_ok st_done mv_done eps_done rs_done xn_done aff_done xh_done
    q_mm k_mm v_mm x_mm q_ev k_ev v_ev x_hi_ev x_ev bias_col qk_done max_done sub_done exp_done sum_done rec_done norm_done
    t_done pt_ev pv_done cxhi_done cxlo_done o_done pbt_done pbt_ev fin_done xout_done layer_end
    m_w1ld m_w2ld m_bld m_lnld m_w1h m_w2h m_w1 m_w2 m_b1t m_b1 m_xld m_rld m_sto m_st m_mv m_eps m_rs m_xn m_aff m_xh m_x m_xhi m_xlo
    m_fc1 m_gelu m_ghi m_glo m_fc2 m_res m_out""".split()
    S = type("Semaphores", (), {n: nc.alloc_semaphore(n) for n in names})
    z_ld = [S.z_ld0, S.z_ld1, S.z_ld2, S.z_ld3]
    z_so = [S.z_so0, S.z_so1]
    z_pt_ev = [S.z_pt_ev0, S.z_pt_ev1]
    w_ld = {"q": S.wq_ld, "k": S.wk_ld, "v": S.wv_ld, "o": S.wo_ld}
    w_hi_ok = {"q": S.wq_hi, "k": S.wk_hi, "v": S.wv_hi, "o": S.wo_hi}
    w_ok = {"q": S.wq_ok, "k": S.wk_ok, "v": S.wv_ok, "o": S.wo_ok}

    tok = lambda a: a.rearrange("(j p) d -> p j d", p=P)
    xp = x.rearrange("(i p) d -> i p d", p=P)
    cp = ctx.rearrange("(i p) d -> i p d", p=P)
    cb = ctx.rearrange("(b t) d -> b t d", t=TOK)
    ob = out.rearrange("(b t) d -> b t d", t=TOK)
    sp_pairs = scr.rearrange("b (j p) d -> (b j) p d", p=P)

    def evac_of(use, gb):
        kind, idx, nxt = use
        sem = {"Q": S.q_ev, "K": S.k_ev, "V": S.v_ev, "X": S.x_ev}[kind]
        return sem, (gb + nxt) * (4 if kind == "X" else SLOTS) + idx + 1

    with nc.Block() as block:

        @block.sync
        def _(e):
            def load_w(n, layer):
                src = {"q": wq, "k": wk, "v": wv, "o": wo}[n]
                e.dma_start(w_raw[n][:], src[layer].rearrange("(c p) n -> p c n", p=P)).then_inc(w_ld[n], 16)

            def load_layer_constants(layer):
                e.dma_start(rows_sb[0:5 * H, :], rows[layer]).then_inc(S.rows_ld, 16)
                e.dma_start(bo_row[:], bo[layer:layer + 1, :]).then_inc(S.bo_ld, 16)
                e.dma_start(ln_bc[:], ln[layer].partition_broadcast(P)).then_inc(S.lnb_ld, 16)

            def z_load(i, k):
                e.dma_start(z_x[:, k, :], xp[i]).then_inc(z_ld[k], 16)
                e.dma_start(z_s[:, k, :], cp[i]).then_inc(z_ld[k], 16)

            def z_store(i, k):
                e.wait_ge(S.z_outd, i + 1)
                e.dma_start(sp_pairs[i], z_o[:, k % 2, :]).then_inc(z_so[k % 2], 16)

            for n in range(4):
                if n == 0:
                    e.wait_ge(S.z_zero, 1)
                for half in range(2):
                    r = slice(64 * half, 64 * half + 64)
                    e.dma_start(z_w[r, n, r], zw[n]).then_inc(S.z_wld, 16)
                    e.dma_start(z_b[r, n:n + 1], zb[n].rearrange("(p a) -> p a", a=1)).then_inc(S.z_wld, 16)
            for k in range(ZUN):
                z_load(k, k)
            load_layer_constants(0)
            for n in "qkvo":
                load_w(n, 0)
            with e.Fori(0, ZPAIRS // ZUN - 1) as g:
                for k in range(ZUN):
                    z_store(g * ZUN + k, k)
                    z_load(g * ZUN + ZUN + k, k)
            for k in range(ZUN):
                z_store(ZPAIRS - ZUN + k, k)

            def load_x(gb):
                e.dma_start(x_st[:], tok(scr[gb])).then_inc(S.x_ld, 16)

            def store_out(gb):
                e.wait_ge(S.xout_done, gb + 1)
                e.dma_start(tok(scr[gb + BLOCKS]), x_st[:]).then_inc(S.x_st_ok, 16)

            def sp_block(gb, b, first, last):
                if not first:
                    store_out(gb - 1)
                if not last:
                    if not first:
                        e.wait_ge(S.x_st_ok, gb * 16)
                    else:
                        e.wait_ge(S.x_mm, gb * 4 + 2)
                    load_x(gb + 1)
                    e.wait_ge(S.x_mm, gb * 4 + 4)
                    e.dma_start(kv_st[:], tok(cb[b + 1])).then_inc(S.kv_ld, 16)
                    e.wait_ge(S.x_mm, gb * 4 + 6)
                else:
                    e.wait_ge(S.x_st_ok, gb * 16)
                e.dma_start(x_st[:], tok(scr[gb])).then_inc(S.res_ld, 16)

            for layer in range(LAYERS):
                g0 = layer * BLOCKS
                if layer == 0:
                    for k in range(2):
                        e.wait_ge(z_so[k], 16 * ZPAIRS // 2)
                else:
                    e.wait_ge(S.x_st_ok, g0 * 16)
                load_x(g0)
                e.dma_start(kv_st[:], tok(cb[0])).then_inc(S.kv_ld, 16)
                if layer:
                    load_layer_constants(layer)
                sp_block(g0, 0, True, False)
                with e.Fori(1, BLOCKS - 1) as b:
                    sp_block(b + g0, b, False, False)
                sp_block(g0 + BLOCKS - 1, BLOCKS - 1, False, True)
                gl = (g0 + BLOCKS) * 16
                if layer + 1 < LAYERS:
                    e.wait_ge(S.q_mm, gl)
                    load_w("q", layer + 1)
                    e.wait_ge(S.k_mm, gl)
                    load_w("k", layer + 1)
                    e.wait_ge(S.v_mm, gl)
                    load_w("v", layer + 1)
                    e.wait_ge(S.layer_end, layer + 2)
                    load_w("o", layer + 1)
                else:
                    e.wait_ge(S.q_mm, gl)
                    e.dma_start(w1_raw[:], w1.rearrange("(c p) n -> p c n", p=P)).then_inc(S.m_w1ld, 16)
                    e.dma_start(w2_raw[:], w2.rearrange("(c p) n -> p c n", p=P)).then_inc(S.m_w2ld, 16)
                    e.wait_ge(S.v_mm, gl)
                    e.dma_start(b1_rows[:], b1).then_inc(S.m_bld, 16)
                    e.dma_start(b2_bc[:], b2.partition_broadcast(P)).then_inc(S.m_bld, 16)
                    e.dma_start(mln_bc[:], ln[LAYERS].partition_broadcast(P)).then_inc(S.m_lnld, 16)
                store_out(g0 + BLOCKS - 1)

            e.wait_ge(S.x_st_ok, LAYERS * BLOCKS * 16)
            e.wait_ge(S.layer_end, LAYERS + 1)
            m0 = LAYERS * BLOCKS
            e.dma_start(kv_st[:], tok(scr[m0])).then_inc(S.m_xld, 16)
            e.dma_start(x_st[:], tok(scr[m0])).then_inc(S.m_rld, 16)

            def m_store(b):
                e.wait_ge(S.m_out, b * 2 + 2)
                e.dma_start(tok(ob[b]), x_st[:]).then_inc(S.m_sto, 16)
                e.wait_ge(S.m_sto, b * 16 + 16)

            def m_load(b):
                e.wait_ge(S.m_x, b * 2)
                e.dma_start(kv_st[:], tok(scr[b + m0])).then_inc(S.m_xld, 16)

            def m_residual(b):
                m_store(b - 1)
                e.dma_start(x_st[:], tok(scr[b + m0])).then_inc(S.m_rld, 16)

            m_load(1)
            with e.Fori(1, BLOCKS - 1) as b:
                m_load(b + 1)
                m_residual(b)
            m_residual(BLOCKS - 1)
            m_store(BLOCKS - 1)

        @block.gpsimd
        def _(e):
            e.memset(z_w[:], 0.0).then_inc(S.z_zero, 1)
            e.memset(ident[:], 0.0).then_inc(S.consts_ok, 1)
            e.memset(p_sb[:], 0.0).then_inc(S.consts_ok, 1)
            e.memset(pbt_sb[:], 0.0).then_inc(S.consts_ok, 1)
            e.memset(bw_sb[:], 0.0).then_inc(S.consts_ok, 1)
            e.memset(pb_sb[:], 1.0).then_inc(S.consts_ok, 1)
            e.memset(onehot[:], 0.0).then_inc(S.consts_ok, 1)
            e.memset(mhalf[:], -0.5).then_inc(S.consts_ok, 1)
            e.memset(z_mn[:], 0.0).then_inc(S.consts_ok, 1)
            e.wait_ge(S.consts_ok, 8)
            e.memset(onehot[:, H:H + 1], 1.0).then_inc(S.consts_ok, 1)
            e.affine_select(out=ident[:], in_=ident[:], compare_op=ALU.not_equal, fill=1.0, base=0,
                            pattern=[[-1, P]], channel_multiplier=1).then_inc(S.ident_ok, 1)

            def z_rstd(i, par):
                ge_apart(e, S.z_mvd, i + 1, S.apart_pool)
                e.tensor_scalar(z_rs[:, par, :], z_mv[:, par, :, 1], EPS, None, ALU.add).then_inc(S.z_eps, 1)
                e.wait_ge(S.z_eps, i + 1)
                e.tensor_tensor(z_rs[:, par, :], z_rs[:, par, :], mhalf[:, 0:2], ALU.pow).then_inc(S.z_rsd, 1)

            with e.Fori(0, ZPAIRS // 2) as g:
                for k in range(2):
                    z_rstd(g * 2 + k, k)

            def rstd_of(n):
                ge_apart(e, S.mv_done, n, S.apart_pool)
                e.tensor_scalar(rstd[:], mv[:, :, 1], EPS, None, ALU.add).then_inc(S.eps_done, 1)
                e.wait_ge(S.eps_done, n)
                e.tensor_tensor(rstd[:], rstd[:], mhalf[:], ALU.pow).then_inc(S.rs_done, 1)

            def affine(n):
                e.wait_ge(S.xn_done, n)
                e.tensor_tensor(x_st[:], x_st[:], ln_bc[:, 0:1, :].to_broadcast([P, PAIRS, D]), ALU.mult).then_inc(S.aff_done, 1)
                e.wait_ge(S.aff_done, n)
                e.tensor_tensor(x_st[:], x_st[:], ln_bc[:, 1:2, :].to_broadcast([P, PAIRS, D]), ALU.add).then_inc(S.xh_done, 1)

            def bias_columns(hg):
                par = hg % 2
                e.tensor_copy(k_sb[:, par, :, :, Q], bkey_c[:, HG * hg:HG * hg + HG].unsqueeze(2)
                              .to_broadcast([P, HG, 2 * PAIRS])).then_inc(S.bias_col, 1)

            def pool_block(gb, first, last):
                for hg in (1, 2):
                    if not (first and hg == 1):
                        ge_apart(e, S.qk_done, gb * SLOTS + PAIRS * (hg - 1), S.apart_pool)
                    bias_columns(hg)
                if not last:
                    rstd_of(gb + 2)
                ge_apart(e, S.qk_done, gb * SLOTS + PAIRS * 2, S.apart_pool)
                bias_columns(3)
                if not last:
                    affine(gb + 2)
                    ge_apart(e, S.qk_done, gb * SLOTS + PAIRS * 3, S.apart_pool)
                    bias_columns(0)

            with e.Fori(0, LAYERS) as layer:
                g0 = layer * BLOCKS
                e.wait_ge(S.layer_end, layer + 1)
                rstd_of(g0 + 1)
                e.wait_ge(S.lnb_ld, layer * 16 + 16)
                affine(g0 + 1)
                ge_apart(e, S.prm_ok, layer + 1, S.apart_pool)
                bias_columns(0)
                pool_block(g0, True, False)
                with e.Fori(1, BLOCKS - 1) as b:
                    pool_block(b + g0, False, False)
                pool_block(g0 + (BLOCKS - 1), False, True)

            def m_norm(n):
                ge_apart(e, S.m_mv, n, S.apart_pool)
                e.tensor_scalar(rstd[:], mv[:, :, 1], EPS, None, ALU.add).then_inc(S.m_eps, 1)
                e.wait_ge(S.m_eps, n)
                e.tensor_tensor(rstd[:], rstd[:], mhalf[:], ALU.pow).then_inc(S.m_rs, 1)
                e.wait_ge(S.m_xn, n)
                e.tensor_tensor(kv_st[:], kv_st[:], mln_bc[:, 0:1, :].to_broadcast([P, PAIRS, D]), ALU.mult).then_inc(S.m_aff, 1)
                e.wait_ge(S.m_aff, n)
                e.tensor_tensor(kv_st[:], kv_st[:], mln_bc[:, 1:2, :].to_broadcast([P, PAIRS, D]), ALU.add).then_inc(S.m_xh, 1)

            def m_residual(n):
                e.wait_ge(S.m_rld, n * 16)
                e.tensor_tensor(x_st[:], x_st[:], b2_bc[:].unsqueeze(1).to_broadcast([P, PAIRS, D]), ALU.add).then_inc(S.m_res, 1)

            e.wait_ge(S.m_lnld, 16)
            e.wait_ge(S.m_bld, 32)
            m_norm(1)
            with e.Fori(0, BLOCKS - 1) as b:
                m_norm(b + 2)
                m_residual(b + 1)
            m_residual(BLOCKS)

        @block.scalar
        def _(e):
            def z_exp(i, par, b):
                e.wait_ge(S.z_nmx_ok, i * 2 + (b + 1))
                for tc in range(2):
                    ins = e.activation(z_p[:, par, b, tc, :], ps_l[:, b, 256 * tc:256 * tc + 256], ACT.Exp,
                                       bias=z_nmx[:, b, tc:tc + 1], accum_out=z_sum[:, b, tc:tc + 1])
                ins.then_inc(S.z_exp, 1)

            def z_ptev(i):
                e.wait_ge(S.z_t, i * 2 + 2)
                e.activation(z_pt[:, 1].rearrange("p a t -> p (a t)"), ps_c[:], ACT.Copy).then_inc(S.z_pt_ev1, 1)

            def z_evac_m(i):
                e.wait_ge(S.z_s1, i + 1)
                for b in range(2):
                    r = slice(64 * b, 64 * b + 64)
                    e.activation(z_mn[r, b, :], ps_pr[0][r, 0:256], ACT.Identity, bias=z_b[r, 0:1])
                e.activation(z_mm[:], ps_pr[0][:, 256:512], ACT.Identity, bias=z_b[:, 1:2]).then_inc(S.z_m_ev, 1)

            def z_evac_v(i, k):
                e.wait_ge(S.z_vmm, i + 1)
                e.activation(z_v[:, k].rearrange("p a b -> p (a b)"), ps_pr[1][:, 0:256], ACT.Copy).then_inc(S.z_v_ev, 1)

            e.wait_ge(S.z_wt_mm, 1)
            e.activation(z_wt[:].rearrange("p a b -> p (a b)"), ps_pr[0][:], ACT.Copy).then_inc(S.z_wt_ev, 1)
            e.wait_ge(S.z_wl_mm, 1)
            e.activation(z_wt[:, 2, :], ps_pr[1][:, 0:128], ACT.Copy).then_inc(S.z_wl_ev, 1)
            e.activation(z_c[:], ps_pr[1][:, 128:129], ACT.Identity, bias=z_b[:, 3:4]).then_inc(S.z_bias, 1)
            e.wait_ge(S.consts_ok, 9)
            z_evac_m(0)
            z_evac_v(0, 0)
            def z_step(i, k, prev, nxt):
                z_exp(i, k % 2, 0)
                if nxt:
                    z_evac_m(i + 1)
                if prev:
                    z_ptev(i - 1)
                z_exp(i, k % 2, 1)
                if nxt:
                    z_evac_v(i + 1, (k + 1) % ZUN)

            for k in range(ZUN):
                z_step(k, k, k > 0, True)
            with e.Fori(1, ZPAIRS // ZUN - 1) as g:
                for k in range(ZUN):
                    z_step(g * ZUN + k, k, True, True)
            for k in range(ZUN):
                z_step(ZPAIRS - ZUN + k, k, True, k < ZUN - 1)
            z_ptev(ZPAIRS - 1)

            plans = {last: block_plan(last) for last in (False, True)}
            first_plan = bank_plan(PROLOGUE, 0, [])

            def evac(use, bank, gb):
                kind, idx, nxt = use
                n = gb + nxt
                if kind == "Q":
                    e.wait_ge(S.q_mm, n * SLOTS + (idx + 1))
                    e.activation(q_sb[:, idx // HG % 2, idx % HG, :], ps_pr[bank][:], ACT.Identity,
                                 bias=bq_c[:, idx:idx + 1]).then_inc(S.q_ev, 1)
                elif kind == "K":
                    e.wait_ge(S.k_mm, n * SLOTS + (idx + 1))
                    e.activation(k_sb[:, idx // HG % 2, idx % HG, :, 0:Q], ps_pr[bank][:].rearrange("p (a c) -> p a c", c=Q),
                                 ACT.Identity, bias=bk_c[:, idx:idx + 1]).then_inc(S.k_ev, 1)
                elif kind == "X":
                    dst = h_hi if idx < 2 else c_hi
                    t = 256 * (idx % 2)
                    e.wait_ge(S.x_mm, n * 4 + (idx + 1))
                    e.activation(dst[:, :, t:t + 256], ps_pr[bank][:].rearrange("p (c t) -> p c t", c=DC), ACT.Copy).then_inc(S.x_hi_ev, 1)

            def act_slot(gb, s, first, plan, uses, work=True):
                B = gb * SLOTS
                if work:
                    e.wait_ge(S.sub_done, B + (s + 1))
                    e.activation(s_sb[:], s_sb[:], ACT.Exp, scale=SCALE).then_inc(S.exp_done, 1)
                for u in uses[0]:
                    evac(u, plan[u][0], gb)
                if not (first and s == 0) and s < 17:
                    e.wait_ge(S.t_done, B + s)
                    if not (first and s == 1):
                        e.wait_ge(S.pv_done, B + (s - 1))
                    e.activation(pt_sb[:], ps_t[:], ACT.Copy).then_inc(S.pt_ev, 1)
                    if s in (0, SLOTS):
                        nb = gb if s == 0 else gb + 1
                        e.wait_ge(S.pbt_done, nb)
                        e.activation(pbt_sb[0:H + 1, :], ps_c[0:H + 1, :], ACT.Copy).then_inc(S.pbt_ev, 1)
                for u in uses[1]:
                    evac(u, plan[u][0], gb)
                if not (first and s == 0) and s < 17:
                    e.wait_ge(S.pv_done, B + s)
                    if not (first and s == 1):
                        e.wait_ge(S.o_done, B + (s - 1))
                    e.activation(cx_hi[:], ps_c[:], ACT.Copy).then_inc(S.cxhi_done, 1)
                for u in uses[2]:
                    evac(u, plan[u][0], gb)

            def act_block(gb, first, last):
                for s in range(SLOTS):
                    act_slot(gb, s, first, plans[last], projections(s, last))

            with e.Fori(0, LAYERS) as layer:
                g0 = layer * BLOCKS
                for n in "qkvo":
                    e.wait_ge(w_ld[n], layer * 16 + 16)
                    e.activation(w_hi[n][:], w_raw[n][:], ACT.Copy).then_inc(w_hi_ok[n], 1)
                e.wait_ge(S.prm_ok, layer + 1)
                for u in PROLOGUE:
                    evac(u, first_plan[u][0], g0)
                act_block(g0, True, False)
                with e.Fori(1, BLOCKS - 1) as b:
                    act_block(b + g0, False, False)
                act_block(g0 + (BLOCKS - 1), False, True)
                act_slot(g0 + (BLOCKS - 1), SLOTS, False, None, [[], [], []], work=False)

            e.wait_ge(S.m_w1ld, 16)
            e.activation(w1_hi[:], w1_raw[:], ACT.Copy).then_inc(S.m_w1h, 1)
            e.wait_ge(S.m_w2ld, 16)
            e.activation(w2_hi[:], w2_raw[:], ACT.Copy).then_inc(S.m_w2h, 1)

            def m_xhi(b, i):
                e.wait_ge(S.m_x, b * 2 + (i + 1))
                e.activation(h_hi[:, :, 256 * i:256 * i + 256], ps_pr[i][:].rearrange("p (c t) -> p c t", c=DC), ACT.Copy).then_inc(S.m_xhi, 1)

            def m_gelu(b, first):
                for j in range(FT):
                    e.wait_ge(S.m_fc1, b * FT + (j + 1))
                    if not (first and j < 2):
                        e.wait_ge(S.m_glo, b * FT + (j - 1))
                    e.activation(g_raw[:, j % 2, :], ps_pr[j % 2][:], ACT.Gelu, bias=b1_c[:, j:j + 1]).then_inc(S.m_gelu, 1)

            m_xhi(0, 0)
            m_xhi(0, 1)
            e.wait_ge(S.m_b1, 1)
            m_gelu(0, True)
            with e.Fori(1, BLOCKS) as b:
                m_xhi(b, 0)
                m_xhi(b, 1)
                m_gelu(b, False)

        @block.vector
        def _(e):
            def z_stats(i, k, rnd, par):
                e.wait_ge(z_ld[k], rnd * 32 + 32)
                ge(e, S.z_mvd, i)
                e.bn_stats(z_st6[:, 0, :], z_x[:, k, :])
                e.bn_stats(z_st6[:, 1, :], z_s[:, k, :]).then_inc(S.z_st, 1)
                ge_apart(e, S.z_st, i + 1, S.apart_dve)
                e.bn_aggr(z_mv[:, par, 0, :], z_st6[:, 0, :])
                e.bn_aggr(z_mv[:, par, 1, :], z_st6[:, 1, :]).then_inc(S.z_mvd, 1)

            def z_normalise(i, k, par):
                e.wait_ge(S.z_rsd, i + 1)
                ge(e, S.z_s1, i)
                for j, (dst, src) in enumerate(((z_xn, z_x), (z_sn, z_s))):
                    ins = e.tensor_scalar(dst[:], src[:, k, :], z_mv[:, par, j, 0:1], z_rs[:, par, j:j + 1], ALU.subtract, ALU.mult)
                ins.then_inc(S.z_norm_x, 1)

            def z_max(i, b):
                e.wait_ge(S.z_l, i * 2 + (b + 1))
                e.reduce_max(z_mxv[:, b, :], ps_l[:, b, :].rearrange("p (a s) -> p a s", a=2), AX.X).then_inc(S.z_max, 1)
                e.wait_ge(S.z_max, i * 2 + (b + 1))
                e.tensor_scalar(z_nmx[:, b, :], z_mxv[:, b, :], -1.0, None, ALU.mult).then_inc(S.z_nmx_ok, 1)

            def z_probs(i, par, b):
                e.wait_ge(S.z_exp, i * 2 + (b + 1))
                e.reciprocal(z_rc[:, b, :], z_sum[:, b, :]).then_inc(S.z_rec, 1)
                e.wait_ge(S.z_rec, i * 2 + (b + 1))
                for tc in range(2):
                    ins = e.tensor_scalar(z_p[:, par, b, tc, :], z_p[:, par, b, tc, :], z_rc[:, b, tc:tc + 1], None, ALU.mult)
                ins.then_inc(S.z_normd, 1)

            def z_ptev(i):
                e.wait_ge(S.z_t, i * 2 + 1)
                e.tensor_copy(z_pt[:, 0].rearrange("p a t -> p (a t)"), ps_t[:]).then_inc(S.z_pt_ev0, 1)

            def z_final(i, k, stored):
                e.wait_ge(S.z_pv, i + 1)
                ge(e, z_so[k % 2], stored)
                e.scalar_tensor_tensor(out=z_o[:, k % 2, :], in0=ps_o[0][:, 0:256], scalar=z_c[:, 0:1], in1=z_x[:, k, :],
                                       op0=ALU.add, op1=ALU.add).then_inc(S.z_outd, 1)

            def z_step(i, k, rnd, prev, nxt2):
                z_max(i, 0)
                if prev:
                    z_probs(i - 1, (k - 1) % 2, 1)
                z_max(i, 1)
                if prev:
                    z_ptev(i - 1)
                if nxt2:
                    z_stats(i + 2, (k + 2) % ZUN, rnd + (k + 2) // ZUN, k % 2)
                z_probs(i, k % 2, 0)
                if prev:
                    z_final(i - 1, (k - 1) % ZUN, (rnd * (ZUN // 2) + (k - 1) // 2) * 16)
                if nxt2:
                    z_normalise(i + 2, (k + 2) % ZUN, k % 2)

            z_stats(0, 0, 0, 0)
            z_stats(1, 1, 0, 1)
            z_normalise(0, 0, 0)
            z_normalise(1, 1, 1)
            e.wait_ge(S.z_bias, 1)
            for k in range(ZUN):
                z_step(k, k, 0, k > 0, True)
            with e.Fori(1, ZPAIRS // ZUN - 1) as g:
                for k in range(ZUN):
                    z_step(g * ZUN + k, k, g, True, True)
            for k in range(ZUN):
                z_step(ZPAIRS - ZUN + k, k, ZPAIRS // ZUN - 1, True, k < ZUN - 2)
            z_probs(ZPAIRS - 1, 1, 1)
            z_ptev(ZPAIRS - 1)
            z_final(ZPAIRS - 1, ZUN - 1, 16 * ((ZPAIRS - 1) // 2))

            plans = {last: block_plan(last) for last in (False, True)}
            first_plan = bank_plan(PROLOGUE, 0, [])

            def evac(use, bank, gb):
                kind, idx, nxt = use
                n = gb + nxt
                if kind == "V":
                    e.wait_ge(S.v_mm, n * SLOTS + (idx + 1))
                    e.tensor_copy(v_sb[:, idx % PAIRS, :], ps_pr[bank][:]).then_inc(S.v_ev, 1)
                elif kind == "X":
                    hi, lo = (h_hi, h_lo) if idx < 2 else (c_hi, c_lo)
                    t = 256 * (idx % 2)
                    e.wait_ge(S.x_hi_ev, n * 4 + (idx + 1))
                    e.tensor_tensor(lo[:, :, t:t + 256], ps_pr[bank][:].rearrange("p (c t) -> p c t", c=DC),
                                    hi[:, :, t:t + 256].bitcast(F32), ALU.subtract).then_inc(S.x_ev, 1)

            def ln_stats(gb, p):
                if p == 0:
                    e.wait_ge(S.x_ld, gb * 16 + 16)
                ins = e.bn_stats(st6[:, p, :], x_st[:, p, :])
                if p == PAIRS - 1:
                    ins.then_inc(S.st_done, 1)

            def ln_mean(gb):
                ge_apart(e, S.st_done, gb + 1, S.apart_dve)
                for p in range(PAIRS):
                    ins = e.bn_aggr(mv[:, p, :], st6[:, p, :])
                ins.then_inc(S.mv_done, 1)

            def ln_normalise(gb):
                e.wait_ge(S.rs_done, gb + 1)
                for p in range(PAIRS):
                    ins = e.tensor_scalar(x_st[:, p, :], x_st[:, p, :], mv[:, p, 0:1], rstd[:, p:p + 1], ALU.subtract, ALU.mult)
                ins.then_inc(S.xn_done, 1)

            def x_out(gb):
                e.wait_ge(S.fin_done, gb + 1)
                e.wait_ge(S.res_ld, gb * 16 + 16)
                for i in range(2):
                    dst = x_st[:, 2 * i:2 * i + 2, :].rearrange("p a d -> p (a d)")
                    ins = e.tensor_tensor(dst, ps_o[i][:], dst, ALU.add)
                ins.then_inc(S.xout_done, 1)

            def logits(b):
                r = slice(64 * b, 64 * b + 64)
                return ps_l[r, :, 0:4 * KEYS].rearrange("p a (h c) -> p a h c", h=2)[:, :, :, KEYS * b:KEYS * b + KEYS]

            def dve_slot(gb, s, first, last, plan, uses, work=True):
                B = gb * SLOTS
                if work:
                    hg, p = s // PAIRS, s % PAIRS
                    e.wait_ge(S.qk_done, B + (s + 1))
                    for b in range(2):
                        r = slice(64 * b, 64 * b + 64)
                        ins = e.reduce_max(mx[r, :].rearrange("p (a h) -> p a h", a=2), logits(b), AX.X)
                    ins.then_inc(S.max_done, 1)
                    e.wait_ge(S.max_done, B + (s + 1))
                    for b in range(2):
                        r = slice(64 * b, 64 * b + 64)
                        top = mx[r, :].rearrange("p (a h) -> p a h", a=2).unsqueeze(3).to_broadcast([64, 2, 2, KEYS])
                        ins = e.tensor_tensor(s_sb[r, :, :].rearrange("p (a h) c -> p a h c", a=2), logits(b), top, ALU.subtract)
                    ins.then_inc(S.sub_done, 1)
                if s == 1 and not first:
                    x_out(gb - 1)
                if work:
                    e.wait_ge(S.exp_done, B + (s + 1))
                    e.reduce_sum(sm, s_sb[:], AX.X).then_inc(S.sum_done, 1)
                    e.wait_ge(S.sum_done, B + (s + 1))
                    e.reciprocal(rc, sm).then_inc(S.rec_done, 1)
                    e.wait_ge(S.rec_done, B + (s + 1))
                    if not (first and s == 0):
                        e.wait_ge(S.t_done, B + s)
                    for b in range(2):
                        r = slice(64 * b, 64 * b + 64)
                        e.tensor_tensor(p_sb[r, :, 64 * b:64 * b + 64], s_sb[r, :, 0:Q],
                                        rc[r, :].unsqueeze(2).to_broadcast([64, HG, Q]), ALU.mult)
                    if s == 0 and not first:
                        e.wait_ge(S.pbt_done, gb)
                    e.tensor_tensor(pb_sb[:, p, HG * hg:HG * hg + HG], s_sb[:, :, Q], rc, ALU.mult).then_inc(S.norm_done, 1)
                for u in uses[0] + uses[1]:
                    evac(u, plan[u][0], gb)
                if not (first and s == 0):
                    e.wait_ge(S.cxhi_done, B + s)
                    e.tensor_tensor(cx_lo[:], ps_c[:], cx_hi[:].bitcast(F32), ALU.subtract).then_inc(S.cxlo_done, 1)
                for u in uses[2]:
                    evac(u, plan[u][0], gb)
                if work and not last:
                    if 4 <= s < 8:
                        ln_stats(gb + 1, s - 4)
                    elif s == 8:
                        ln_mean(gb + 1)
                    elif s == 9:
                        ln_normalise(gb + 1)

            def dve_block(gb, first, last):
                for s in range(SLOTS):
                    dve_slot(gb, s, first, last, plans[last], projections(s, last))

            def split_low(n, layer):
                e.wait_ge(w_hi_ok[n], layer + 1)
                e.tensor_tensor(w_lo[n][:], w_raw[n][:], w_hi[n][:].bitcast(F32), ALU.subtract).then_inc(w_ok[n], 1)

            with e.Fori(0, LAYERS) as layer:
                g0 = layer * BLOCKS
                for p in range(PAIRS):
                    ln_stats(g0, p)
                ln_mean(g0)
                ln_normalise(g0)
                e.wait_ge(S.rows_t, layer + 1)
                e.tensor_copy(prm[:], ps_c[:, 0:5 * H]).then_inc(S.prm_ok, 1)
                e.memset(lmat[:], 0.0).then_inc(S.l_zero, 1)
                e.wait_ge(S.l_zero, layer + 1)
                e.wait_ge(S.prm_ok, layer + 1)
                e.tensor_tensor(lmat[:].rearrange("p h c -> p (h c)")[:, 0:H * (H + 1):H + 2],
                                prm[:, 3 * H:4 * H], prm[:, 4 * H:5 * H], ALU.subtract)
                e.tensor_copy(lmat[:, :, H], prm[:, 4 * H:5 * H]).then_inc(S.lmat_ok, 1)
                for n in "qkvo":
                    split_low(n, layer)
                for u in PROLOGUE:
                    evac(u, first_plan[u][0], g0)
                e.wait_ge(S.bw_mm, layer + 1)
                e.tensor_copy(bw_sb[0:H + 1, :], ps_c[0:H + 1, 0:D]).then_inc(S.bw_ok, 1)
                dve_block(g0, True, False)
                with e.Fori(1, BLOCKS - 1) as b:
                    dve_block(b + g0, False, False)
                gl = g0 + (BLOCKS - 1)
                dve_block(gl, False, True)
                dve_slot(gl, SLOTS, False, True, None, [[], [], []], work=False)
                x_out(gl)

            def m_stats(b):
                e.wait_ge(S.m_xld, b * 16 + 16)
                for p in range(PAIRS):
                    ins = e.bn_stats(st6[:, p, :], kv_st[:, p, :])
                ins.then_inc(S.m_st, 1)
                ge_apart(e, S.m_st, b + 1, S.apart_dve)
                for p in range(PAIRS):
                    ins = e.bn_aggr(mv[:, p, :], st6[:, p, :])
                ins.then_inc(S.m_mv, 1)

            def m_normalise(b):
                e.wait_ge(S.m_rs, b + 1)
                for p in range(PAIRS):
                    ins = e.tensor_scalar(kv_st[:, p, :], kv_st[:, p, :], mv[:, p, 0:1], rstd[:, p:p + 1], ALU.subtract, ALU.mult)
                ins.then_inc(S.m_xn, 1)

            def m_xlo(b):
                for i in range(2):
                    t = 256 * i
                    e.wait_ge(S.m_xhi, b * 2 + (i + 1))
                    e.tensor_tensor(h_lo[:, :, t:t + 256], ps_pr[i][:].rearrange("p (c t) -> p c t", c=DC),
                                    h_hi[:, :, t:t + 256].bitcast(F32), ALU.subtract).then_inc(S.m_xlo, 1)

            def m_split(b, j):
                e.wait_ge(S.m_gelu, b * FT + (j + 1))
                e.tensor_copy(g_hi[:, j, :], g_raw[:, j % 2, :]).then_inc(S.m_ghi, 1)
                e.wait_ge(S.m_ghi, b * FT + (j + 1))
                e.tensor_tensor(g_lo[:, j, :], g_raw[:, j % 2, :], g_hi[:, j, :].bitcast(F32), ALU.subtract).then_inc(S.m_glo, 1)

            def m_outs(b):
                e.wait_ge(S.m_res, b + 1)
                for i in range(2):
                    e.wait_ge(S.m_fc2, b * 2 + (i + 1))
                    dst = x_st[:, 2 * i:2 * i + 2, :].rearrange("p a d -> p (a d)")
                    e.tensor_tensor(dst, ps_o[i][:], dst, ALU.add).then_inc(S.m_out, 1)

            m_stats(0)
            m_normalise(0)
            e.wait_ge(S.m_w1h, 1)
            e.tensor_tensor(w1_lo[:], w1_raw[:], w1_hi[:].bitcast(F32), ALU.subtract).then_inc(S.m_w1, 1)
            e.wait_ge(S.m_w2h, 1)
            e.tensor_tensor(w2_lo[:], w2_raw[:], w2_hi[:].bitcast(F32), ALU.subtract).then_inc(S.m_w2, 1)
            e.wait_ge(S.m_b1t, 1)
            e.tensor_copy(b1_c[:], ps_c[:, 0:FT]).then_inc(S.m_b1, 1)
            m_xlo(0)
            m_stats(1)

            def m_block(b, b1, b2):
                for j in range(FT):
                    m_split(b, j)
                    if j == 0 and b1:
                        m_normalise(b + 1)
                if b1:
                    m_xlo(b + 1)
                if b2:
                    m_stats(b + 2)
                m_outs(b)

            with e.Fori(0, BLOCKS - 2) as b:
                m_block(b, True, True)
            m_block(BLOCKS - 2, True, False)
            m_block(BLOCKS - 1, False, False)

        @block.tensor
        def _(e):
            e.wait_ge(S.ident_ok, 1)
            e.wait_ge(S.z_wld, 16 * 16)
            for n in range(4):
                ins = e.transpose(ps_pr[0][:, P * n:P * n + P], z_w[:, n, :], ident[:])
            ins.then_inc(S.z_wt_mm, 1)
            e.wait_ge(S.z_wt_ev, 1)
            e.matmul(ps_pr[1][:, 0:P], z_w[:, 2, :], z_wt[:, 3, :], start=True, stop=True)
            e.matmul(ps_pr[1][:, P:P + 1], z_wt[:, 3, :], z_b[:, 2:3], start=True, stop=True).then_inc(S.z_wl_mm, 1)
            e.wait_ge(S.z_wl_ev, 1)
            e.wait_ge(S.z_bias, 1)

            def z_project(i, k, first):
                e.wait_ge(S.z_norm_x, i + 1)
                e.matmul(ps_pr[0][:, 0:256], z_wt[:, 0, :], z_xn[:], start=True, stop=True)
                e.matmul(ps_pr[0][:, 256:512], z_wt[:, 1, :], z_sn[:], start=True, stop=True).then_inc(S.z_s1, 1)
                if not first:
                    e.wait_ge(S.z_v_ev, i)
                for sc in range(2):
                    ins = e.matmul(ps_pr[1][:, P * sc:P * sc + P], z_s[:, k, P * sc:P * sc + P], z_wt[:, 2, :], start=True, stop=True)
                ins.then_inc(S.z_vmm, 1)

            def z_logits(i, first):
                e.wait_ge(S.z_m_ev, i + 1)
                for b in range(2):
                    if not first:
                        e.wait_ge(S.z_exp, i * 2 + (b - 1))
                    for tc in range(2):
                        ins = e.matmul(ps_l[:, b, 256 * tc:256 * tc + 256], z_mn[:, b, P * tc:P * tc + P], z_mm[:], start=True, stop=True)
                    ins.then_inc(S.z_l, 1)

            def z_transposes(i, par, first):
                for b in range(2):
                    e.wait_ge(S.z_normd, i * 2 + (b + 1))
                    if not first:
                        e.wait_ge(z_pt_ev[b], i)
                    dst = ps_t if b == 0 else ps_c
                    for sc in range(2):
                        for tc in range(2):
                            o = 256 * sc + P * tc
                            ins = e.transpose(dst[:, o:o + P], z_p[:, par, b, tc, P * sc:P * sc + P], ident[:])
                    ins.then_inc(S.z_t, 1)

            def z_values(i, k, first):
                for b in range(2):
                    e.wait_ge(z_pt_ev[b], i + 1)
                if not first:
                    e.wait_ge(S.z_outd, i)
                for b in range(2):
                    for sc in range(2):
                        ins = e.matmul(ps_o[0][64 * b:64 * b + 64, 0:256], z_v[:, k, sc, 64 * b:64 * b + 64], z_pt[:, b, sc, :],
                                       start=(sc == 0), stop=(sc == 1))
                ins.then_inc(S.z_pv, 1)

            def z_step(i, k, prev, prev_first, nxt):
                z_logits(i, not prev)
                if nxt:
                    z_project(i + 1, (k + 1) % ZUN, False)
                if prev:
                    z_transposes(i - 1, (k - 1) % 2, prev_first)
                    z_values(i - 1, (k - 1) % ZUN, prev_first)

            z_project(0, 0, True)
            for k in range(ZUN):
                z_step(k, k, k > 0, k == 1, True)
            with e.Fori(1, ZPAIRS // ZUN - 1) as g:
                for k in range(ZUN):
                    z_step(g * ZUN + k, k, True, False, True)
            for k in range(ZUN):
                z_step(ZPAIRS - ZUN + k, k, True, False, k < ZUN - 1)
            z_transposes(ZPAIRS - 1, 1, False)
            z_values(ZPAIRS - 1, ZUN - 1, False)

            plans = {last: block_plan(last) for last in (False, True)}
            first_plan = bank_plan(PROLOGUE, 0, [])

            def three(dst, pairs, inc=None):
                terms = [t for (a_hi, a_lo), (b_hi, b_lo) in pairs for t in ((a_hi, b_hi), (a_hi, b_lo), (a_lo, b_hi))]
                for n, (a, b) in enumerate(terms):
                    ins = e.matmul(dst, a, b, start=(n == 0), stop=(n == len(terms) - 1))
                if inc is not None:
                    ins.then_inc(inc, 1)

            def project(use, plan, gb):
                kind, idx, nxt = use
                bank, before = plan[use]
                n = gb + nxt
                if before is not None:
                    sem, count = evac_of(before, gb)
                    e.wait_ge(sem, count)
                dst = ps_pr[bank][:]
                if kind == "X":
                    src = x_st if idx < 2 else kv_st
                    if idx == 0:
                        e.wait_ge(S.xh_done, n + 1)
                    if idx == 2:
                        e.wait_ge(S.kv_ld, n * 16 + 16)
                    for c in range(DC):
                        for j in range(2):
                            o = 256 * c + P * j
                            ins = e.transpose(ps_pr[bank][:, o:o + P], src[:, 2 * (idx % 2) + j, P * c:P * c + P], ident[:])
                    ins.then_inc(S.x_mm, 1)
                    return
                if kind in "QK":
                    if idx == 0:
                        e.wait_ge(S.x_ev, n * 4 + (2 if kind == "Q" else 4))
                    w, sem = ("q", S.q_mm) if kind == "Q" else ("k", S.k_mm)
                    hi, lo = (h_hi, h_lo) if kind == "Q" else (c_hi, c_lo)
                    col = slice(K * idx, K * idx + K)
                    three(dst, [((w_hi[w][:, c, col], w_lo[w][:, c, col]), (hi[:, c, :], lo[:, c, :])) for c in range(DC)], sem)
                else:
                    if idx == 0:
                        e.wait_ge(S.x_ev, n * 4 + 4)
                    t = slice(P * (idx % PAIRS), P * (idx % PAIRS) + P)
                    col = slice(HG * K * (idx // PAIRS), HG * K * (idx // PAIRS) + HG * K)
                    three(dst, [((c_hi[:, c, t], c_lo[:, c, t]), (w_hi["v"][:, c, col], w_lo["v"][:, c, col])) for c in range(DC)], S.v_mm)

            def o_slot(gb, s, first):
                hg, p = s // PAIRS % GROUPS, s % PAIRS
                B = gb * SLOTS
                e.wait_ge(S.cxlo_done, B + (s + 1))
                if s == 0 and not first:
                    e.wait_ge(S.xout_done, gb)
                dst = ps_o[p // 2][:, D * (p % 2):D * (p % 2) + D]
                for hh in range(HG):
                    head = HG * hg + hh
                    col = slice(P * hh, P * hh + P)
                    for n, (a, b) in enumerate(((cx_hi, w_hi["o"]), (cx_hi, w_lo["o"]), (cx_lo, w_hi["o"]))):
                        ins = e.matmul(dst, a[:, col], b[:, head, :], start=(hg == 0 and p % 2 == 0 and hh == 0 and n == 0),
                                       stop=False, skip_group_check=True)
                ins.then_inc(S.o_done, 1)

            def pe_slot(gb, s, first, plan, uses, work=True):
                B = gb * SLOTS
                hg, p, par = s // PAIRS, s % PAIRS, s // PAIRS % 2
                if work:
                    if p == 0:
                        e.wait_ge(S.q_ev, B + (PAIRS * hg + HG))
                        e.wait_ge(S.k_ev, B + (PAIRS * hg + HG))
                        e.wait_ge(S.bias_col, gb * GROUPS + (hg + 1))
                    if not (first and s == 0):
                        e.wait_ge(S.sub_done, B + s)
                    for hh in range(HG):
                        o = 2 * KEYS * (hh % 2)
                        ins = e.matmul(ps_l[:, hh // 2, o:o + 2 * KEYS], q_sb[:, par, hh, P * p:P * p + P],
                                       k_sb[:, par, hh, 2 * p:2 * p + 2, :].rearrange("p a c -> p (a c)"), start=True, stop=True)
                    ins.then_inc(S.qk_done, 1)
                if not (first and s < 2):
                    o_slot(gb if s >= 2 else gb - 1, s - 2 if s >= 2 else s + 14, first)
                if s == SLOTS + 1 or (s == 1 and not first):
                    for pp in range(PAIRS):
                        ins = e.matmul(ps_o[pp // 2][:, D * (pp % 2):D * (pp % 2) + D], pbt_sb[:, P * pp:P * pp + P], bw_sb[:],
                                       start=False, stop=True, skip_group_check=True)
                    ins.then_inc(S.fin_done, 1)
                for u in uses[0]:
                    project(u, plan, gb)
                if not (first and s == 0) and s <= SLOTS:
                    e.wait_ge(S.norm_done, B + s)
                    if not (first and s == 1):
                        e.wait_ge(S.pt_ev, B + (s - 1))
                    for hh in range(HG):
                        ins = e.transpose(ps_t[:, P * hh:P * hh + P], p_sb[:, hh, :], ident[:])
                    ins.then_inc(S.t_done, 1)
                    if s % SLOTS == 0:
                        for pp in range(PAIRS):
                            ins = e.transpose(ps_c[0:H + 1, P * pp:P * pp + P], pb_sb[:, pp, :], ident[:])
                        ins.then_inc(S.pbt_done, 1)
                for u in uses[1]:
                    project(u, plan, gb)
                if not (first and s == 0) and s <= SLOTS:
                    e.wait_ge(S.pt_ev, B + s)
                    e.wait_ge(S.v_ev, B + s)
                    if s % SLOTS == 0:
                        e.wait_ge(S.pbt_ev, gb + s // SLOTS)
                    pp = (s - 1) % PAIRS
                    for hh in range(HG):
                        col = slice(P * hh, P * hh + P)
                        ins = e.matmul(ps_c[:, col], v_sb[:, pp, K * hh:K * hh + K], pt_sb[:, col], start=True, stop=True)
                    ins.then_inc(S.pv_done, 1)
                for u in uses[2]:
                    project(u, plan, gb)

            def pe_block(gb, first, last):
                for s in range(SLOTS):
                    pe_slot(gb, s, first, plans[last], projections(s, last))

            e.wait_ge(S.z_outd, ZPAIRS)
            e.transpose(ps_c[0:P, 0:P], ident[:], ident[:]).then_inc(S.layer_end, 1)
            with e.Fori(0, LAYERS) as layer:
                g0 = layer * BLOCKS
                e.wait_ge(S.rows_ld, layer * 16 + 16)
                e.transpose(ps_c[:, 0:5 * H], rows_sb[0:5 * H, :], ident[0:5 * H, 0:5 * H]).then_inc(S.rows_t, 1)
                for u in PROLOGUE:
                    if u[1] == 0 and u[0] in "QKV":
                        e.wait_ge(w_ok[u[0].lower()], layer + 1)
                    project(u, first_plan, g0)
                e.wait_ge(S.lmat_ok, layer + 1)
                e.wait_ge(S.wo_ok, layer + 1)
                e.wait_ge(S.bo_ld, layer * 16 + 16)
                for h in range(H):
                    for n, w in enumerate((w_hi["o"], w_lo["o"])):
                        e.matmul(ps_c[0:H + 1, 0:D], lmat[:, h, :], w[:, h, :].bitcast(F32), start=(h == 0 and n == 0), stop=False)
                e.matmul(ps_c[0:H + 1, 0:D], onehot[:], bo_row[:], start=False, stop=True).then_inc(S.bw_mm, 1)
                e.wait_ge(S.bw_ok, layer + 1)
                pe_block(g0, True, False)
                with e.Fori(1, BLOCKS - 1) as b:
                    pe_block(b + g0, False, False)
                gl = g0 + (BLOCKS - 1)
                pe_block(gl, False, True)
                pe_slot(gl, SLOTS, False, None, [[], [], []], work=False)
                pe_slot(gl, SLOTS + 1, False, None, [[], [], []], work=False)
                e.wait_ge(S.xout_done, g0 + BLOCKS)
                e.transpose(ps_c[0:P, 0:P], ident[:], ident[:]).then_inc(S.layer_end, 1)

            e.wait_ge(S.m_bld, 32)
            e.transpose(ps_c[:, 0:FT], b1_rows[:], ident[0:FT, 0:FT]).then_inc(S.m_b1t, 1)

            def m_transposes(b, first):
                e.wait_ge(S.m_xh, b + 1)
                for i in range(2):
                    if not first:
                        e.wait_ge(S.m_gelu, b * FT + (i - 1))
                    for c in range(DC):
                        for j in range(2):
                            o = 256 * c + P * j
                            ins = e.transpose(ps_pr[i][:, o:o + P], kv_st[:, 2 * i + j, P * c:P * c + P], ident[:])
                    ins.then_inc(S.m_x, 1)

            def m_block(b, first, last):
                for j in range(FT):
                    if j < 2:
                        e.wait_ge(S.m_xlo, b * 2 + 2)
                    else:
                        e.wait_ge(S.m_gelu, b * FT + (j - 1))
                    col = slice(P * j, P * j + P)
                    three(ps_pr[j % 2][:], [((w1_hi[:, c, col], w1_lo[:, c, col]), (h_hi[:, c, :], h_lo[:, c, :])) for c in range(DC)], S.m_fc1)
                if not last:
                    m_transposes(b + 1, False)
                e.wait_ge(S.m_glo, b * FT + FT)
                if not first:
                    e.wait_ge(S.m_out, b * 2)
                for p in range(PAIRS):
                    t = slice(P * p, P * p + P)
                    dst = ps_o[p // 2][:, D * (p % 2):D * (p % 2) + D]
                    three(dst, [((g_hi[:, j, t], g_lo[:, j, t]), (w2_hi[:, j, :], w2_lo[:, j, :])) for j in range(FT)],
                          S.m_fc2 if p % 2 else None)

            m_transposes(0, True)
            e.wait_ge(S.m_w1, 1)
            e.wait_ge(S.m_w2, 1)
            m_block(0, True, False)
            with e.Fori(1, BLOCKS - 1) as b:
                m_block(b, False, False)
            m_block(BLOCKS - 1, False, True)


def kernel(**inputs):
    import numpy as np
    import concourse.bacc as bacc
    from concourse.bass_utils import run_bass_kernel_spmd

    a = {k: np.asarray(v) for k, v in inputs.items()}
    z = lambda n: a["L0_xattn_" + n]
    w = lambda n: a["L1_xattn_" + n]
    heads = lambda n: w(n).reshape(H, K)
    arrays = {
        "x": a["x"].reshape(BATCH * Q, D),
        "ctx": a["ctx_2048"].reshape(BATCH * Q, D),
        "zw": np.stack([z("Wn"), z("Wm"), z("Wl"), z("Wo")]),
        "zb": np.stack([z("bn"), z("bm"), z("bl"), z("bo")]),
        "wq": np.stack([w("wq1"), w("wq2")]),
        "wk": np.stack([w("wk1"), w("wk2")]),
        "wv": np.stack([w("wv1"), w("wv2")]),
        "wo": np.stack([w("wo1"), w("wo2")]),
        "rows": np.stack([np.concatenate([heads(f"{n}{i}") for n in ("bq", "bk", "bias_k", "bias_v", "bv")]) for i in (1, 2)]),
        "ln": np.stack([np.stack([w(f"{n}_scale"), w(f"{n}_offset")]) for n in ("ln1", "ln2", "ln_mlp")]),
        "bo": np.stack([w("bo1"), w("bo2")]),
        "w1": w("w_fc1"),
        "w2": w("w_fc2"),
        "b1": w("b_fc1").reshape(FT, P),
        "b2": w("b_fc2"),
    }
    arrays = {k: np.ascontiguousarray(v) for k, v in arrays.items()}
    nc = bacc.Bacc("TRN2", target_bir_lowering=False, num_devices=1)
    args = {k: nc.dram_tensor(k, v.shape, mybir.dt.from_np(v.dtype), kind="ExternalInput").ap() for k, v in arrays.items()}
    out = nc.dram_tensor("out", (BATCH * Q, D), F32, kind="ExternalOutput").ap()
    build(nc, out=out, **args)
    r = run_bass_kernel_spmd(nc, [arrays], core_ids=[0])
    return r.results[0]["out"].reshape(BATCH, Q, D)
```

```python
import concourse.bass as bass
from concourse import mybir

F32 = mybir.dt.float32
F32R = mybir.dt.float32r
ACT = mybir.ActivationFunctionType
ALU = mybir.AluOpType
AX = mybir.AxisListType

P = 128
BATCH, Q, D = 64, 64, 256
H, K, F = 16, 128, 1024
LAYERS = 2
TOK = 512
BLOCKS = BATCH * Q // TOK
PAIRS = TOK // P
DC = D // P
HG = 4
GROUPS = H // HG
SLOTS = GROUPS * PAIRS
KEYS = Q + 1
FT = F // P
EPS = 1e-5
SCALE = float(K) ** -0.5
ZPAIRS = BATCH // 2
ZUN = 4



def projections(slot, last):
    if slot < 12:
        uses = ([("Q", slot + 4, 0)], [("K", slot + 4, 0)], [("V", slot + 3, 0)])
    elif slot == 12:
        uses = ([], [("X", 0, 1), ("X", 1, 1)], [("V", 15, 0), ("X", 2, 1), ("X", 3, 1)])
    elif slot == 13:
        uses = ([("Q", 0, 1), ("K", 0, 1)], [("Q", 1, 1)], [("V", 0, 1)])
    elif slot == 14:
        uses = ([("K", 1, 1), ("Q", 2, 1)], [("K", 2, 1)], [("V", 1, 1)])
    else:
        uses = ([("Q", 3, 1)], [("K", 3, 1)], [("V", 2, 1)])
    return [[u for u in part if not (last and u[2] and u[0] != "X")] for part in uses]


FIRST_X = [("X", n, 0) for n in range(4)]
PROLOGUE = [("Q", 0, 0), ("Q", 1, 0), ("K", 0, 0), ("Q", 2, 0), ("V", 0, 0), ("K", 1, 0), ("Q", 3, 0), ("K", 2, 0),
            ("V", 1, 0), ("K", 3, 0), ("V", 2, 0)]

TOP_SPLITS = [("k", 0), ("v", 0), ("k", 1)]
SLOT_SPLITS = {0: [("v", 1)], 1: [("o", 0)], 2: [("k", 2)], 4: [("v", 2)], 5: [("o", 1)], 6: [("k", 3)], 8: [("v", 3)],
               9: [("o", 2)], 12: [("o", 3)]}
Q_SPLIT_SLOT = 13


def bank_plan(uses, first_bank, before):
    seq = list(before)
    plan = {}
    for n, use in enumerate(uses):
        plan[use] = ((first_bank + n) % 2, seq[-2] if len(seq) > 1 else None)
        seq.append(use)
    return plan


def block_plan(last):
    uses = [u for s in range(SLOTS) for part in projections(s, last) for u in part]
    return bank_plan(uses, len(PROLOGUE) % 2, PROLOGUE[-2:])


def split_now(slot, first, last):
    if first:
        return SLOT_SPLITS.get(slot, [])
    return [("q", slot - Q_SPLIT_SLOT)] if last and slot >= Q_SPLIT_SLOT else []


def ge(engine, sem, value):
    if isinstance(value, int) and value <= 0:
        return
    engine.wait_ge(sem, value)


def ge_apart(engine, sem, value, apart):
    engine.wait_ge(sem, value)
    engine.sem_inc(apart, 1)


class Space:

    def __init__(self, nc, at):
        self.nc, self.at = nc, at

    def put(self, name, shape, dtype=F32, at=None):
        size = 4
        for n in shape[1:]:
            size *= n
        if at is None:
            at = self.at
            self.at += (size + 31) // 32 * 32
        t = self.nc.alloc_sbuf_tensor_at(name, shape, dtype, offset=at)
        t_at = at
        return t, t_at


def build(nc, x, ctx, zw, zb, weights, rows, ln, bo, b2, out):
    base = (nc.sbuf_base + 31) // 32 * 32
    sp = Space(nc, base)
    w_hi, w_lo, w_raw, w_at = {}, {}, {}, {}
    PIECE = DC * HG * K
    for n in "qkvo":
        w_hi[n], w_at[n] = sp.put("w_hi_" + n, [P, GROUPS, PIECE], F32R)
        w_lo[n], lo_at = sp.put("w_lo_" + n, [P, GROUPS, PIECE], F32R)
        w_raw[n], _ = sp.put("w_raw_" + n, [P, GROUPS, PIECE], F32, lo_at)
    q_sb, shared_at = sp.put("q_sb", [P, 2, HG, TOK])
    k_sb, _ = sp.put("k_sb", [P, 2, HG, 2 * PAIRS, KEYS])
    v_sb, v_at = sp.put("v_sb", [P, PAIRS, HG * K])
    rows_sb, _ = sp.put("rows_sb", [P, K], F32, v_at + 2 * HG * K * 4)
    h_hi, _ = sp.put("h_hi", [P, DC, TOK], F32R)
    h_lo, _ = sp.put("h_lo", [P, DC, TOK], F32R)
    c_hi, _ = sp.put("c_hi", [P, DC, TOK], F32R)
    c_lo, shared_end = sp.put("c_lo", [P, DC, TOK], F32R)
    shared_end += DC * TOK * 4
    x_st, _ = sp.put("x_st", [P, PAIRS, D])
    kv_st, _ = sp.put("kv_st", [P, PAIRS, D])
    ln_bc, _ = sp.put("ln_bc", [P, 2, D])
    s_sb, _ = sp.put("s_sb", [P, HG, KEYS])
    p_sb, _ = sp.put("p_sb", [P, HG, P])
    pt_sb, pt_at = sp.put("pt_sb", [P, HG * P])
    lmat, _ = sp.put("lmat", [P, H, H + 1], F32, pt_at)
    cx_hi, _ = sp.put("cx_hi", [P, HG * P], F32R)
    cx_lo, _ = sp.put("cx_lo", [P, HG * P], F32R)
    ident, _ = sp.put("ident", [P, P])
    pbt_sb, _ = sp.put("pbt_sb", [P, TOK])
    bw_sb, _ = sp.put("bw_sb", [P, D])
    pb_sb, _ = sp.put("pb_sb", [P, PAIRS, H + 2])
    prm, _ = sp.put("prm", [P, 5 * H])
    small, _ = sp.put("small", [P, 3, HG])
    mx, sm, rc = small[:, 0, :], small[:, 1, :], small[:, 2, :]
    st6, _ = sp.put("st6", [P, PAIRS, 6])
    mv, _ = sp.put("mv", [P, PAIRS, 2])
    rstd, _ = sp.put("rstd", [P, PAIRS])
    mhalf, _ = sp.put("mhalf", [P, PAIRS])
    assert sp.at <= nc.sbuf_usable_end, (sp.at, nc.sbuf_usable_end)
    bq_c, bk_c, bkey_c = prm[:, 0:H], prm[:, H:2 * H], prm[:, 2 * H:3 * H]

    zs = Space(nc, shared_at)
    z_x, _ = zs.put("z_x", [P, ZUN, D])
    z_s, _ = zs.put("z_s", [P, ZUN, D])
    z_o, _ = zs.put("z_o", [P, 2, D], F32, w_at["o"])
    z_v, _ = zs.put("z_v", [P, ZUN, 2, P])
    z_xn, _ = zs.put("z_xn", [P, D])
    z_sn, _ = zs.put("z_sn", [P, D])
    z_mn, _ = zs.put("z_mn", [P, 2, D])
    z_mm, _ = zs.put("z_mm", [P, D])
    z_p, _ = zs.put("z_p", [P, 2, 2, 2, D])
    z_pt, _ = zs.put("z_pt", [P, 2, 2, D])
    z_w, _ = zs.put("z_w", [P, 4, P])
    z_wt, _ = zs.put("z_wt", [P, 4, P])
    z_b, _ = zs.put("z_b", [P, 4])
    z_c, _ = zs.put("z_c", [P, 1])
    z_st6, _ = zs.put("z_st6", [P, 2, 6])
    z_mv, _ = zs.put("z_mv", [P, 2, 2, 2])
    z_rs, _ = zs.put("z_rs", [P, 2, 2])
    z_nmx, _ = zs.put("z_nmx", [P, 2, 2])
    z_mxv, _ = zs.put("z_mxv", [P, 2, 2])
    z_sum, _ = zs.put("z_sum", [P, 2, 2])
    z_rc, _ = zs.put("z_rc", [P, 2, 2])
    assert zs.at <= v_at + 2 * HG * K * 4

    g_hi, _ = sp.put("g_hi", [P, FT, TOK], F32R, w_at["k"])
    g_lo, _ = sp.put("g_lo", [P, FT, TOK], F32R, w_at["k"] + 16384)
    g_raw, _ = sp.put("g_raw", [P, 2, TOK], F32, w_at["v"])
    b2_bc, _ = sp.put("b2_bc", [P, D], F32, w_at["v"] + 4096)

    ps_pr = [nc.alloc_psum_tensor(f"ps_pr{i}", [P, 512], F32) for i in range(2)]
    ps_l = nc.alloc_psum_tensor("ps_l", [P, 2, 512], F32)
    ps_t = nc.alloc_psum_tensor("ps_t", [P, 512], F32)
    ps_c = nc.alloc_psum_tensor("ps_c", [P, 512], F32)
    ps_o = [nc.alloc_psum_tensor(f"ps_o{i}", [P, 512], F32) for i in range(2)]

    scr = nc.dram_tensor("x_scratch", (3 * BLOCKS, TOK, D), F32, kind="Internal").ap()

    names = """apart_dve apart_pool ident_ok consts_ok
    z_wld z_wt_mm z_wt_ev z_wl_mm z_wl_ev z_bias z_zero z_ld0 z_ld1 z_ld2 z_ld3 z_so0 z_so1
    z_st z_mvd z_eps z_rsd z_norm_x z_s1 z_vmm z_m_ev z_v_ev z_l z_max z_nmx_ok z_exp z_rec z_normd z_t z_pt_ev0 z_pt_ev1 z_pv z_outd
    wq_ld wk_ld wv_ld wo_ld wq_hi wk_hi wv_hi wo_hi wq_ok wk_ok wv_ok wo_ok rows_ld rows_t prm_ok l_zero lmat_ok bo_ld bw_mm bw_ok lnb_ld
    x_ld kv_ld res_ld x_st_ok st_done mv_done eps_done rs_done xn_done aff_done xh_done
    q_mm k_mm v_mm x_mm q_ev k_ev v_ev x_hi_ev x_ev bias_col qk_done max_done sub_done exp_done sum_done rec_done norm_done
    t_done pt_ev pv_done cxhi_done cxlo_done o_done pbt_done pbt_ev fin_done xout_done
    m_bld m_xld m_rld m_sto m_st m_mv m_eps m_rs m_xn m_aff m_xh m_x m_xhi m_xlo
    m_fc1 m_gelu m_ghi m_glo m_fc2 m_res m_out""".split()
    S = type("Semaphores", (), {n: nc.alloc_semaphore(n) for n in names})
    z_ld = [S.z_ld0, S.z_ld1, S.z_ld2, S.z_ld3]
    z_so = [S.z_so0, S.z_so1]
    z_pt_ev = [S.z_pt_ev0, S.z_pt_ev1]
    w_ld = {"q": S.wq_ld, "k": S.wk_ld, "v": S.wv_ld, "o": S.wo_ld}
    w_hi_ok = {"q": S.wq_hi, "k": S.wk_hi, "v": S.wv_hi, "o": S.wo_hi}
    w_ok = {"q": S.wq_ok, "k": S.wk_ok, "v": S.wv_ok, "o": S.wo_ok}

    tok = lambda a: a.rearrange("(j p) d -> p j d", p=P)
    xp = x.rearrange("(i p) d -> i p d", p=P)
    cp = ctx.rearrange("(i p) d -> i p d", p=P)
    cb = ctx.rearrange("(b t) d -> b t d", t=TOK)
    ob = out.rearrange("(b t) d -> b t d", t=TOK)
    sp_pairs = scr.rearrange("b (j p) d -> (b j) p d", p=P)

    def evac_of(use, gb):
        kind, idx, nxt = use
        sem = {"Q": S.q_ev, "K": S.k_ev, "V": S.v_ev, "X": S.x_ev}[kind]
        return sem, (gb + nxt) * (4 if kind == "X" else SLOTS) + idx + 1

    with nc.Block() as block:

        @block.sync
        def _(e):
            def load_w(n, stage):
                e.dma_start(w_raw[n][:].rearrange("p g c -> p (g c)"), weights[4 * stage + "qkvo".index(n)]).then_inc(w_ld[n], 16)

            def load_rows(stage):
                e.dma_start(rows_sb[0:5 * H, :], rows[stage]).then_inc(S.rows_ld, 16)

            def load_ln(stage):
                e.dma_start(ln_bc[:], ln[stage].partition_broadcast(P)).then_inc(S.lnb_ld, 16)

            def load_bo(layer):
                e.dma_start(bw_sb[H + 1:H + 2, :], bo[layer:layer + 1, :]).then_inc(S.bo_ld, 16)

            def z_load(i, k):
                e.dma_start(z_x[:, k, :], xp[i]).then_inc(z_ld[k], 16)
                e.dma_start(z_s[:, k, :], cp[i]).then_inc(z_ld[k], 16)

            def z_store(i, k):
                e.wait_ge(S.z_outd, i + 1)
                e.dma_start(sp_pairs[i], z_o[:, k % 2, :]).then_inc(z_so[k % 2], 16)

            for n in range(4):
                if n == 0:
                    e.wait_ge(S.z_zero, 1)
                for half in range(2):
                    r = slice(64 * half, 64 * half + 64)
                    e.dma_start(z_w[r, n, r], zw[n]).then_inc(S.z_wld, 16)
                    e.dma_start(z_b[r, n:n + 1], zb[n].rearrange("(p a) -> p a", a=1)).then_inc(S.z_wld, 16)
            for k in range(ZUN):
                z_load(k, k)
            load_ln(0)
            load_rows(0)
            e.wait_ge(S.consts_ok, 7)
            load_bo(0)
            for n in "qkvo":
                load_w(n, 0)
            def z_group(g):
                for k in range(ZUN):
                    z_store(g * ZUN + k, k)
                    z_load(g * ZUN + ZUN + k, k)

            with e.Fori(0, ZPAIRS // ZUN - 2) as g:
                z_group(g)
            for k in range(2):
                e.wait_ge(z_so[k], 16 * PAIRS // 2)
            e.dma_start(x_st[:], tok(scr[0])).then_inc(S.x_ld, 16)
            e.dma_start(kv_st[:], tok(cb[0])).then_inc(S.kv_ld, 16)
            z_group(ZPAIRS // ZUN - 2)
            for k in range(ZUN):
                z_store(ZPAIRS - ZUN + k, k)

            for k in range(2):
                e.wait_ge(z_so[k], 16 * ZPAIRS // 2)

            def store_out(gb):
                e.wait_ge(S.xout_done, gb + 1)
                e.dma_start(tok(scr[gb + BLOCKS]), x_st[:]).then_inc(S.x_st_ok, 16)

            def sp_block(gb, very_first, next_context):
                if very_first:
                    e.wait_ge(S.x_mm, 2)
                else:
                    store_out(gb - 1)
                    e.wait_ge(S.x_st_ok, gb * 16)
                e.dma_start(x_st[:], tok(scr[gb + 1])).then_inc(S.x_ld, 16)
                e.wait_ge(S.x_mm, gb * 4 + 4)
                e.dma_start(kv_st[:], tok(cb[next_context])).then_inc(S.kv_ld, 16)
                e.wait_ge(S.x_mm, gb * 4 + 6)
                e.dma_start(x_st[:], tok(scr[gb])).then_inc(S.res_ld, 16)

            for layer in range(LAYERS):
                g0 = layer * BLOCKS
                gl = g0 + BLOCKS - 1
                sp_block(g0, layer == 0, 1)
                with e.Fori(1, BLOCKS - 1) as b:
                    sp_block(b + g0, False, b + 1)
                e.wait_ge(S.xh_done, gl + 1)
                load_ln(layer + 1)
                sp_block(gl, False, 0)
                e.wait_ge(S.q_mm, (gl + 1) * SLOTS)
                load_w("q", layer + 1)
                if layer + 1 < LAYERS:
                    e.wait_ge(S.k_mm, (gl + 1) * SLOTS)
                    load_w("k", layer + 1)
                e.wait_ge(S.v_mm, (gl + 1) * SLOTS)
                if layer + 1 < LAYERS:
                    load_w("v", layer + 1)
                else:
                    e.dma_start(b2_bc[:], b2.partition_broadcast(P)).then_inc(S.m_bld, 16)
                e.wait_ge(S.pv_done, gl * SLOTS + (SLOTS - 1))
                load_rows(layer + 1)
                if layer + 1 < LAYERS:
                    e.wait_ge(S.o_done, (gl + 1) * SLOTS)
                    load_w("o", layer + 1)
                    e.wait_ge(S.fin_done, gl + 1)
                    load_bo(layer + 1)

            m0 = LAYERS * BLOCKS

            def m_load(b):
                e.dma_start(kv_st[:], tok(scr[b + m0])).then_inc(S.m_xld, 16)

            e.wait_ge(S.x_mm, m0 * 4 + 4)
            m_load(1)
            store_out(m0 - 1)
            e.wait_ge(S.x_st_ok, m0 * 16)
            e.dma_start(x_st[:], tok(scr[m0])).then_inc(S.m_rld, 16)

            def m_store(b):
                e.wait_ge(S.m_out, b * 2 + 2)
                e.dma_start(tok(ob[b]), x_st[:]).then_inc(S.m_sto, 16)
                e.wait_ge(S.m_sto, b * 16 + 16)

            def m_residual(b):
                m_store(b - 1)
                e.dma_start(x_st[:], tok(scr[b + m0])).then_inc(S.m_rld, 16)

            with e.Fori(1, BLOCKS - 1) as b:
                e.wait_ge(S.m_x, b * 2)
                m_load(b + 1)
                m_residual(b)
            m_residual(BLOCKS - 1)
            m_store(BLOCKS - 1)

        @block.gpsimd
        def _(e):
            e.memset(z_w[:], 0.0).then_inc(S.z_zero, 1)
            e.memset(ident[:], 0.0).then_inc(S.consts_ok, 1)
            e.memset(p_sb[:], 0.0).then_inc(S.consts_ok, 1)
            e.memset(pbt_sb[:], 0.0).then_inc(S.consts_ok, 1)
            e.memset(bw_sb[:], 0.0).then_inc(S.consts_ok, 1)
            e.memset(pb_sb[:], 1.0).then_inc(S.consts_ok, 1)
            e.memset(mhalf[:], -0.5).then_inc(S.consts_ok, 1)
            e.memset(z_mn[:], 0.0).then_inc(S.consts_ok, 1)
            e.wait_ge(S.consts_ok, 7)
            e.affine_select(out=ident[:], in_=ident[:], compare_op=ALU.not_equal, fill=1.0, base=0,
                            pattern=[[-1, P]], channel_multiplier=1).then_inc(S.ident_ok, 1)

            def z_rstd(i, par):
                ge_apart(e, S.z_mvd, i + 1, S.apart_pool)
                e.tensor_scalar(z_rs[:, par, :], z_mv[:, par, :, 1], EPS, None, ALU.add).then_inc(S.z_eps, 1)
                e.wait_ge(S.z_eps, i + 1)
                e.tensor_tensor(z_rs[:, par, :], z_rs[:, par, :], mhalf[:, 0:2], ALU.pow).then_inc(S.z_rsd, 1)

            def rstd_of(n):
                ge_apart(e, S.mv_done, n, S.apart_pool)
                e.tensor_scalar(rstd[:], mv[:, :, 1], EPS, None, ALU.add).then_inc(S.eps_done, 1)
                e.wait_ge(S.eps_done, n)
                e.tensor_tensor(rstd[:], rstd[:], mhalf[:], ALU.pow).then_inc(S.rs_done, 1)

            def affine(n):
                e.wait_ge(S.xn_done, n)
                e.tensor_tensor(x_st[:], x_st[:], ln_bc[:, 0:1, :].to_broadcast([P, PAIRS, D]), ALU.mult).then_inc(S.aff_done, 1)
                e.wait_ge(S.aff_done, n)
                e.tensor_tensor(x_st[:], x_st[:], ln_bc[:, 1:2, :].to_broadcast([P, PAIRS, D]), ALU.add).then_inc(S.xh_done, 1)

            def bias_columns(hg):
                par = hg % 2
                e.tensor_copy(k_sb[:, par, :, :, Q], bkey_c[:, HG * hg:HG * hg + HG].unsqueeze(2)
                              .to_broadcast([P, HG, 2 * PAIRS])).then_inc(S.bias_col, 1)

            def pool_block(gb, first, last, layer):
                for hg in (1, 2):
                    if not (first and hg == 1):
                        ge_apart(e, S.qk_done, gb * SLOTS + PAIRS * (hg - 1), S.apart_pool)
                    bias_columns(hg)
                rstd_of(gb + 2)
                ge_apart(e, S.qk_done, gb * SLOTS + PAIRS * 2, S.apart_pool)
                bias_columns(3)
                if last:
                    e.wait_ge(S.lnb_ld, layer * 16 + 32)
                affine(gb + 2)
                if not last:
                    ge_apart(e, S.qk_done, gb * SLOTS + PAIRS * 3, S.apart_pool)
                    bias_columns(0)

            with e.Fori(0, ZPAIRS // 2 - 1) as g:
                for k in range(2):
                    z_rstd(g * 2 + k, k)
            rstd_of(1)
            for k in range(2):
                z_rstd(ZPAIRS - 2 + k, k)
            e.wait_ge(S.lnb_ld, 16)
            affine(1)

            with e.Fori(0, LAYERS) as layer:
                g0 = layer * BLOCKS
                ge_apart(e, S.prm_ok, layer + 1, S.apart_pool)
                bias_columns(0)
                pool_block(g0, True, False, layer)
                with e.Fori(1, BLOCKS - 1) as b:
                    pool_block(b + g0, False, False, layer)
                pool_block(g0 + (BLOCKS - 1), False, True, layer)

            def m_norm(n):
                ge_apart(e, S.m_mv, n, S.apart_pool)
                e.tensor_scalar(rstd[:], mv[:, :, 1], EPS, None, ALU.add).then_inc(S.m_eps, 1)
                e.wait_ge(S.m_eps, n)
                e.tensor_tensor(rstd[:], rstd[:], mhalf[:], ALU.pow).then_inc(S.m_rs, 1)
                e.wait_ge(S.m_xn, n)
                e.tensor_tensor(kv_st[:], kv_st[:], ln_bc[:, 0:1, :].to_broadcast([P, PAIRS, D]), ALU.mult).then_inc(S.m_aff, 1)
                e.wait_ge(S.m_aff, n)
                e.tensor_tensor(kv_st[:], kv_st[:], ln_bc[:, 1:2, :].to_broadcast([P, PAIRS, D]), ALU.add).then_inc(S.m_xh, 1)

            def m_residual(n):
                e.wait_ge(S.m_rld, n * 16)
                e.tensor_tensor(x_st[:], x_st[:], b2_bc[:].unsqueeze(1).to_broadcast([P, PAIRS, D]), ALU.add).then_inc(S.m_res, 1)

            e.wait_ge(S.m_bld, 16)
            with e.Fori(0, BLOCKS - 1) as b:
                m_norm(b + 1)
                m_residual(b + 1)
            m_residual(BLOCKS)

        @block.scalar
        def _(e):
            def z_exp(i, par, b):
                e.wait_ge(S.z_nmx_ok, i * 2 + (b + 1))
                for tc in range(2):
                    ins = e.activation(z_p[:, par, b, tc, :], ps_l[:, b, 256 * tc:256 * tc + 256], ACT.Exp,
                                       bias=z_nmx[:, b, tc:tc + 1], accum_out=z_sum[:, b, tc:tc + 1])
                ins.then_inc(S.z_exp, 1)

            def z_ptev(i):
                e.wait_ge(S.z_t, i * 2 + 2)
                e.activation(z_pt[:, 1].rearrange("p a t -> p (a t)"), ps_c[:], ACT.Copy).then_inc(S.z_pt_ev1, 1)

            def z_evac_m(i):
                e.wait_ge(S.z_s1, i + 1)
                for b in range(2):
                    r = slice(64 * b, 64 * b + 64)
                    e.activation(z_mn[r, b, :], ps_pr[0][r, 0:256], ACT.Identity, bias=z_b[r, 0:1])
                e.activation(z_mm[:], ps_pr[0][:, 256:512], ACT.Identity, bias=z_b[:, 1:2]).then_inc(S.z_m_ev, 1)

            def z_evac_v(i, k):
                e.wait_ge(S.z_vmm, i + 1)
                e.activation(z_v[:, k].rearrange("p a b -> p (a b)"), ps_pr[1][:, 0:256], ACT.Copy).then_inc(S.z_v_ev, 1)

            e.wait_ge(S.z_wt_mm, 1)
            e.activation(z_wt[:].rearrange("p a b -> p (a b)"), ps_pr[0][:], ACT.Copy).then_inc(S.z_wt_ev, 1)
            e.wait_ge(S.z_wl_mm, 1)
            e.activation(z_wt[:, 2, :], ps_pr[1][:, 0:128], ACT.Copy).then_inc(S.z_wl_ev, 1)
            e.activation(z_c[:], ps_pr[1][:, 128:129], ACT.Identity, bias=z_b[:, 3:4]).then_inc(S.z_bias, 1)
            e.wait_ge(S.consts_ok, 7)
            z_evac_m(0)
            z_evac_v(0, 0)
            plans = {last: block_plan(last) for last in (False, True)}
            first_plan = bank_plan(FIRST_X + PROLOGUE, 0, [])

            def split_high(n, group, stage):
                if group == 0:
                    e.wait_ge(w_ld[n], stage * 16 + 16)
                e.activation(w_hi[n][:, group, :], w_raw[n][:, group, :], ACT.Copy).then_inc(w_hi_ok[n], 1)

            def evac(use, bank, gb):
                kind, idx, nxt = use
                n = gb + nxt
                if kind == "Q":
                    e.wait_ge(S.q_mm, n * SLOTS + (idx + 1))
                    e.activation(q_sb[:, idx // HG % 2, idx % HG, :], ps_pr[bank][:], ACT.Identity,
                                 bias=bq_c[:, idx:idx + 1]).then_inc(S.q_ev, 1)
                elif kind == "K":
                    e.wait_ge(S.k_mm, n * SLOTS + (idx + 1))
                    e.activation(k_sb[:, idx // HG % 2, idx % HG, :, 0:Q], ps_pr[bank][:].rearrange("p (a c) -> p a c", c=Q),
                                 ACT.Identity, bias=bk_c[:, idx:idx + 1]).then_inc(S.k_ev, 1)
                elif kind == "X":
                    dst = h_hi if idx < 2 else c_hi
                    t = 256 * (idx % 2)
                    e.wait_ge(S.x_mm, n * 4 + (idx + 1))
                    e.activation(dst[:, :, t:t + 256], ps_pr[bank][:].rearrange("p (c t) -> p c t", c=DC), ACT.Copy).then_inc(S.x_hi_ev, 1)

            def z_step(i, k, prev, nxt):
                z_exp(i, k % 2, 0)
                if nxt:
                    z_evac_m(i + 1)
                if prev:
                    z_ptev(i - 1)
                z_exp(i, k % 2, 1)
                if nxt:
                    z_evac_v(i + 1, (k + 1) % ZUN)

            for k in range(ZUN):
                z_step(k, k, k > 0, True)
            with e.Fori(1, ZPAIRS // ZUN - 1) as g:
                for k in range(ZUN):
                    z_step(g * ZUN + k, k, True, True)
            for k in range(ZUN):
                z_step(ZPAIRS - ZUN + k, k, True, k < ZUN - 1)
                split_high("q", k, 0)
            for u in FIRST_X[0:2]:
                evac(u, first_plan[u][0], 0)
            z_ptev(ZPAIRS - 1)
            for u in FIRST_X[2:4]:
                evac(u, first_plan[u][0], 0)


            def act_slot(gb, s, first, last, layer, plan, uses, work=True):
                B = gb * SLOTS
                if work:
                    e.wait_ge(S.sub_done, B + (s + 1))
                    e.activation(s_sb[:], s_sb[:], ACT.Exp, scale=SCALE).then_inc(S.exp_done, 1)
                for u in uses[0]:
                    evac(u, plan[u][0], gb)
                if not (first and s == 0) and s < 17:
                    e.wait_ge(S.t_done, B + s)
                    if not (first and s == 1):
                        e.wait_ge(S.pv_done, B + (s - 1))
                    e.activation(pt_sb[:], ps_t[:], ACT.Copy).then_inc(S.pt_ev, 1)
                    if s in (0, SLOTS):
                        nb = gb if s == 0 else gb + 1
                        e.wait_ge(S.pbt_done, nb)
                        e.activation(pbt_sb[0:H + 2, :], ps_c[0:H + 2, :], ACT.Copy).then_inc(S.pbt_ev, 1)
                for u in uses[1]:
                    evac(u, plan[u][0], gb)
                if not (first and s == 0) and s < 17:
                    e.wait_ge(S.pv_done, B + s)
                    if not (first and s == 1):
                        e.wait_ge(S.o_done, B + (s - 1))
                    e.activation(cx_hi[:], ps_c[:], ACT.Copy).then_inc(S.cxhi_done, 1)
                for u in uses[2]:
                    evac(u, plan[u][0], gb)
                for n, group in split_now(s, first, last):
                    split_high(n, group, layer + 1 if last else layer)

            def act_block(gb, first, last, layer):
                for s in range(SLOTS):
                    act_slot(gb, s, first, last, layer, plans[last], projections(s, last))

            with e.Fori(0, LAYERS) as layer:
                g0 = layer * BLOCKS
                for n, group in TOP_SPLITS:
                    split_high(n, group, layer)
                e.wait_ge(S.prm_ok, layer + 1)
                for u in PROLOGUE:
                    evac(u, first_plan[u][0], g0)
                act_block(g0, True, False, layer)
                with e.Fori(1, BLOCKS - 1) as b:
                    act_block(b + g0, False, False, layer)
                act_block(g0 + (BLOCKS - 1), False, True, layer)
                act_slot(g0 + (BLOCKS - 1), SLOTS, False, True, layer, None, [[], [], []], work=False)

            def m_xhi(b, i):
                e.wait_ge(S.m_x, b * 2 + (i - 1))
                e.activation(h_hi[:, :, 256 * i:256 * i + 256], ps_pr[i][:].rearrange("p (c t) -> p c t", c=DC), ACT.Copy).then_inc(S.m_xhi, 1)

            def m_gelu(b, first):
                for j in range(FT):
                    e.wait_ge(S.m_fc1, b * FT + (j + 1))
                    if not (first and j < 2):
                        e.wait_ge(S.m_glo, b * FT + (j - 1))
                    e.activation(g_raw[:, j % 2, :], ps_pr[j % 2][:], ACT.Gelu, bias=prm[:, j:j + 1]).then_inc(S.m_gelu, 1)

            e.wait_ge(S.prm_ok, LAYERS + 1)
            m_gelu(0, True)
            with e.Fori(1, BLOCKS) as b:
                m_xhi(b, 0)
                m_xhi(b, 1)
                m_gelu(b, False)

        @block.vector
        def _(e):
            def z_stats(i, k, rnd, par):
                e.wait_ge(z_ld[k], rnd * 32 + 32)
                ge(e, S.z_mvd, i)
                e.bn_stats(z_st6[:, 0, :], z_x[:, k, :])
                e.bn_stats(z_st6[:, 1, :], z_s[:, k, :]).then_inc(S.z_st, 1)
                ge_apart(e, S.z_st, i + 1, S.apart_dve)
                e.bn_aggr(z_mv[:, par, 0, :], z_st6[:, 0, :])
                e.bn_aggr(z_mv[:, par, 1, :], z_st6[:, 1, :]).then_inc(S.z_mvd, 1)

            def z_normalise(i, k, par):
                e.wait_ge(S.z_rsd, i + 1)
                ge(e, S.z_s1, i)
                for j, (dst, src) in enumerate(((z_xn, z_x), (z_sn, z_s))):
                    ins = e.tensor_scalar(dst[:], src[:, k, :], z_mv[:, par, j, 0:1], z_rs[:, par, j:j + 1], ALU.subtract, ALU.mult)
                ins.then_inc(S.z_norm_x, 1)

            def z_max(i, b):
                e.wait_ge(S.z_l, i * 2 + (b + 1))
                e.reduce_max(z_mxv[:, b, :], ps_l[:, b, :].rearrange("p (a s) -> p a s", a=2), AX.X).then_inc(S.z_max, 1)
                e.wait_ge(S.z_max, i * 2 + (b + 1))
                e.tensor_scalar(z_nmx[:, b, :], z_mxv[:, b, :], -1.0, None, ALU.mult).then_inc(S.z_nmx_ok, 1)

            def z_probs(i, par, b):
                e.wait_ge(S.z_exp, i * 2 + (b + 1))
                e.reciprocal(z_rc[:, b, :], z_sum[:, b, :]).then_inc(S.z_rec, 1)
                e.wait_ge(S.z_rec, i * 2 + (b + 1))
                for tc in range(2):
                    ins = e.tensor_scalar(z_p[:, par, b, tc, :], z_p[:, par, b, tc, :], z_rc[:, b, tc:tc + 1], None, ALU.mult)
                ins.then_inc(S.z_normd, 1)

            def z_ptev(i):
                e.wait_ge(S.z_t, i * 2 + 1)
                e.tensor_copy(z_pt[:, 0].rearrange("p a t -> p (a t)"), ps_t[:]).then_inc(S.z_pt_ev0, 1)

            def z_final(i, k, stored):
                e.wait_ge(S.z_pv, i + 1)
                ge(e, z_so[k % 2], stored)
                e.scalar_tensor_tensor(out=z_o[:, k % 2, :], in0=ps_o[0][:, 0:256], scalar=z_c[:, 0:1], in1=z_x[:, k, :],
                                       op0=ALU.add, op1=ALU.add).then_inc(S.z_outd, 1)

            plans = {last: block_plan(last) for last in (False, True)}
            first_plan = bank_plan(FIRST_X + PROLOGUE, 0, [])

            def evac(use, bank, gb):
                kind, idx, nxt = use
                n = gb + nxt
                if kind == "V":
                    e.wait_ge(S.v_mm, n * SLOTS + (idx + 1))
                    e.tensor_copy(v_sb[:, idx % PAIRS, :], ps_pr[bank][:]).then_inc(S.v_ev, 1)
                elif kind == "X":
                    hi, lo = (h_hi, h_lo) if idx < 2 else (c_hi, c_lo)
                    t = 256 * (idx % 2)
                    e.wait_ge(S.x_hi_ev, n * 4 + (idx + 1))
                    e.tensor_tensor(lo[:, :, t:t + 256], ps_pr[bank][:].rearrange("p (c t) -> p c t", c=DC),
                                    hi[:, :, t:t + 256].bitcast(F32), ALU.subtract).then_inc(S.x_ev, 1)

            def ln_stats(gb, p):
                if p == 0:
                    e.wait_ge(S.x_ld, gb * 16 + 16)
                ins = e.bn_stats(st6[:, p, :], x_st[:, p, :])
                if p == PAIRS - 1:
                    ins.then_inc(S.st_done, 1)

            def ln_mean(gb):
                ge_apart(e, S.st_done, gb + 1, S.apart_dve)
                for p in range(PAIRS):
                    ins = e.bn_aggr(mv[:, p, :], st6[:, p, :])
                ins.then_inc(S.mv_done, 1)

            def ln_normalise(gb):
                e.wait_ge(S.rs_done, gb + 1)
                for p in range(PAIRS):
                    ins = e.tensor_scalar(x_st[:, p, :], x_st[:, p, :], mv[:, p, 0:1], rstd[:, p:p + 1], ALU.subtract, ALU.mult)
                ins.then_inc(S.xn_done, 1)

            def parameters(stage):
                e.wait_ge(S.rows_t, stage + 1)
                e.tensor_copy(prm[:], ps_t[:, 0:5 * H]).then_inc(S.prm_ok, 1)

            def split_low(n, group, stage):
                e.wait_ge(w_hi_ok[n], stage * GROUPS + (group + 1))
                if n == "o" and group == 0:
                    e.wait_ge(S.bw_mm, stage + 1)
                e.tensor_tensor(w_lo[n][:, group, :], w_raw[n][:, group, :], w_hi[n][:, group, :].bitcast(F32), ALU.subtract).then_inc(w_ok[n], 1)

            def z_step(i, k, rnd, prev, nxt2):
                z_max(i, 0)
                if prev:
                    z_probs(i - 1, (k - 1) % 2, 1)
                z_max(i, 1)
                if prev:
                    z_ptev(i - 1)
                if nxt2:
                    z_stats(i + 2, (k + 2) % ZUN, rnd + (k + 2) // ZUN, k % 2)
                z_probs(i, k % 2, 0)
                if prev:
                    z_final(i - 1, (k - 1) % ZUN, (rnd * (ZUN // 2) + (k - 1) // 2) * 16)
                if nxt2:
                    z_normalise(i + 2, (k + 2) % ZUN, k % 2)

            z_stats(0, 0, 0, 0)
            z_stats(1, 1, 0, 1)
            z_normalise(0, 0, 0)
            z_normalise(1, 1, 1)
            e.wait_ge(S.z_bias, 1)
            for k in range(ZUN):
                z_step(k, k, 0, k > 0, True)
            with e.Fori(1, ZPAIRS // ZUN - 1) as g:
                for k in range(ZUN):
                    z_step(g * ZUN + k, k, g, True, True)
            for k in range(ZUN):
                if k == 0:
                    for p in range(PAIRS):
                        ln_stats(0, p)
                    ln_mean(0)
                elif k == 1:
                    ln_normalise(0)
                z_step(ZPAIRS - ZUN + k, k, ZPAIRS // ZUN - 1, True, k < ZUN - 2)
            z_probs(ZPAIRS - 1, 1, 1)
            z_ptev(ZPAIRS - 1)
            for u in FIRST_X[0:2]:
                evac(u, first_plan[u][0], 0)
            z_final(ZPAIRS - 1, ZUN - 1, 16 * ((ZPAIRS - 1) // 2))
            for u in FIRST_X[2:4]:
                evac(u, first_plan[u][0], 0)
            parameters(0)
            for group in range(GROUPS):
                split_low("q", group, 0)

            def x_out(gb):
                e.wait_ge(S.fin_done, gb + 1)
                e.wait_ge(S.res_ld, gb * 16 + 16)
                for i in range(2):
                    dst = x_st[:, 2 * i:2 * i + 2, :].rearrange("p a d -> p (a d)")
                    ins = e.tensor_tensor(dst, ps_o[i][:], dst, ALU.add)
                ins.then_inc(S.xout_done, 1)

            def logits(b):
                r = slice(64 * b, 64 * b + 64)
                return ps_l[r, :, 0:4 * KEYS].rearrange("p a (h c) -> p a h c", h=2)[:, :, :, KEYS * b:KEYS * b + KEYS]

            def dve_slot(gb, s, first, last, layer, plan, uses, work=True):
                B = gb * SLOTS
                if work:
                    hg, p = s // PAIRS, s % PAIRS
                    e.wait_ge(S.qk_done, B + (s + 1))
                    for b in range(2):
                        r = slice(64 * b, 64 * b + 64)
                        ins = e.reduce_max(mx[r, :].rearrange("p (a h) -> p a h", a=2), logits(b), AX.X)
                    ins.then_inc(S.max_done, 1)
                    e.wait_ge(S.max_done, B + (s + 1))
                    for b in range(2):
                        r = slice(64 * b, 64 * b + 64)
                        top = mx[r, :].rearrange("p (a h) -> p a h", a=2).unsqueeze(3).to_broadcast([64, 2, 2, KEYS])
                        ins = e.tensor_tensor(s_sb[r, :, :].rearrange("p (a h) c -> p a h c", a=2), logits(b), top, ALU.subtract)
                    ins.then_inc(S.sub_done, 1)
                if s == 1 and not first:
                    x_out(gb - 1)
                if work:
                    e.wait_ge(S.exp_done, B + (s + 1))
                    e.reduce_sum(sm, s_sb[:], AX.X).then_inc(S.sum_done, 1)
                    e.wait_ge(S.sum_done, B + (s + 1))
                    e.reciprocal(rc, sm).then_inc(S.rec_done, 1)
                    e.wait_ge(S.rec_done, B + (s + 1))
                    if not (first and s == 0):
                        e.wait_ge(S.t_done, B + s)
                    for b in range(2):
                        r = slice(64 * b, 64 * b + 64)
                        e.tensor_tensor(p_sb[r, :, 64 * b:64 * b + 64], s_sb[r, :, 0:Q],
                                        rc[r, :].unsqueeze(2).to_broadcast([64, HG, Q]), ALU.mult)
                    if s == 0 and not first:
                        e.wait_ge(S.pbt_done, gb)
                    e.tensor_tensor(pb_sb[:, p, HG * hg:HG * hg + HG], s_sb[:, :, Q], rc, ALU.mult).then_inc(S.norm_done, 1)
                for u in uses[0] + uses[1]:
                    evac(u, plan[u][0], gb)
                if not (first and s == 0):
                    e.wait_ge(S.cxhi_done, B + s)
                    e.tensor_tensor(cx_lo[:], ps_c[:], cx_hi[:].bitcast(F32), ALU.subtract).then_inc(S.cxlo_done, 1)
                for u in uses[2]:
                    evac(u, plan[u][0], gb)
                if first and s == 0:
                    e.wait_ge(S.bw_mm, layer + 1)
                    e.tensor_copy(bw_sb[0:H + 1, :], ps_c[0:H + 1, 0:D]).then_inc(S.bw_ok, 1)
                for n, group in split_now(s, first, last):
                    split_low(n, group, layer + 1 if last else layer)
                if work:
                    if 4 <= s < 8:
                        ln_stats(gb + 1, s - 4)
                    elif s == 8:
                        ln_mean(gb + 1)
                    elif s == 9:
                        ln_normalise(gb + 1)

            def dve_block(gb, first, last, layer):
                for s in range(SLOTS):
                    dve_slot(gb, s, first, last, layer, plans[last], projections(s, last))

            with e.Fori(0, LAYERS) as layer:
                g0 = layer * BLOCKS
                for n, group in TOP_SPLITS:
                    split_low(n, group, layer)
                e.memset(lmat[:], 0.0).then_inc(S.l_zero, 1)
                e.wait_ge(S.l_zero, layer + 1)
                e.wait_ge(S.prm_ok, layer + 1)
                e.tensor_tensor(lmat[:].rearrange("p h c -> p (h c)")[:, 0:H * (H + 1):H + 2],
                                prm[:, 3 * H:4 * H], prm[:, 4 * H:5 * H], ALU.subtract)
                e.tensor_copy(lmat[:, :, H], prm[:, 4 * H:5 * H]).then_inc(S.lmat_ok, 1)
                for u in PROLOGUE:
                    evac(u, first_plan[u][0], g0)
                dve_block(g0, True, False, layer)
                with e.Fori(1, BLOCKS - 1) as b:
                    dve_block(b + g0, False, False, layer)
                gl = g0 + (BLOCKS - 1)
                dve_block(gl, False, True, layer)
                dve_slot(gl, SLOTS, False, True, layer, None, [[], [], []], work=False)
                parameters(layer + 1)
                x_out(gl)

            def m_stats(b):
                e.wait_ge(S.m_xld, b * 16)
                for p in range(PAIRS):
                    ins = e.bn_stats(st6[:, p, :], kv_st[:, p, :])
                ins.then_inc(S.m_st, 1)
                ge_apart(e, S.m_st, b, S.apart_dve)
                for p in range(PAIRS):
                    ins = e.bn_aggr(mv[:, p, :], st6[:, p, :])
                ins.then_inc(S.m_mv, 1)

            def m_normalise(b):
                e.wait_ge(S.m_rs, b)
                for p in range(PAIRS):
                    ins = e.tensor_scalar(kv_st[:, p, :], kv_st[:, p, :], mv[:, p, 0:1], rstd[:, p:p + 1], ALU.subtract, ALU.mult)
                ins.then_inc(S.m_xn, 1)

            def m_xlo(b):
                for i in range(2):
                    t = 256 * i
                    e.wait_ge(S.m_xhi, b * 2 + (i - 1))
                    e.tensor_tensor(h_lo[:, :, t:t + 256], ps_pr[i][:].rearrange("p (c t) -> p c t", c=DC),
                                    h_hi[:, :, t:t + 256].bitcast(F32), ALU.subtract).then_inc(S.m_xlo, 1)

            def m_split(b, j):
                e.wait_ge(S.m_gelu, b * FT + (j + 1))
                e.tensor_copy(g_hi[:, j, :], g_raw[:, j % 2, :]).then_inc(S.m_ghi, 1)
                e.wait_ge(S.m_ghi, b * FT + (j + 1))
                e.tensor_tensor(g_lo[:, j, :], g_raw[:, j % 2, :], g_hi[:, j, :].bitcast(F32), ALU.subtract).then_inc(S.m_glo, 1)

            def m_outs(b, norm_next):
                e.wait_ge(S.m_res, b + 1)
                for i in range(2):
                    e.wait_ge(S.m_fc2, b * 2 + (i + 1))
                    dst = x_st[:, 2 * i:2 * i + 2, :].rearrange("p a d -> p (a d)")
                    e.tensor_tensor(dst, ps_o[i][:], dst, ALU.add).then_inc(S.m_out, 1)
                    if i == 0 and norm_next:
                        m_normalise(b + 2)

            m_stats(1)
            m_normalise(1)

            def m_block(b, b1, b2):
                for j in range(FT):
                    m_split(b, j)
                if b1:
                    m_xlo(b + 1)
                if b2:
                    m_stats(b + 2)
                m_outs(b, b2)

            with e.Fori(0, BLOCKS - 2) as b:
                m_block(b, True, True)
            m_block(BLOCKS - 2, True, False)
            m_block(BLOCKS - 1, False, False)

        @block.tensor
        def _(e):
            e.wait_ge(S.ident_ok, 1)
            e.wait_ge(S.z_wld, 16 * 16)
            for n in range(4):
                ins = e.transpose(ps_pr[0][:, P * n:P * n + P], z_w[:, n, :], ident[:])
            ins.then_inc(S.z_wt_mm, 1)
            e.wait_ge(S.z_wt_ev, 1)
            e.matmul(ps_pr[1][:, 0:P], z_w[:, 2, :], z_wt[:, 3, :], start=True, stop=True)
            e.matmul(ps_pr[1][:, P:P + 1], z_wt[:, 3, :], z_b[:, 2:3], start=True, stop=True).then_inc(S.z_wl_mm, 1)
            e.wait_ge(S.z_wl_ev, 1)
            e.wait_ge(S.z_bias, 1)

            def z_project(i, k, first):
                e.wait_ge(S.z_norm_x, i + 1)
                e.matmul(ps_pr[0][:, 0:256], z_wt[:, 0, :], z_xn[:], start=True, stop=True)
                e.matmul(ps_pr[0][:, 256:512], z_wt[:, 1, :], z_sn[:], start=True, stop=True).then_inc(S.z_s1, 1)
                if not first:
                    e.wait_ge(S.z_v_ev, i)
                for sc in range(2):
                    ins = e.matmul(ps_pr[1][:, P * sc:P * sc + P], z_s[:, k, P * sc:P * sc + P], z_wt[:, 2, :], start=True, stop=True)
                ins.then_inc(S.z_vmm, 1)

            def z_logits(i, first):
                e.wait_ge(S.z_m_ev, i + 1)
                for b in range(2):
                    if not first:
                        e.wait_ge(S.z_exp, i * 2 + (b - 1))
                    for tc in range(2):
                        ins = e.matmul(ps_l[:, b, 256 * tc:256 * tc + 256], z_mn[:, b, P * tc:P * tc + P], z_mm[:], start=True, stop=True)
                    ins.then_inc(S.z_l, 1)

            def z_transposes(i, par, first):
                for b in range(2):
                    e.wait_ge(S.z_normd, i * 2 + (b + 1))
                    if not first:
                        e.wait_ge(z_pt_ev[b], i)
                    dst = ps_t if b == 0 else ps_c
                    for sc in range(2):
                        for tc in range(2):
                            o = 256 * sc + P * tc
                            ins = e.transpose(dst[:, o:o + P], z_p[:, par, b, tc, P * sc:P * sc + P], ident[:])
                    ins.then_inc(S.z_t, 1)

            def z_values(i, k, first):
                for b in range(2):
                    e.wait_ge(z_pt_ev[b], i + 1)
                if not first:
                    e.wait_ge(S.z_outd, i)
                for b in range(2):
                    for sc in range(2):
                        ins = e.matmul(ps_o[0][64 * b:64 * b + 64, 0:256], z_v[:, k, sc, 64 * b:64 * b + 64], z_pt[:, b, sc, :],
                                       start=(sc == 0), stop=(sc == 1))
                ins.then_inc(S.z_pv, 1)

            plans = {last: block_plan(last) for last in (False, True)}
            first_plan = bank_plan(FIRST_X + PROLOGUE, 0, [])

            def three(dst, pairs, inc=None):
                terms = [t for (a_hi, a_lo), (b_hi, b_lo) in pairs for t in ((a_hi, b_hi), (a_hi, b_lo), (a_lo, b_hi))]
                for n, (a, b) in enumerate(terms):
                    ins = e.matmul(dst, a, b, start=(n == 0), stop=(n == len(terms) - 1))
                if inc is not None:
                    ins.then_inc(inc, 1)

            def cols(n, c, idx):
                o = HG * K * c + K * (idx % HG)
                return w_hi[n][:, idx // HG, o:o + K], w_lo[n][:, idx // HG, o:o + K]

            def project(use, plan, gb, layer=None):
                kind, idx, nxt = use
                bank, before = plan[use]
                n = gb + nxt
                if before is not None:
                    sem, count = evac_of(before, gb)
                    e.wait_ge(sem, count)
                dst = ps_pr[bank][:]
                group = idx // HG
                if kind in "QKV" and idx % HG == 0 and layer is not None and nxt == 0:
                    e.wait_ge(w_ok[kind.lower()], layer * GROUPS + (group + 1))
                if kind == "X":
                    src = x_st if idx < 2 else kv_st
                    if idx == 0:
                        e.wait_ge(S.xh_done, n + 1)
                    if idx == 2:
                        e.wait_ge(S.kv_ld, n * 16 + 16)
                    for c in range(DC):
                        for j in range(2):
                            o = 256 * c + P * j
                            ins = e.transpose(ps_pr[bank][:, o:o + P], src[:, 2 * (idx % 2) + j, P * c:P * c + P], ident[:])
                    ins.then_inc(S.x_mm, 1)
                    return
                if kind in "QK":
                    if idx == 0:
                        e.wait_ge(S.x_ev, n * 4 + (2 if kind == "Q" else 4))
                    w, sem = ("q", S.q_mm) if kind == "Q" else ("k", S.k_mm)
                    hi, lo = (h_hi, h_lo) if kind == "Q" else (c_hi, c_lo)
                    three(dst, [(cols(w, c, idx), (hi[:, c, :], lo[:, c, :])) for c in range(DC)], sem)
                else:
                    if idx == 0:
                        e.wait_ge(S.x_ev, n * 4 + 4)
                    t = slice(P * (idx % PAIRS), P * (idx % PAIRS) + P)
                    three(dst, [((c_hi[:, c, t], c_lo[:, c, t]), (w_hi["v"][:, group, HG * K * c:HG * K * c + HG * K], w_lo["v"][:, group, HG * K * c:HG * K * c + HG * K])) for c in range(DC)], S.v_mm)

            def transpose_rows(stage):
                e.wait_ge(S.rows_ld, stage * 16 + 16)
                e.transpose(ps_t[:, 0:5 * H], rows_sb[0:5 * H, :], ident[0:5 * H, 0:5 * H]).then_inc(S.rows_t, 1)

            def z_step(i, k, prev, prev_first, nxt):
                z_logits(i, not prev)
                if nxt:
                    z_project(i + 1, (k + 1) % ZUN, False)
                if prev:
                    z_transposes(i - 1, (k - 1) % 2, prev_first)
                    z_values(i - 1, (k - 1) % ZUN, prev_first)

            z_project(0, 0, True)
            for k in range(ZUN):
                z_step(k, k, k > 0, k == 1, True)
            with e.Fori(1, ZPAIRS // ZUN - 1) as g:
                for k in range(ZUN):
                    z_step(g * ZUN + k, k, True, False, True)
            for k in range(ZUN):
                z_step(ZPAIRS - ZUN + k, k, True, False, k < ZUN - 1)
            e.wait_ge(S.z_m_ev, ZPAIRS)
            e.wait_ge(S.z_v_ev, ZPAIRS)
            for u in FIRST_X[0:2]:
                project(u, first_plan, 0)
            z_transposes(ZPAIRS - 1, 1, False)
            z_values(ZPAIRS - 1, ZUN - 1, False)
            for u in FIRST_X[2:4]:
                project(u, first_plan, 0)
            e.wait_ge(S.z_outd, ZPAIRS)
            transpose_rows(0)

            def o_slot(gb, s, first, layer):
                hg, p = s // PAIRS % GROUPS, s % PAIRS
                B = gb * SLOTS
                if p == 0 and layer is not None:
                    e.wait_ge(S.wo_ok, layer * GROUPS + (hg + 1))
                e.wait_ge(S.cxlo_done, B + (s + 1))
                if s == 0 and not first:
                    e.wait_ge(S.xout_done, gb)
                dst = ps_o[p // 2][:, D * (p % 2):D * (p % 2) + D]
                for hh in range(HG):
                    col = slice(P * hh, P * hh + P)
                    for n, (a, b) in enumerate(((cx_hi, w_hi["o"]), (cx_hi, w_lo["o"]), (cx_lo, w_hi["o"]))):
                        ins = e.matmul(dst, a[:, col], b[:, hg, D * hh:D * hh + D], start=(hg == 0 and p % 2 == 0 and hh == 0 and n == 0),
                                       stop=False, skip_group_check=True)
                ins.then_inc(S.o_done, 1)

            def pe_slot(gb, s, first, plan, uses, layer=None, work=True):
                B = gb * SLOTS
                hg, p, par = s // PAIRS, s % PAIRS, s // PAIRS % 2
                if work:
                    if p == 0:
                        e.wait_ge(S.q_ev, B + (PAIRS * hg + HG))
                        e.wait_ge(S.k_ev, B + (PAIRS * hg + HG))
                        e.wait_ge(S.bias_col, gb * GROUPS + (hg + 1))
                    if not (first and s == 0):
                        e.wait_ge(S.sub_done, B + s)
                    for hh in range(HG):
                        o = 2 * KEYS * (hh % 2)
                        ins = e.matmul(ps_l[:, hh // 2, o:o + 2 * KEYS], q_sb[:, par, hh, P * p:P * p + P],
                                       k_sb[:, par, hh, 2 * p:2 * p + 2, :].rearrange("p a c -> p (a c)"), start=True, stop=True)
                    ins.then_inc(S.qk_done, 1)
                if not (first and s < 2):
                    o_slot(gb if s >= 2 else gb - 1, s - 2 if s >= 2 else s + 14, first, layer)
                if s == SLOTS + 1 or (s == 1 and not first):
                    for pp in range(PAIRS):
                        ins = e.matmul(ps_o[pp // 2][:, D * (pp % 2):D * (pp % 2) + D], pbt_sb[:, P * pp:P * pp + P], bw_sb[:],
                                       start=False, stop=True, skip_group_check=True)
                    ins.then_inc(S.fin_done, 1)
                for u in uses[0]:
                    project(u, plan, gb, layer)
                if not (first and s == 0) and s <= SLOTS:
                    e.wait_ge(S.norm_done, B + s)
                    if not (first and s == 1):
                        e.wait_ge(S.pt_ev, B + (s - 1))
                    for hh in range(HG):
                        ins = e.transpose(ps_t[:, P * hh:P * hh + P], p_sb[:, hh, :], ident[:])
                    ins.then_inc(S.t_done, 1)
                    if s % SLOTS == 0:
                        for pp in range(PAIRS):
                            ins = e.transpose(ps_c[0:H + 2, P * pp:P * pp + P], pb_sb[:, pp, :], ident[:])
                        ins.then_inc(S.pbt_done, 1)
                for u in uses[1]:
                    project(u, plan, gb, layer)
                if first and s == 0:
                    e.wait_ge(S.lmat_ok, layer + 1)
                    e.wait_ge(S.wo_ld, layer * 16 + 16)
                    for k in range(2):
                        e.wait_ge(z_so[k], 16 * ZPAIRS // 2)
                    for h in range(H):
                        ins = e.matmul(ps_c[0:H + 1, 0:D], lmat[:, h, :], w_raw["o"][:, h // HG, D * (h % HG):D * (h % HG) + D],
                                       start=(h == 0), stop=(h == H - 1))
                    ins.then_inc(S.bw_mm, 1)
                if first and s == 1:
                    e.wait_ge(S.bw_ok, layer + 1)
                    e.wait_ge(S.bo_ld, layer * 16 + 16)
                if not (first and s == 0) and s <= SLOTS:
                    e.wait_ge(S.pt_ev, B + s)
                    e.wait_ge(S.v_ev, B + s)
                    if s % SLOTS == 0:
                        e.wait_ge(S.pbt_ev, gb + s // SLOTS)
                    pp = (s - 1) % PAIRS
                    for hh in range(HG):
                        col = slice(P * hh, P * hh + P)
                        ins = e.matmul(ps_c[:, col], v_sb[:, pp, K * hh:K * hh + K], pt_sb[:, col], start=True, stop=True)
                    ins.then_inc(S.pv_done, 1)
                for u in uses[2]:
                    project(u, plan, gb, layer)

            def pe_block(gb, first, last, layer=None):
                for s in range(SLOTS):
                    pe_slot(gb, s, first, plans[last], projections(s, last), layer)

            with e.Fori(0, LAYERS) as layer:
                g0 = layer * BLOCKS
                for u in PROLOGUE:
                    project(u, first_plan, g0, layer)
                pe_block(g0, True, False, layer)
                with e.Fori(1, BLOCKS - 1) as b:
                    pe_block(b + g0, False, False)
                gl = g0 + (BLOCKS - 1)
                pe_block(gl, False, True)
                pe_slot(gl, SLOTS, False, None, [[], [], []], work=False)
                e.wait_ge(S.pt_ev, gl * SLOTS + SLOTS)
                transpose_rows(layer + 1)
                pe_slot(gl, SLOTS + 1, False, None, [[], [], []], work=False)

            def m_fc1(b, j, first):
                if j < 2:
                    if first:
                        e.wait_ge(S.x_ev, LAYERS * BLOCKS * 4 + 4)
                    else:
                        e.wait_ge(S.m_xlo, b * 2)
                else:
                    e.wait_ge(S.m_gelu, b * FT + (j - 1))
                three(ps_pr[j % 2][:], [(cols("q", c, j), (h_hi[:, c, :], h_lo[:, c, :])) for c in range(DC)], S.m_fc1)

            def m_transposes(b, i):
                if i == 0:
                    e.wait_ge(S.m_xh, b)
                e.wait_ge(S.m_gelu, b * FT + (i - 1))
                for c in range(DC):
                    for j in range(2):
                        o = 256 * c + P * j
                        ins = e.transpose(ps_pr[i][:, o:o + P], kv_st[:, 2 * i + j, P * c:P * c + P], ident[:])
                ins.then_inc(S.m_x, 1)

            def m_fc2(b, p, tiles):
                t = slice(P * p, P * p + P)
                for j in tiles:
                    w2 = [w["q"][:, 2 + j // HG, D * (j % HG):D * (j % HG) + D] for w in (w_hi, w_lo)]
                    for n, (g, w) in enumerate(((g_hi, w2[0]), (g_hi, w2[1]), (g_lo, w2[0]))):
                        ins = e.matmul(ps_o[p // 2][:, D * (p % 2):D * (p % 2) + D], g[:, j, t], w,
                                       start=(j == 0 and n == 0), stop=(j == FT - 1 and n == 2))
                if p % 2 and tiles[-1] == FT - 1:
                    ins.then_inc(S.m_fc2, 1)

            def m_block(b, first, last):
                for j in range(FT):
                    m_fc1(b, j, first)
                if not last:
                    m_transposes(b + 1, 0)
                if first:
                    e.wait_ge(S.xout_done, LAYERS * BLOCKS)
                else:
                    e.wait_ge(S.m_out, b * 2)
                e.wait_ge(S.m_glo, b * FT + (FT - 1))
                m_fc2(b, 0, range(FT - 1))
                if not last:
                    m_transposes(b + 1, 1)
                e.wait_ge(S.m_glo, b * FT + FT)
                m_fc2(b, 0, range(FT - 1, FT))
                for p in range(1, PAIRS):
                    m_fc2(b, p, range(FT))

            e.wait_ge(S.wq_ok, (LAYERS + 1) * GROUPS)
            m_block(0, True, False)
            with e.Fori(1, BLOCKS - 1) as b:
                m_block(b, False, False)
            m_block(BLOCKS - 1, False, True)


def kernel(**inputs):
    import numpy as np
    import concourse.bacc as bacc
    from concourse.bass_utils import run_bass_kernel_spmd

    a = {k: np.asarray(v) for k, v in inputs.items()}
    z = lambda n: a["L0_xattn_" + n]
    w = lambda n: a["L1_xattn_" + n]
    heads = lambda n: w(n).reshape(H, K)
    grouped = lambda m: m.reshape(DC, P, -1, HG * K).transpose(1, 2, 0, 3).reshape(P, -1)
    by_rows = lambda m: m.reshape(-1, P, D).transpose(1, 0, 2).reshape(P, -1)
    arrays = {
        "x": a["x"].reshape(BATCH * Q, D),
        "ctx": a["ctx_2048"].reshape(BATCH * Q, D),
        "zw": np.stack([z("Wn"), z("Wm"), z("Wl"), z("Wo")]),
        "zb": np.stack([z("bn"), z("bm"), z("bl"), z("bo")]),
        "weights": np.stack([part for i in (1, 2) for part in (grouped(w(f"wq{i}")), grouped(w(f"wk{i}")), grouped(w(f"wv{i}")),
                                                               by_rows(w(f"wo{i}")))]
                            + [np.concatenate([grouped(w("w_fc1")), by_rows(w("w_fc2"))], axis=1)]),
        "rows": np.stack([np.concatenate([heads(f"{n}{i}") for n in ("bq", "bk", "bias_k", "bias_v", "bv")]) for i in (1, 2)]
                         + [np.concatenate([w("b_fc1").reshape(FT, P), np.zeros((5 * H - FT, P), np.float32)])]),
        "ln": np.stack([np.stack([w(f"{n}_scale"), w(f"{n}_offset")]) for n in ("ln1", "ln2", "ln_mlp")]),
        "bo": np.stack([w("bo1"), w("bo2")]),
        "b2": w("b_fc2"),
    }
    arrays = {k: np.ascontiguousarray(v) for k, v in arrays.items()}
    nc = bacc.Bacc("TRN2", target_bir_lowering=False, num_devices=1)
    args = {k: nc.dram_tensor(k, v.shape, mybir.dt.from_np(v.dtype), kind="ExternalInput").ap() for k, v in arrays.items()}
    out = nc.dram_tensor("out", (BATCH * Q, D), F32, kind="ExternalOutput").ap()
    build(nc, out=out, **args)
    r = run_bass_kernel_spmd(nc, [arrays], core_ids=[0])
    return r.results[0]["out"].reshape(BATCH, Q, D)
```

```python
import concourse.bass as bass
from concourse import mybir

F32 = mybir.dt.float32
F32R = mybir.dt.float32r
ACT = mybir.ActivationFunctionType
ALU = mybir.AluOpType
AX = mybir.AxisListType

P = 128
BATCH, Q, D = 64, 64, 256
H, K, F = 16, 128, 1024
LAYERS = 2
TOK = 512
BLOCKS = BATCH * Q // TOK
PAIRS = TOK // P
DC = D // P
HG = 4
GROUPS = H // HG
SLOTS = GROUPS * PAIRS
KEYS = Q + 1
FT = F // P
EPS = 1e-5
SCALE = float(K) ** -0.5
ZPAIRS = BATCH // 2
ZX, ZS = 8, 4
ZAHEAD = 6



def projections(slot, last):
    if slot < 12:
        uses = ([("Q", slot + 4, 0)], [("K", slot + 4, 0)], [("V", slot + 3, 0)] + ([("X", 0, 1)] if slot == 11 else []))
    elif slot == 12:
        uses = ([("X", 1, 1)], [("V", 15, 0)], [("X", 2, 1)])
    elif slot == 13:
        uses = ([("Q", 0, 1)], [("X", 3, 1), ("Q", 1, 1)], [("K", 0, 1), ("V", 0, 1)])
    elif slot == 14:
        uses = ([("K", 1, 1)], [("Q", 2, 1), ("K", 2, 1)], [("V", 1, 1)])
    else:
        uses = ([("Q", 3, 1)], [("K", 3, 1)], [("V", 2, 1)])
    if last and slot >= 11:
        uses = {11: ([("Q", 15, 0)], [("K", 15, 0)], [("X", 0, 1)]),
                12: ([("X", 1, 1)], [("V", 14, 0)], []),
                13: ([], [("V", 15, 0)], [("X", 2, 1)]),
                14: ([], [("X", 3, 1)], [])}.get(slot, ([], [], []))
    return uses


FIRST_X = [("X", n, 0) for n in range(4)]
EARLY = {SLOTS: ("Q", 0, 1), SLOTS + 1: ("Q", 1, 1)}
PROLOGUE = [("Q", 2, 0), ("Q", 3, 0), ("K", 0, 0), ("V", 0, 0), ("K", 1, 0), ("K", 2, 0),
            ("V", 1, 0), ("K", 3, 0), ("V", 2, 0)]

TOP_SPLITS = [("k", 0), ("v", 0)]
PROLOGUE_SPLITS = {("V", 0, 0): ("k", 1), ("V", 1, 0): ("v", 1), ("V", 2, 0): ("k", 2)}
SLOT_SPLITS = {0: [("o", 0)], 1: [("v", 2)], 2: [("o", 1)], 3: [("k", 3)], 5: [("v", 3)], 6: [("o", 2)], 7: [("o", 3)]}
Q_SPLIT_SLOT = 13
SPARSE = 13


def bank_plan(uses, first_bank, before):
    seq = list(before)
    plan = {}
    for n, use in enumerate(uses):
        plan[use] = ((first_bank + n) % 2, seq[-2] if len(seq) > 1 else None)
        seq.append(use)
    return plan


def block_plan(last):
    uses = [u for s in range(SLOTS) for part in projections(s, last) for u in part]
    return bank_plan(uses + (list(EARLY.values()) if last else []), len(PROLOGUE) % 2, PROLOGUE[-2:])


def first_block_plan():
    return bank_plan(FIRST_X + [("Q", 0, 0), ("Q", 1, 0)] + PROLOGUE, 0, [])


def split_now(slot, first, last):
    if first:
        return SLOT_SPLITS.get(slot, [])
    return [("q", slot - Q_SPLIT_SLOT)] if last and slot >= Q_SPLIT_SLOT else []


def ge(engine, sem, value):
    if isinstance(value, int) and value <= 0:
        return
    engine.wait_ge(sem, value)


def ge_apart(engine, sem, value, apart):
    engine.wait_ge(sem, value)
    engine.sem_inc(apart, 1)


class Space:

    def __init__(self, nc, at):
        self.nc, self.at = nc, at

    def put(self, name, shape, dtype=F32, at=None):
        size = 4
        for n in shape[1:]:
            size *= n
        if at is None:
            at = self.at
            self.at += (size + 31) // 32 * 32
        t = self.nc.alloc_sbuf_tensor_at(name, shape, dtype, offset=at)
        t_at = at
        return t, t_at


def build(nc, x, ctx, zw, zb, weights, rows, ln, bo, b2, out):
    base = (nc.sbuf_base + 31) // 32 * 32
    sp = Space(nc, base)
    w_hi, w_lo, w_raw, w_at = {}, {}, {}, {}
    PIECE = DC * HG * K
    for n in "qkvo":
        w_hi[n], w_at[n] = sp.put("w_hi_" + n, [P, GROUPS, PIECE], F32R)
        w_lo[n], lo_at = sp.put("w_lo_" + n, [P, GROUPS, PIECE], F32R)
        w_raw[n], _ = sp.put("w_raw_" + n, [P, GROUPS, PIECE], F32, lo_at)
    q_sb, shared_at = sp.put("q_sb", [P, 2, HG, TOK])
    k_sb, _ = sp.put("k_sb", [P, 2, HG, 2 * PAIRS, KEYS])
    v_sb, v_at = sp.put("v_sb", [P, PAIRS, HG * K])
    rows_sb, _ = sp.put("rows_sb", [P, K], F32, v_at + 2 * HG * K * 4)
    h_hi, _ = sp.put("h_hi", [P, DC, TOK], F32R)
    h_lo, _ = sp.put("h_lo", [P, DC, TOK], F32R)
    c_hi, _ = sp.put("c_hi", [P, DC, TOK], F32R)
    c_lo, shared_end = sp.put("c_lo", [P, DC, TOK], F32R)
    shared_end += DC * TOK * 4
    x_st, _ = sp.put("x_st", [P, PAIRS, D])
    kv_st, _ = sp.put("kv_st", [P, PAIRS, D])
    ln_bc, _ = sp.put("ln_bc", [P, 2, D])
    s_sb, _ = sp.put("s_sb", [P, HG, KEYS])
    p_sb, _ = sp.put("p_sb", [P, HG, P])
    pt_sb, pt_at = sp.put("pt_sb", [P, HG * P])
    lmat, _ = sp.put("lmat", [P, H, H + 1], F32, pt_at)
    cx_hi, cx_at = sp.put("cx_hi", [P, HG * P], F32R)
    bo_row, _ = sp.put("bo_row", [1, D], F32, cx_at)
    cx_lo, _ = sp.put("cx_lo", [P, HG * P], F32R)
    ident, _ = sp.put("ident", [P, P])
    pbt_sb, _ = sp.put("pbt_sb", [P, TOK], F32R)
    bw_sb, _ = sp.put("bw_sb", [P, D], F32R)
    pb_sb, _ = sp.put("pb_sb", [P, PAIRS, H + 1])
    onehot, _ = sp.put("onehot", [1, H + 1])
    prm, _ = sp.put("prm", [P, 5 * H])
    small, _ = sp.put("small", [P, 3, HG])
    mx, sm, rc = small[:, 0, :], small[:, 1, :], small[:, 2, :]
    st6, _ = sp.put("st6", [P, PAIRS, 6])
    mv, _ = sp.put("mv", [P, PAIRS, 2])
    rstd, _ = sp.put("rstd", [P, PAIRS])
    mhalf, _ = sp.put("mhalf", [P, PAIRS])
    assert sp.at <= nc.sbuf_usable_end, (sp.at, nc.sbuf_usable_end)
    bq_c, bk_c, bkey_c = prm[:, 0:H], prm[:, H:2 * H], prm[:, 2 * H:3 * H]

    zs = Space(nc, shared_at)
    z_x, _ = zs.put("z_x", [P, ZX, D])
    z_s, _ = zs.put("z_s", [P, ZS, D])
    z_o, _ = zs.put("z_o", [P, 2, D], F32, w_at["o"] + 3 * PIECE * 4)
    z_v, _ = zs.put("z_v", [P, 2, 2, P])
    z_xn, _ = zs.put("z_xn", [P, D])
    z_sn, _ = zs.put("z_sn", [P, D])
    z_mn, _ = zs.put("z_mn", [P, 2, D])
    z_mm, _ = zs.put("z_mm", [P, D])
    z_p, _ = zs.put("z_p", [P, 2, 2, 2, D])
    z_pt, _ = zs.put("z_pt", [P, 2, 2, D])
    z_w, _ = zs.put("z_w", [P, 4, P])
    z_wt, _ = zs.put("z_wt", [P, 4, P])
    z_b, _ = zs.put("z_b", [P, 4])
    z_c, _ = zs.put("z_c", [P, 1])
    z_st6, _ = zs.put("z_st6", [P, 2, 6])
    z_mv, _ = zs.put("z_mv", [P, 2, 2, 2])
    z_rs, _ = zs.put("z_rs", [P, 2, 2])
    z_nmx, _ = zs.put("z_nmx", [P, 2, 2])
    z_sum, _ = zs.put("z_sum", [P, 2, 2])
    z_rc, _ = zs.put("z_rc", [P, 2, 2])
    assert zs.at <= v_at + 2 * HG * K * 4

    g_hi, _ = sp.put("g_hi", [P, FT, TOK], F32R, w_at["k"])
    g_lo, _ = sp.put("g_lo", [P, FT, TOK], F32R, w_at["k"] + 16384)
    g_raw, _ = sp.put("g_raw", [P, 4, TOK], F32, w_at["v"])
    b2_bc, _ = sp.put("b2_bc", [P, D], F32, w_at["v"] + 8192)

    ps_pr = [nc.alloc_psum_tensor(f"ps_pr{i}", [P, 512], F32) for i in range(2)]
    ps_l = nc.alloc_psum_tensor("ps_l", [P, 2, 512], F32)
    ps_t = nc.alloc_psum_tensor("ps_t", [P, 512], F32)
    ps_c = nc.alloc_psum_tensor("ps_c", [P, 512], F32)
    ps_o = [nc.alloc_psum_tensor(f"ps_o{i}", [P, 512], F32) for i in range(2)]

    scr = nc.dram_tensor("x_scratch", (3 * BLOCKS, TOK, D), F32, kind="Internal").ap()

    names = """apart_dve apart_pool ident_ok consts_ok
    z_wld z_bld z_wt_mm z_wt_ev z_wl_mm z_wl_ev z_bias z_zero z_ld0 z_ld1 z_ld2 z_ld3 z_so0 z_so1
    z_st z_mvd z_eps z_rsd z_norm_x z_norm_s z_s1 z_vmm z_m_ev z_v_ev z_l z_nmx_ok z_exp z_rec z_normd z_t z_pt_ev0 z_pt_ev1 z_pv z_outd
    wq_ld wk_ld wv_ld wo_ld wq_hi wk_hi wv_hi wo_hi wq_ok wk_ok wv_ok wo_ok rows_ld rows_t prm_ok l_zero lmat_ok bo_ld bw_mm bw_ok lnb_ld
    x_ld kv_ld res_ld x_st_ok st_done mv_done eps_done rs_done xn_done aff_done xh_done
    q_mm k_mm v_mm x_mm q_ev k_ev v_ev x_hi_ev x_ev bias_col qk_done max_done sub_done exp_done sum_done rec_done norm_done
    t_done pt_ev pv_done cxhi_done cxlo_done o_done pbt_done pbt_hi pbt_ev pbt_copied bw_hi fin_done xout_done
    m_bld m_xld m_rld m_sto m_st m_mv m_eps m_rs m_xn m_aff m_xh m_x m_xhi m_xlo
    m_fc1 m_gelu m_ghi m_glo m_fc2 m_res m_out""".split()
    S = type("Semaphores", (), {n: nc.alloc_semaphore(n) for n in names})
    z_ld = [S.z_ld0, S.z_ld1, S.z_ld2, S.z_ld3]
    z_so = [S.z_so0, S.z_so1]
    z_pt_ev = [S.z_pt_ev0, S.z_pt_ev1]
    w_ld = {"q": S.wq_ld, "k": S.wk_ld, "v": S.wv_ld, "o": S.wo_ld}
    w_hi_ok = {"q": S.wq_hi, "k": S.wk_hi, "v": S.wv_hi, "o": S.wo_hi}
    w_ok = {"q": S.wq_ok, "k": S.wk_ok, "v": S.wv_ok, "o": S.wo_ok}

    tok = lambda a: a.rearrange("(j p) d -> p j d", p=P)
    xp = x.rearrange("(i p) d -> i p d", p=P)
    cp = ctx.rearrange("(i p) d -> i p d", p=P)
    cb = ctx.rearrange("(b t) d -> b t d", t=TOK)
    ob = out.rearrange("(b t) d -> b t d", t=TOK)
    sp_pairs = scr.rearrange("b (j p) d -> (b j) p d", p=P)

    def evac_of(use, gb):
        kind, idx, nxt = use
        sem = {"Q": S.q_ev, "K": S.k_ev, "V": S.v_ev, "X": S.x_ev}[kind]
        return sem, (gb + nxt) * (4 if kind == "X" else SLOTS) + idx + 1

    with nc.Block() as block:

        @block.sync
        def _(e):
            def load_piece(n, group, stage):
                src = weights[4 * stage + "qkvo".index(n)].rearrange("p (g c) -> p g c", g=GROUPS)
                e.dma_start(w_raw[n][:, group, :], src[:, group, :]).then_inc(w_ld[n], 16)

            def load_w(n, stage):
                for group in range(GROUPS):
                    load_piece(n, group, stage)

            def load_rows(stage):
                e.dma_start(rows_sb[0:5 * H, :], rows[stage]).then_inc(S.rows_ld, 16)

            def load_ln(stage):
                e.dma_start(ln_bc[:], ln[stage].partition_broadcast(P)).then_inc(S.lnb_ld, 16)

            def load_bo(layer):
                e.dma_start(bo_row[:], bo[layer:layer + 1, :]).then_inc(S.bo_ld, 16)

            def z_load(i, r):
                e.dma_start(z_x[:, r % ZX, :], xp[i]).then_inc(z_ld[r % ZS], 16)
                e.dma_start(z_s[:, r % ZS, :], cp[i]).then_inc(z_ld[r % ZS], 16)

            def z_store(i, r):
                e.wait_ge(S.z_outd, i + 1)
                e.dma_start(sp_pairs[i], z_o[:, r % 2, :]).then_inc(z_so[r % 2], 16)

            z_load(0, 0)
            halves = [slice(64 * half, 64 * half + 64) for half in range(2)]
            for r in halves:
                e.dma_start(z_w[r, :, r], zw.rearrange("n p c -> p n c")).then_inc(S.z_wld, 16)
            for r in halves:
                e.dma_start(z_b[r, :], zb).then_inc(S.z_bld, 16)
            for k in range(1, ZS):
                z_load(k, k)
            load_ln(0)
            load_rows(0)
            load_bo(0)

            for i in range(ZS, ZAHEAD):
                e.wait_ge(S.z_vmm, i - ZS + 1)
                z_load(i, i)
            for i in range(ZX):
                z_store(i, i)
                z_load(i + ZAHEAD, i + ZAHEAD)
                for n in range(2):
                    load_piece("qkvo"[i // 2], 2 * (i % 2) + n, 0)
            with e.Fori(1, ZPAIRS // ZX - 1) as g:
                for r in range(ZX):
                    z_store(g * ZX + r, r)
                    z_load(g * ZX + (r + ZAHEAD), r + ZAHEAD)
            for k in range(2):
                e.wait_ge(z_so[k], 16 * PAIRS // 2)
            e.dma_start(x_st[:], tok(scr[0])).then_inc(S.x_ld, 16)
            e.dma_start(kv_st[:], tok(cb[0])).then_inc(S.kv_ld, 16)
            for i in range(ZPAIRS - ZX, ZPAIRS):
                z_store(i, i)
                if i + ZAHEAD < ZPAIRS:
                    z_load(i + ZAHEAD, i + ZAHEAD)

            for k in range(2):
                e.wait_ge(z_so[k], 16 * ZPAIRS // 2)

            def store_out(gb):
                e.wait_ge(S.xout_done, gb + 1)
                e.dma_start(tok(scr[gb + BLOCKS]), x_st[:]).then_inc(S.x_st_ok, 16)

            def sp_block(gb, very_first, next_context):
                if very_first:
                    e.wait_ge(S.x_mm, 2)
                else:
                    store_out(gb - 1)
                    e.wait_ge(S.x_st_ok, gb * 16)
                e.dma_start(x_st[:], tok(scr[gb + 1])).then_inc(S.x_ld, 16)
                e.wait_ge(S.x_mm, gb * 4 + 4)
                e.dma_start(kv_st[:], tok(cb[next_context])).then_inc(S.kv_ld, 16)
                e.wait_ge(S.x_mm, gb * 4 + 6)
                e.dma_start(x_st[:], tok(scr[gb])).then_inc(S.res_ld, 16)

            for layer in range(LAYERS):
                g0 = layer * BLOCKS
                gl = g0 + BLOCKS - 1
                sp_block(g0, layer == 0, 1)
                with e.Fori(1, BLOCKS - 1) as b:
                    sp_block(b + g0, False, b + 1)
                e.wait_ge(S.xh_done, gl + 1)
                load_ln(layer + 1)
                sp_block(gl, False, 0)
                e.wait_ge(S.q_mm, (gl + 1) * SLOTS)
                load_w("q", layer + 1)
                if layer + 1 < LAYERS:
                    e.wait_ge(S.k_mm, (gl + 1) * SLOTS)
                    load_w("k", layer + 1)
                e.wait_ge(S.v_mm, (gl + 1) * SLOTS)
                if layer + 1 < LAYERS:
                    load_w("v", layer + 1)
                else:
                    e.dma_start(b2_bc[:], b2.partition_broadcast(P)).then_inc(S.m_bld, 16)
                e.wait_ge(S.pv_done, gl * SLOTS + (SLOTS - 1))
                load_rows(layer + 1)
                if layer + 1 < LAYERS:
                    e.wait_ge(S.o_done, (gl + 1) * SLOTS)
                    load_w("o", layer + 1)
                    load_bo(layer + 1)

            m0 = LAYERS * BLOCKS

            def m_load(b):
                e.dma_start(kv_st[:], tok(scr[b + m0])).then_inc(S.m_xld, 16)

            e.wait_ge(S.x_mm, m0 * 4 + 4)
            m_load(1)
            store_out(m0 - 1)
            e.wait_ge(S.x_st_ok, m0 * 16)
            e.dma_start(x_st[:], tok(scr[m0])).then_inc(S.m_rld, 16)

            def m_store(b):
                e.wait_ge(S.m_out, b * 2 + 2)
                e.dma_start(tok(ob[b]), x_st[:]).then_inc(S.m_sto, 16)
                e.wait_ge(S.m_sto, b * 16 + 16)

            def m_residual(b):
                m_store(b - 1)
                e.dma_start(x_st[:], tok(scr[b + m0])).then_inc(S.m_rld, 16)

            with e.Fori(1, BLOCKS - 1) as b:
                e.wait_ge(S.m_x, b * 2)
                m_load(b + 1)
                m_residual(b)
            m_residual(BLOCKS - 1)
            for i in range(2):
                e.wait_ge(S.m_out, BLOCKS * 2 - 1 + i)
                e.dma_start(tok(ob[BLOCKS - 1])[:, 2 * i:2 * i + 2, :], x_st[:, 2 * i:2 * i + 2, :]).then_inc(S.m_sto, 16)
            e.wait_ge(S.m_sto, BLOCKS * 16 + 16)

        @block.gpsimd
        def _(e):
            e.memset(ident[:], 0.0).then_inc(S.consts_ok, 1)
            e.memset(p_sb[:], 0.0).then_inc(S.consts_ok, 1)
            e.memset(pbt_sb[:].bitcast(F32), 0.0).then_inc(S.consts_ok, 1)
            e.memset(bw_sb[:].bitcast(F32), 0.0).then_inc(S.consts_ok, 1)
            e.memset(onehot[:], 0.0).then_inc(S.consts_ok, 1)
            e.memset(pb_sb[:], 1.0).then_inc(S.consts_ok, 1)
            e.memset(mhalf[:], -0.5).then_inc(S.consts_ok, 1)
            e.memset(z_mn[:], 0.0).then_inc(S.consts_ok, 1)
            e.wait_ge(S.consts_ok, 8)
            e.memset(onehot[:, H:H + 1], 1.0).then_inc(S.consts_ok, 1)
            e.affine_select(out=ident[:], in_=ident[:], compare_op=ALU.not_equal, fill=1.0, base=0,
                            pattern=[[-1, P]], channel_multiplier=1).then_inc(S.ident_ok, 1)

            def z_normalise(i, r):
                k, par = r % ZS, r % 2
                ge_apart(e, S.z_mvd, i + 1, S.apart_pool)
                e.tensor_scalar(z_rs[:, par, :], z_mv[:, par, :, 1], EPS, None, ALU.add).then_inc(S.z_eps, 1)
                e.wait_ge(S.z_eps, i + 1)
                e.tensor_tensor(z_rs[:, par, :], z_rs[:, par, :], mhalf[:, 0:2], ALU.pow).then_inc(S.z_rsd, 1)
                ge_apart(e, S.z_rsd, i + 1, S.apart_pool)
                if not (isinstance(i, int) and i == 0):
                    ge_apart(e, S.z_s1, i, S.apart_pool)
                e.tensor_scalar(z_sn[:], z_s[:, k, :], z_mv[:, par, 1, 0:1], z_rs[:, par, 1:2], ALU.subtract, ALU.mult).then_inc(S.z_norm_s, 1)

            def rstd_of(n):
                ge_apart(e, S.mv_done, n, S.apart_pool)
                e.tensor_scalar(rstd[:], mv[:, :, 1], EPS, None, ALU.add).then_inc(S.eps_done, 1)
                e.wait_ge(S.eps_done, n)
                e.tensor_tensor(rstd[:], rstd[:], mhalf[:], ALU.pow).then_inc(S.rs_done, 1)

            def affine(n):
                e.wait_ge(S.xn_done, n)
                e.tensor_tensor(x_st[:], x_st[:], ln_bc[:, 0:1, :].to_broadcast([P, PAIRS, D]), ALU.mult).then_inc(S.aff_done, 1)
                e.wait_ge(S.aff_done, n)
                e.tensor_tensor(x_st[:], x_st[:], ln_bc[:, 1:2, :].to_broadcast([P, PAIRS, D]), ALU.add).then_inc(S.xh_done, 1)

            def bias_columns(hg):
                par = hg % 2
                e.tensor_copy(k_sb[:, par, :, :, Q], bkey_c[:, HG * hg:HG * hg + HG].unsqueeze(2)
                              .to_broadcast([P, HG, 2 * PAIRS])).then_inc(S.bias_col, 1)

            def split_low(n, group, stage):
                e.wait_ge(w_hi_ok[n], stage * GROUPS + (group + 1))
                if group:
                    e.wait_ge(w_ok[n], stage * GROUPS + group)
                if n == "o" and group == 0:
                    e.wait_ge(S.bw_mm, stage + 1)
                e.tensor_tensor(w_lo[n][:, group, :], w_raw[n][:, group, :], w_hi[n][:, group, :].bitcast(F32), ALU.subtract).then_inc(w_ok[n], 1)

            def pool_block(gb, first, last, layer):
                def splits(slots):
                    for s in slots:
                        for n, group in split_now(s, first, last):
                            split_low(n, group, layer + 1 if last else layer)

                for hg in (1, 2):
                    if not (first and hg == 1):
                        ge_apart(e, S.qk_done, gb * SLOTS + PAIRS * (hg - 1), S.apart_pool)
                    bias_columns(hg)
                    splits(range(0, 5) if hg == 1 else range(5, 8))
                rstd_of(gb + 2)
                ge_apart(e, S.qk_done, gb * SLOTS + PAIRS * 2, S.apart_pool)
                bias_columns(3)
                if last:
                    e.wait_ge(S.lnb_ld, layer * 16 + 32)
                affine(gb + 2)
                if not last:
                    ge_apart(e, S.qk_done, gb * SLOTS + PAIRS * 3, S.apart_pool)
                    bias_columns(0)
                splits(range(8, SLOTS + 1))

            for i in range(2):
                z_normalise(i, i)
            with e.Fori(0, ZPAIRS // ZS - 1) as g:
                for r in range(2, 2 + ZS):
                    z_normalise(g * ZS + r, r)
            rstd_of(1)
            for i in range(ZPAIRS - 2, ZPAIRS):
                z_normalise(i, i)
            e.wait_ge(S.lnb_ld, 16)
            affine(1)
            for group in range(GROUPS):
                split_low("q", group, 0)

            with e.Fori(0, LAYERS) as layer:
                g0 = layer * BLOCKS
                ge_apart(e, S.prm_ok, layer + 1, S.apart_pool)
                bias_columns(0)
                pool_block(g0, True, False, layer)
                with e.Fori(1, BLOCKS - 1) as b:
                    pool_block(b + g0, False, False, layer)
                pool_block(g0 + (BLOCKS - 1), False, True, layer)

            def m_norm(n):
                ge_apart(e, S.m_mv, n, S.apart_pool)
                e.tensor_scalar(rstd[:], mv[:, :, 1], EPS, None, ALU.add).then_inc(S.m_eps, 1)
                e.wait_ge(S.m_eps, n)
                e.tensor_tensor(rstd[:], rstd[:], mhalf[:], ALU.pow).then_inc(S.m_rs, 1)
                e.wait_ge(S.m_xn, n)
                e.tensor_tensor(kv_st[:], kv_st[:], ln_bc[:, 0:1, :].to_broadcast([P, PAIRS, D]), ALU.mult).then_inc(S.m_aff, 1)
                e.wait_ge(S.m_aff, n)
                e.tensor_tensor(kv_st[:], kv_st[:], ln_bc[:, 1:2, :].to_broadcast([P, PAIRS, D]), ALU.add).then_inc(S.m_xh, 1)

            def m_residual(n):
                e.wait_ge(S.m_rld, n * 16)
                e.tensor_tensor(x_st[:], x_st[:], b2_bc[:].unsqueeze(1).to_broadcast([P, PAIRS, D]), ALU.add).then_inc(S.m_res, 1)

            e.wait_ge(S.m_bld, 16)
            with e.Fori(0, BLOCKS - 1) as b:
                m_norm(b + 1)
                m_residual(b + 1)
            m_residual(BLOCKS)

        @block.scalar
        def _(e):
            def z_exp(i, par, b):
                e.wait_ge(S.z_nmx_ok, i * 2 + (b + 1))
                for tc in range(2):
                    ins = e.activation(z_p[:, par, b, tc, :], ps_l[:, b, 256 * tc:256 * tc + 256], ACT.Exp,
                                       bias=z_nmx[:, b, tc:tc + 1], accum_out=z_sum[:, b, tc:tc + 1])
                ins.then_inc(S.z_exp, 1)

            def z_ptev(i):
                e.wait_ge(S.z_t, i * 2 + 2)
                e.activation(z_pt[:, 1].rearrange("p a t -> p (a t)"), ps_c[:], ACT.Copy).then_inc(S.z_pt_ev1, 1)

            def z_evac_m(i):
                e.wait_ge(S.z_s1, i + 1)
                for b in range(2):
                    r = slice(64 * b, 64 * b + 64)
                    e.activation(z_mn[r, b, :], ps_pr[0][r, 0:256], ACT.Identity, bias=z_b[r, 0:1])
                e.activation(z_mm[:], ps_pr[0][:, 256:512], ACT.Identity, bias=z_b[:, 1:2]).then_inc(S.z_m_ev, 1)

            def z_evac_v(i, k, first=False):
                e.wait_ge(S.z_vmm, i + 1)
                if not first:
                    e.wait_ge(S.z_pv, i - 1)
                e.activation(z_v[:, k].rearrange("p a b -> p (a b)"), ps_pr[1][:, 0:256], ACT.Copy).then_inc(S.z_v_ev, 1)

            e.wait_ge(S.z_wt_mm, 1)
            e.activation(z_wt[:].rearrange("p a b -> p (a b)"), ps_pr[0][:], ACT.Copy).then_inc(S.z_wt_ev, 1)
            e.wait_ge(S.z_wl_mm, 1)
            e.activation(z_wt[:, 2, :], ps_pr[1][:, 0:128], ACT.Copy).then_inc(S.z_wl_ev, 1)
            e.activation(z_c[:], ps_pr[1][:, 128:129], ACT.Identity, bias=z_b[:, 3:4]).then_inc(S.z_bias, 1)
            e.wait_ge(S.consts_ok, 9)
            z_evac_m(0)
            z_evac_v(0, 0, True)
            plans = {last: block_plan(last) for last in (False, True)}
            first_plan = first_block_plan()

            def split_high(n, group, stage):
                if group == 0:
                    e.wait_ge(w_ld[n], (stage + 1) * 16 * GROUPS)
                e.activation(w_hi[n][:, group, :], w_raw[n][:, group, :], ACT.Copy).then_inc(w_hi_ok[n], 1)

            def evac(use, bank, gb):
                kind, idx, nxt = use
                n = gb + nxt
                if kind == "Q":
                    e.wait_ge(S.q_mm, n * SLOTS + (idx + 1))
                    e.activation(q_sb[:, idx // HG % 2, idx % HG, :], ps_pr[bank][:], ACT.Identity,
                                 bias=bq_c[:, idx:idx + 1]).then_inc(S.q_ev, 1)
                elif kind == "K":
                    e.wait_ge(S.k_mm, n * SLOTS + (idx + 1))
                    e.activation(k_sb[:, idx // HG % 2, idx % HG, :, 0:Q], ps_pr[bank][:].rearrange("p (a c) -> p a c", c=Q),
                                 ACT.Identity, bias=bk_c[:, idx:idx + 1]).then_inc(S.k_ev, 1)
                elif kind == "X":
                    dst = h_hi if idx < 2 else c_hi
                    t = 256 * (idx % 2)
                    e.wait_ge(S.x_mm, n * 4 + (idx + 1))
                    e.activation(dst[:, :, t:t + 256], ps_pr[bank][:].rearrange("p (c t) -> p c t", c=DC), ACT.Copy).then_inc(S.x_hi_ev, 1)

            def z_step(i, r, prev, nxt):
                z_exp(i, r % 2, 0)
                if prev:
                    z_ptev(i - 1)
                if nxt:
                    z_evac_m(i + 1)
                z_exp(i, r % 2, 1)
                if nxt:
                    z_evac_v(i + 1, (r + 1) % 2, r == 0)

            z_step(0, 0, False, True)
            with e.Fori(0, ZPAIRS // 2 - 3) as g:
                for r in range(1, 3):
                    z_step(g * 2 + r, r, True, True)
            for i in range(ZPAIRS - 5, ZPAIRS):
                z_step(i, i, True, i + 1 < ZPAIRS)
                if i >= ZPAIRS - GROUPS:
                    split_high("q", i - (ZPAIRS - GROUPS), 0)
            for u in FIRST_X[0:2]:
                evac(u, first_plan[u][0], 0)
            z_ptev(ZPAIRS - 1)
            for u in FIRST_X[2:4]:
                evac(u, first_plan[u][0], 0)


            def act_slot(gb, s, first, last, layer, plan, uses, work=True):
                B = gb * SLOTS

                def exponentials():
                    if work:
                        e.wait_ge(S.sub_done, B + (s + 1))
                        e.activation(s_sb[:], s_sb[:], ACT.Exp, scale=SCALE).then_inc(S.exp_done, 1)

                sparse = last and s >= SPARSE
                if not sparse:
                    exponentials()
                    for u in uses[0]:
                        evac(u, plan[u][0], gb)
                if not (first and s == 0):
                    e.wait_ge(S.t_done, B + s)
                    if not (first and s == 1):
                        e.wait_ge(S.pv_done, B + (s - 1))
                    e.activation(pt_sb[:], ps_t[:], ACT.Copy).then_inc(S.pt_ev, 1)
                if sparse:
                    exponentials()
                if not (first and s == 0):
                    if s in (0, SLOTS):
                        nb = gb if s == 0 else gb + 1
                        e.wait_ge(S.pbt_done, nb)
                        e.activation(pbt_sb[0:H + 1, :], ps_c[0:H + 1, :], ACT.Copy).then_inc(S.pbt_hi, 1)
                for u in uses[1]:
                    evac(u, plan[u][0], gb)
                if not (first and s == 0):
                    e.wait_ge(S.pv_done, B + s)
                    if not (first and s == 1):
                        e.wait_ge(S.o_done, B + (s - 1))
                    e.activation(cx_hi[:], ps_c[:], ACT.Copy).then_inc(S.cxhi_done, 1)
                    if s % SLOTS == 0:
                        e.wait_ge(S.pbt_hi, gb + s // SLOTS)
                        e.activation(pbt_sb[64:64 + H + 1, :], pbt_sb[0:H + 1, :].bitcast(F32), ACT.Copy).then_inc(S.pbt_copied, 1)
                for u in uses[2]:
                    evac(u, plan[u][0], gb)
                for n, group in split_now(s, first, last):
                    split_high(n, group, layer + 1 if last else layer)

            def act_block(gb, first, last, layer):
                for s in range(SLOTS):
                    act_slot(gb, s, first, last, layer, plans[last], projections(s, last))

            with e.Fori(0, LAYERS) as layer:
                g0 = layer * BLOCKS
                for n, group in TOP_SPLITS:
                    split_high(n, group, layer)
                e.wait_ge(S.prm_ok, layer + 1)
                for u in [("Q", 0, 0), ("Q", 1, 0)] + PROLOGUE:
                    evac(u, first_plan[u][0], g0)
                    if u in PROLOGUE_SPLITS:
                        split_high(*PROLOGUE_SPLITS[u], layer)
                act_block(g0, True, False, layer)
                with e.Fori(1, BLOCKS - 1) as b:
                    act_block(b + g0, False, False, layer)
                act_block(g0 + (BLOCKS - 1), False, True, layer)
                act_slot(g0 + (BLOCKS - 1), SLOTS, False, True, layer, None, [[], [], []], work=False)

            def m_xhi(b, i):
                e.wait_ge(S.m_x, b * 2 + (i - 1))
                e.activation(h_hi[:, :, 256 * i:256 * i + 256], ps_pr[i][:].rearrange("p (c t) -> p c t", c=DC), ACT.Copy).then_inc(S.m_xhi, 1)

            def m_gelu(b, first):
                for j in range(FT):
                    if first and j < 2:
                        e.wait_ge(S.q_mm, LAYERS * BLOCKS * SLOTS + (j + 1))
                    else:
                        e.wait_ge(S.m_fc1, b * FT + (j - 1))
                    if not (first and j < 4):
                        e.wait_ge(S.m_glo, b * FT + (j - 3))
                    e.activation(g_raw[:, j % 4, :], ps_pr[j % 2][:], ACT.Gelu, bias=prm[:, j:j + 1]).then_inc(S.m_gelu, 1)
                    e.wait_ge(S.m_gelu, b * FT + (j + 1))
                    e.activation(g_hi[:, j, :], g_raw[:, j % 4, :], ACT.Copy).then_inc(S.m_ghi, 1)

            e.wait_ge(S.prm_ok, LAYERS + 1)
            m_gelu(0, True)
            with e.Fori(1, BLOCKS) as b:
                m_xhi(b, 0)
                m_xhi(b, 1)
                m_gelu(b, False)

        @block.vector
        def _(e):
            for half in range(2):
                e.memset(z_w[64 * half:64 * half + 64, :, 64 * (1 - half):64 * (1 - half) + 64], 0.0).then_inc(S.z_zero, 1)

            def z_stats(g, r):
                i, k, par = g * ZX + r, r % ZX, r % 2
                e.wait_ge(z_ld[r % ZS], g * (ZX // ZS * 32) + (r // ZS + 1) * 32)
                ge(e, S.z_mvd, i)
                e.bn_stats(z_st6[:, 0, :], z_x[:, k, :])
                e.bn_stats(z_st6[:, 1, :], z_s[:, r % ZS, :]).then_inc(S.z_st, 1)
                ge_apart(e, S.z_st, i + 1, S.apart_dve)
                e.bn_aggr(z_mv[:, par, 0, :], z_st6[:, 0, :])
                e.bn_aggr(z_mv[:, par, 1, :], z_st6[:, 1, :]).then_inc(S.z_mvd, 1)

            def z_normalise(g, r):
                i, k, par = g * ZX + r, r % ZX, r % 2
                e.wait_ge(S.z_rsd, i + 1)
                ge(e, S.z_s1, i)
                e.tensor_scalar(z_xn[:], z_x[:, k, :], z_mv[:, par, 0, 0:1], z_rs[:, par, 0:1], ALU.subtract, ALU.mult).then_inc(S.z_norm_x, 1)

            def z_max(i, b):
                e.wait_ge(S.z_l, i * 2 + (b + 1))
                e.reduce_max(z_nmx[:, b, :], ps_l[:, b, :].rearrange("p (a s) -> p a s", a=2), AX.X, negate=True).then_inc(S.z_nmx_ok, 1)

            def z_probs(i, par, b):
                e.wait_ge(S.z_exp, i * 2 + (b + 1))
                e.reciprocal(z_rc[:, b, :], z_sum[:, b, :]).then_inc(S.z_rec, 1)
                e.wait_ge(S.z_rec, i * 2 + (b + 1))
                for tc in range(2):
                    ins = e.tensor_scalar(z_p[:, par, b, tc, :], z_p[:, par, b, tc, :], z_rc[:, b, tc:tc + 1], None, ALU.mult)
                ins.then_inc(S.z_normd, 1)

            def z_ptev(i):
                e.wait_ge(S.z_t, i * 2 + 1)
                e.tensor_copy(z_pt[:, 0].rearrange("p a t -> p (a t)"), ps_t[:]).then_inc(S.z_pt_ev0, 1)

            def z_final(g, r):
                i, k = g * ZX + r, r % ZX
                e.wait_ge(S.z_pv, i + 1)
                ge(e, z_so[k % 2], (g * (ZX // 2) + r // 2) * 16)
                e.scalar_tensor_tensor(out=z_o[:, k % 2, :], in0=ps_o[0][:, 0:256], scalar=z_c[:, 0:1], in1=z_x[:, k, :],
                                       op0=ALU.add, op1=ALU.add).then_inc(S.z_outd, 1)

            plans = {last: block_plan(last) for last in (False, True)}
            first_plan = first_block_plan()

            def evac(use, bank, gb):
                kind, idx, nxt = use
                n = gb + nxt
                if kind == "V":
                    e.wait_ge(S.v_mm, n * SLOTS + (idx + 1))
                    e.tensor_copy(v_sb[:, idx % PAIRS, :], ps_pr[bank][:]).then_inc(S.v_ev, 1)
                elif kind == "X":
                    hi, lo = (h_hi, h_lo) if idx < 2 else (c_hi, c_lo)
                    t = 256 * (idx % 2)
                    e.wait_ge(S.x_hi_ev, n * 4 + (idx + 1))
                    e.tensor_tensor(lo[:, :, t:t + 256], ps_pr[bank][:].rearrange("p (c t) -> p c t", c=DC),
                                    hi[:, :, t:t + 256].bitcast(F32), ALU.subtract).then_inc(S.x_ev, 1)

            def ln_stats(gb, p):
                if p == 0:
                    e.wait_ge(S.x_ld, gb * 16 + 16)
                ins = e.bn_stats(st6[:, p, :], x_st[:, p, :])
                if p == PAIRS - 1:
                    ins.then_inc(S.st_done, 1)

            def ln_mean(gb):
                ge_apart(e, S.st_done, gb + 1, S.apart_dve)
                for p in range(PAIRS):
                    ins = e.bn_aggr(mv[:, p, :], st6[:, p, :])
                ins.then_inc(S.mv_done, 1)

            def ln_normalise(gb):
                e.wait_ge(S.rs_done, gb + 1)
                for p in range(PAIRS):
                    ins = e.tensor_scalar(x_st[:, p, :], x_st[:, p, :], mv[:, p, 0:1], rstd[:, p:p + 1], ALU.subtract, ALU.mult)
                ins.then_inc(S.xn_done, 1)

            def parameters(stage):
                e.wait_ge(S.rows_t, stage + 1)
                e.tensor_copy(prm[:], ps_t[:, 0:5 * H]).then_inc(S.prm_ok, 1)

            def split_low(n, group, stage):
                e.wait_ge(w_hi_ok[n], stage * GROUPS + (group + 1))
                e.tensor_tensor(w_lo[n][:, group, :], w_raw[n][:, group, :], w_hi[n][:, group, :].bitcast(F32), ALU.subtract).then_inc(w_ok[n], 1)

            def z_step(g, r, prev, nxt2):
                i = g * ZX + r
                z_max(i, 0)
                if prev:
                    z_probs(i - 1, (r - 1) % 2, 1)
                z_max(i, 1)
                if prev:
                    z_ptev(i - 1)
                if nxt2:
                    z_stats(g, r + 2)
                z_probs(i, r % 2, 0)
                if prev:
                    z_final(g, r - 1)
                if nxt2:
                    z_normalise(g, r + 2)

            z_stats(0, 0)
            z_stats(0, 1)
            z_normalise(0, 0)
            z_normalise(0, 1)
            e.wait_ge(S.z_bias, 1)
            for i in range(3):
                z_step(0, i, i > 0, True)
            with e.Fori(0, ZPAIRS // ZX - 1) as g:
                for r in range(3, 3 + ZX):
                    z_step(g, r, True, True)
            for i in range(ZPAIRS - 5, ZPAIRS):
                if i == ZPAIRS - 4:
                    for p in range(PAIRS):
                        ln_stats(0, p)
                    ln_mean(0)
                elif i == ZPAIRS - 3:
                    ln_normalise(0)
                z_step(0, i, True, i + 2 < ZPAIRS)
            z_probs(ZPAIRS - 1, 1, 1)
            z_ptev(ZPAIRS - 1)
            for u in FIRST_X[0:2]:
                evac(u, first_plan[u][0], 0)
            z_final(0, ZPAIRS - 1)
            for u in FIRST_X[2:4]:
                evac(u, first_plan[u][0], 0)
            parameters(0)

            def x_out(gb):
                e.wait_ge(S.fin_done, gb + 1)
                e.wait_ge(S.res_ld, gb * 16 + 16)
                for i in range(2):
                    dst = x_st[:, 2 * i:2 * i + 2, :].rearrange("p a d -> p (a d)")
                    ins = e.tensor_tensor(dst, ps_o[i][:], dst, ALU.add)
                ins.then_inc(S.xout_done, 1)

            def logits(b):
                r = slice(64 * b, 64 * b + 64)
                return ps_l[r, :, 0:4 * KEYS].rearrange("p a (h c) -> p a h c", h=2)[:, :, :, KEYS * b:KEYS * b + KEYS]

            def dve_slot(gb, s, first, last, layer, plan, uses, work=True):
                B = gb * SLOTS
                if work:
                    hg, p = s // PAIRS, s % PAIRS
                    e.wait_ge(S.qk_done, B + (s + 1))
                    for b in range(2):
                        r = slice(64 * b, 64 * b + 64)
                        ins = e.reduce_max(mx[r, :].rearrange("p (a h) -> p a h", a=2), logits(b), AX.X)
                    ins.then_inc(S.max_done, 1)
                    e.wait_ge(S.max_done, B + (s + 1))
                    for b in range(2):
                        r = slice(64 * b, 64 * b + 64)
                        top = mx[r, :].rearrange("p (a h) -> p a h", a=2).unsqueeze(3).to_broadcast([64, 2, 2, KEYS])
                        ins = e.tensor_tensor(s_sb[r, :, :].rearrange("p (a h) c -> p a h c", a=2), logits(b), top, ALU.subtract)
                    ins.then_inc(S.sub_done, 1)
                if s == 1 and not first:
                    x_out(gb - 1)
                if work:
                    e.wait_ge(S.exp_done, B + (s + 1))
                    e.reduce_sum(sm, s_sb[:], AX.X).then_inc(S.sum_done, 1)
                    e.wait_ge(S.sum_done, B + (s + 1))
                    e.reciprocal(rc, sm).then_inc(S.rec_done, 1)
                    e.wait_ge(S.rec_done, B + (s + 1))
                    if not (first and s == 0):
                        e.wait_ge(S.t_done, B + s)
                    for b in range(2):
                        r = slice(64 * b, 64 * b + 64)
                        e.tensor_tensor(p_sb[r, :, 64 * b:64 * b + 64], s_sb[r, :, 0:Q],
                                        rc[r, :].unsqueeze(2).to_broadcast([64, HG, Q]), ALU.mult)
                    if s == 0 and not first:
                        e.wait_ge(S.pbt_done, gb)
                    e.tensor_tensor(pb_sb[:, p, HG * hg:HG * hg + HG], s_sb[:, :, Q], rc, ALU.mult).then_inc(S.norm_done, 1)
                late = [u for u in uses[1] if u == ("V", s + 3, 0)]
                for u in uses[0] + uses[1]:
                    if u not in late:
                        evac(u, plan[u][0], gb)
                if s % SLOTS == 0 and not (first and s == 0):
                    e.wait_ge(S.pbt_hi, gb + s // SLOTS)
                    e.tensor_tensor(pbt_sb[32:32 + H + 1, :], ps_c[0:H + 1, :], pbt_sb[0:H + 1, :].bitcast(F32), ALU.subtract).then_inc(S.pbt_ev, 1)
                if not (first and s == 0):
                    e.wait_ge(S.cxhi_done, B + s)
                    e.tensor_tensor(cx_lo[:], ps_c[:], cx_hi[:].bitcast(F32), ALU.subtract).then_inc(S.cxlo_done, 1)
                for u in late + uses[2]:
                    evac(u, plan[u][0], gb)
                if first and s == 0:
                    e.wait_ge(S.bw_mm, layer + 1)
                    e.tensor_copy(bw_sb[0:H + 1, :], ps_c[0:H + 1, 0:D]).then_inc(S.bw_hi, 1)
                    e.wait_ge(S.bw_hi, layer + 1)
                    e.tensor_copy(bw_sb[32:32 + H + 1, :], ps_c[0:H + 1, 0:D])
                    e.tensor_tensor(bw_sb[64:64 + H + 1, :], ps_c[0:H + 1, 0:D], bw_sb[0:H + 1, :].bitcast(F32), ALU.subtract).then_inc(S.bw_ok, 1)
                if work:
                    if 4 <= s < 8:
                        ln_stats(gb + 1, s - 4)
                    elif s == 8:
                        ln_mean(gb + 1)
                    elif s == 9:
                        ln_normalise(gb + 1)

            def dve_block(gb, first, last, layer):
                for s in range(SLOTS):
                    dve_slot(gb, s, first, last, layer, plans[last], projections(s, last))

            with e.Fori(0, LAYERS) as layer:
                g0 = layer * BLOCKS
                for n, group in TOP_SPLITS:
                    split_low(n, group, layer)
                e.memset(lmat[:], 0.0).then_inc(S.l_zero, 1)
                e.wait_ge(S.l_zero, layer + 1)
                e.wait_ge(S.prm_ok, layer + 1)
                e.tensor_tensor(lmat[:].rearrange("p h c -> p (h c)")[:, 0:H * (H + 1):H + 2],
                                prm[:, 3 * H:4 * H], prm[:, 4 * H:5 * H], ALU.subtract)
                e.tensor_copy(lmat[:, :, H], prm[:, 4 * H:5 * H]).then_inc(S.lmat_ok, 1)
                for u in PROLOGUE:
                    evac(u, first_plan[u][0], g0)
                    if u in PROLOGUE_SPLITS:
                        split_low(*PROLOGUE_SPLITS[u], layer)
                dve_block(g0, True, False, layer)
                with e.Fori(1, BLOCKS - 1) as b:
                    dve_block(b + g0, False, False, layer)
                gl = g0 + (BLOCKS - 1)
                dve_block(gl, False, True, layer)
                dve_slot(gl, SLOTS, False, True, layer, None, [[], [], []], work=False)
                parameters(layer + 1)
                x_out(gl)

            def m_stats(b):
                e.wait_ge(S.m_xld, b * 16)
                for p in range(PAIRS):
                    ins = e.bn_stats(st6[:, p, :], kv_st[:, p, :])
                ins.then_inc(S.m_st, 1)
                ge_apart(e, S.m_st, b, S.apart_dve)
                for p in range(PAIRS):
                    ins = e.bn_aggr(mv[:, p, :], st6[:, p, :])
                ins.then_inc(S.m_mv, 1)

            def m_normalise(b):
                e.wait_ge(S.m_rs, b)
                for p in range(PAIRS):
                    ins = e.tensor_scalar(kv_st[:, p, :], kv_st[:, p, :], mv[:, p, 0:1], rstd[:, p:p + 1], ALU.subtract, ALU.mult)
                ins.then_inc(S.m_xn, 1)

            def m_xlo(b):
                for i in range(2):
                    t = 256 * i
                    e.wait_ge(S.m_xhi, b * 2 + (i - 1))
                    e.tensor_tensor(h_lo[:, :, t:t + 256], ps_pr[i][:].rearrange("p (c t) -> p c t", c=DC),
                                    h_hi[:, :, t:t + 256].bitcast(F32), ALU.subtract).then_inc(S.m_xlo, 1)

            def m_split(b, j):
                e.wait_ge(S.m_ghi, b * FT + (j + 1))
                e.tensor_tensor(g_lo[:, j, :], g_raw[:, j % 4, :], g_hi[:, j, :].bitcast(F32), ALU.subtract).then_inc(S.m_glo, 1)

            def m_outs(b, norm_next):
                e.wait_ge(S.m_res, b + 1)
                for i in range(2):
                    e.wait_ge(S.m_fc2, b * 2 + (i + 1))
                    dst = x_st[:, 2 * i:2 * i + 2, :].rearrange("p a d -> p (a d)")
                    e.tensor_tensor(dst, ps_o[i][:], dst, ALU.add).then_inc(S.m_out, 1)
                    if i == 0 and norm_next:
                        m_normalise(b + 2)

            def m_block(b, b1, b2, first=False):
                for j in range(FT):
                    m_split(b, j)
                    if first and j == 3:
                        m_stats(1)
                    if first and j == 5:
                        m_normalise(1)
                if b1:
                    m_xlo(b + 1)
                if b2:
                    m_stats(b + 2)
                m_outs(b, b2)

            m_block(0, True, True, True)
            with e.Fori(1, BLOCKS - 2) as b:
                m_block(b, True, True)
            m_block(BLOCKS - 2, True, False)
            m_block(BLOCKS - 1, False, False)

        @block.tensor
        def _(e):
            e.wait_ge(S.ident_ok, 1)
            e.wait_ge(S.z_zero, 2)
            e.wait_ge(S.z_wld, 2 * 16)
            for n in range(4):
                ins = e.transpose(ps_pr[0][:, P * n:P * n + P], z_w[:, n, :], ident[:])
            ins.then_inc(S.z_wt_mm, 1)
            e.wait_ge(S.z_wt_ev, 1)
            e.wait_ge(S.z_bld, 2 * 16)
            e.matmul(ps_pr[1][:, 0:P], z_w[:, 2, :], z_wt[:, 3, :], start=True, stop=True)
            e.matmul(ps_pr[1][:, P:P + 1], z_wt[:, 3, :], z_b[:, 2:3], start=True, stop=True).then_inc(S.z_wl_mm, 1)
            e.wait_ge(S.z_wl_ev, 1)
            e.wait_ge(S.z_bias, 1)

            def z_project_x(i):
                e.wait_ge(S.z_norm_x, i + 1)
                e.matmul(ps_pr[0][:, 0:256], z_wt[:, 0, :], z_xn[:], start=True, stop=True)

            def z_project_s(i, r, first):
                e.wait_ge(S.z_norm_s, i + 1)
                e.matmul(ps_pr[0][:, 256:512], z_wt[:, 1, :], z_sn[:], start=True, stop=True).then_inc(S.z_s1, 1)
                if not first:
                    e.wait_ge(S.z_v_ev, i)
                for sc in range(2):
                    ins = e.matmul(ps_pr[1][:, P * sc:P * sc + P], z_s[:, r % ZS, P * sc:P * sc + P], z_wt[:, 2, :], start=True, stop=True)
                ins.then_inc(S.z_vmm, 1)

            def z_logits(i, first):
                e.wait_ge(S.z_m_ev, i + 1)
                for b in range(2):
                    if not first:
                        e.wait_ge(S.z_exp, i * 2 + (b - 1))
                    for tc in range(2):
                        ins = e.matmul(ps_l[:, b, 256 * tc:256 * tc + 256], z_mn[:, b, P * tc:P * tc + P], z_mm[:], start=True, stop=True)
                    ins.then_inc(S.z_l, 1)

            def z_transposes(i, par, first):
                for b in range(2):
                    e.wait_ge(S.z_normd, i * 2 + (b + 1))
                    if not first:
                        e.wait_ge(z_pt_ev[b], i)
                    dst = ps_t if b == 0 else ps_c
                    for sc in range(2):
                        for tc in range(2):
                            o = 256 * sc + P * tc
                            ins = e.transpose(dst[:, o:o + P], z_p[:, par, b, tc, P * sc:P * sc + P], ident[:])
                    ins.then_inc(S.z_t, 1)

            def z_values(i, k, first):
                e.wait_ge(S.z_v_ev, i + 1)
                for b in range(2):
                    e.wait_ge(z_pt_ev[b], i + 1)
                if not first:
                    e.wait_ge(S.z_outd, i)
                for b in range(2):
                    for sc in range(2):
                        ins = e.matmul(ps_o[0][64 * b:64 * b + 64, 0:256], z_v[:, k, sc, 64 * b:64 * b + 64], z_pt[:, b, sc, :],
                                       start=(sc == 0), stop=(sc == 1))
                ins.then_inc(S.z_pv, 1)

            plans = {last: block_plan(last) for last in (False, True)}
            first_plan = first_block_plan()

            def three(dst, pairs, inc=None):
                terms = [t for (a_hi, a_lo), (b_hi, b_lo) in pairs for t in ((a_hi, b_hi), (a_hi, b_lo), (a_lo, b_hi))]
                for n, (a, b) in enumerate(terms):
                    ins = e.matmul(dst, a, b, start=(n == 0), stop=(n == len(terms) - 1))
                if inc is not None:
                    ins.then_inc(inc, 1)

            def cols(n, c, idx):
                o = HG * K * c + K * (idx % HG)
                return w_hi[n][:, idx // HG, o:o + K], w_lo[n][:, idx // HG, o:o + K]

            def project(use, plan, gb, layer=None):
                kind, idx, nxt = use
                bank, before = plan[use]
                n = gb + nxt
                if before is not None:
                    sem, count = evac_of(before, gb)
                    e.wait_ge(sem, count)
                dst = ps_pr[bank][:]
                group = idx // HG
                if kind in "QKV" and idx % HG == 0 and layer is not None:
                    e.wait_ge(w_ok[kind.lower()], layer * GROUPS + (group + 1))
                if kind == "X":
                    src = x_st if idx < 2 else kv_st
                    if idx == 0:
                        e.wait_ge(S.xh_done, n + 1)
                    if idx == 2:
                        e.wait_ge(S.kv_ld, n * 16 + 16)
                    for c in range(DC):
                        for j in range(2):
                            o = 256 * c + P * j
                            ins = e.transpose(ps_pr[bank][:, o:o + P], src[:, 2 * (idx % 2) + j, P * c:P * c + P], ident[:])
                    ins.then_inc(S.x_mm, 1)
                    return
                if kind in "QK":
                    if idx == 0:
                        e.wait_ge(S.x_ev, n * 4 + (2 if kind == "Q" else 4))
                    w, sem = ("q", S.q_mm) if kind == "Q" else ("k", S.k_mm)
                    hi, lo = (h_hi, h_lo) if kind == "Q" else (c_hi, c_lo)
                    three(dst, [(cols(w, c, idx), (hi[:, c, :], lo[:, c, :])) for c in range(DC)], sem)
                else:
                    if idx == 0:
                        e.wait_ge(S.x_ev, n * 4 + 4)
                    t = slice(P * (idx % PAIRS), P * (idx % PAIRS) + P)
                    cols_v = [slice(HG * K * c, HG * K * c + HG * K) for c in range(DC)]
                    three(dst, [((c_hi[:, c, t], c_lo[:, c, t]), (w_hi["v"][:, group, cols_v[c]], w_lo["v"][:, group, cols_v[c]]))
                                for c in range(DC)], S.v_mm)

            def transpose_rows(stage):
                e.wait_ge(S.rows_ld, stage * 16 + 16)
                e.transpose(ps_t[:, 0:5 * H], rows_sb[0:5 * H, :], ident[0:5 * H, 0:5 * H]).then_inc(S.rows_t, 1)

            def z_step(i, r, nxt):
                z_logits(i, r == 0)
                if nxt:
                    z_project_x(i + 1)
                if r > 0:
                    z_transposes(i - 1, (r - 1) % 2, r == 1)
                if nxt:
                    z_project_s(i + 1, r + 1, False)
                if r > 0:
                    z_values(i - 1, (r - 1) % 2, r == 1)

            z_project_x(0)
            z_project_s(0, 0, True)
            for i in range(2):
                z_step(i, i, True)
            with e.Fori(0, ZPAIRS // ZS - 1) as g:
                for r in range(2, 2 + ZS):
                    z_step(g * ZS + r, r, True)
            for i in range(ZPAIRS - 2, ZPAIRS):
                z_step(i, i, i + 1 < ZPAIRS)
            e.wait_ge(S.z_m_ev, ZPAIRS)
            e.wait_ge(S.z_v_ev, ZPAIRS)
            for u in FIRST_X[0:2]:
                project(u, first_plan, 0)
            z_transposes(ZPAIRS - 1, 1, False)
            z_values(ZPAIRS - 1, 1, False)
            for u in FIRST_X[2:4]:
                project(u, first_plan, 0)
            e.wait_ge(S.z_outd, ZPAIRS)
            transpose_rows(0)
            for u in [("Q", 0, 0), ("Q", 1, 0)]:
                project(u, first_plan, 0, 0)

            def o_slot(gb, s, first, layer):
                hg, p = s // PAIRS % GROUPS, s % PAIRS
                B = gb * SLOTS
                if p == 0 and layer is not None:
                    e.wait_ge(S.wo_ok, layer * GROUPS + (hg + 1))
                e.wait_ge(S.cxlo_done, B + (s + 1))
                if s == 0 and not first:
                    e.wait_ge(S.xout_done, gb)
                dst = ps_o[p // 2][:, D * (p % 2):D * (p % 2) + D]
                for hh in range(HG):
                    col = slice(P * hh, P * hh + P)
                    for n, (a, b) in enumerate(((cx_hi, w_hi["o"]), (cx_hi, w_lo["o"]), (cx_lo, w_hi["o"]))):
                        ins = e.matmul(dst, a[:, col], b[:, hg, D * hh:D * hh + D], start=(hg == 0 and p % 2 == 0 and hh == 0 and n == 0),
                                       stop=False, skip_group_check=True)
                ins.then_inc(S.o_done, 1)

            def pe_slot(gb, s, first, plan, uses, layer=None, next_layer=None, work=True, sparse=False):
                B = gb * SLOTS
                hg, p, par = s // PAIRS, s % PAIRS, s // PAIRS % 2
                if work:
                    if p == 0:
                        e.wait_ge(S.q_ev, B + (PAIRS * hg + HG))
                        e.wait_ge(S.k_ev, B + (PAIRS * hg + HG))
                        e.wait_ge(S.bias_col, gb * GROUPS + (hg + 1))
                    if not (first and s == 0):
                        e.wait_ge(S.sub_done, B + s)
                    for hh in range(HG):
                        o = 2 * KEYS * (hh % 2)
                        ins = e.matmul(ps_l[:, hh // 2, o:o + 2 * KEYS], q_sb[:, par, hh, P * p:P * p + P],
                                       k_sb[:, par, hh, 2 * p:2 * p + 2, :].rearrange("p a c -> p (a c)"), start=True, stop=True)
                    ins.then_inc(S.qk_done, 1)
                def output_part():
                    if not (first and s < 2):
                        o_slot(gb if s >= 2 else gb - 1, s - 2 if s >= 2 else s + 14, first, layer)
                    if s == SLOTS + 1 or (s == 1 and not first):
                        e.wait_ge(S.pbt_copied, gb + s // SLOTS)
                        for pp in range(PAIRS):
                            ins = e.matmul(ps_o[pp // 2][:, D * (pp % 2):D * (pp % 2) + D], pbt_sb[:, P * pp:P * pp + P], bw_sb[:],
                                           start=False, stop=True, skip_group_check=True)
                        ins.then_inc(S.fin_done, 1)

                if not sparse:
                    output_part()
                for u in uses[0]:
                    project(u, plan, gb, next_layer if u[2] else layer)
                if not (first and s == 0) and s <= SLOTS:
                    e.wait_ge(S.norm_done, B + s)
                    if not (first and s == 1):
                        e.wait_ge(S.pt_ev, B + (s - 1))
                    for hh in range(HG):
                        ins = e.transpose(ps_t[:, P * hh:P * hh + P], p_sb[:, hh, :], ident[:])
                    ins.then_inc(S.t_done, 1)
                if s % SLOTS == 0 and not (first and s == 0):
                    e.wait_ge(S.cxlo_done, B + (s - 1))
                    for pp in range(PAIRS):
                        ins = e.transpose(ps_c[0:H + 1, P * pp:P * pp + P], pb_sb[:, pp, :], ident[:])
                    ins.then_inc(S.pbt_done, 1)
                if sparse:
                    output_part()
                for u in uses[1]:
                    project(u, plan, gb, next_layer if u[2] else layer)
                if first and s == 0:
                    e.wait_ge(S.bo_ld, layer * 16 + 16)
                    e.wait_ge(S.lmat_ok, layer + 1)
                    e.wait_ge(S.wo_ld, (layer + 1) * 16 * GROUPS)
                    for k in range(2):
                        e.wait_ge(z_so[k], 16 * ZPAIRS // 2)
                    for h in range(H):
                        ins = e.matmul(ps_c[0:H + 1, 0:D], lmat[:, h, :], w_raw["o"][:, h // HG, D * (h % HG):D * (h % HG) + D],
                                       start=(h == 0), stop=False)
                    e.matmul(ps_c[0:H + 1, 0:D], onehot[:], bo_row[:], start=False, stop=True).then_inc(S.bw_mm, 1)
                if first and s == 1:
                    e.wait_ge(S.bw_ok, layer + 1)
                if not (first and s == 0) and s <= SLOTS:
                    e.wait_ge(S.pt_ev, B + s)
                    e.wait_ge(S.v_ev, B + s)
                    if s % SLOTS == 0:
                        e.wait_ge(S.pbt_ev, gb + s // SLOTS)
                    pp = (s - 1) % PAIRS
                    for hh in range(HG):
                        col = slice(P * hh, P * hh + P)
                        ins = e.matmul(ps_c[:, col], v_sb[:, pp, K * hh:K * hh + K], pt_sb[:, col], start=True, stop=True)
                    ins.then_inc(S.pv_done, 1)
                for u in uses[2]:
                    project(u, plan, gb, next_layer if u[2] else layer)

            def pe_block(gb, first, last, layer=None):
                for s in range(SLOTS):
                    pe_slot(gb, s, first, plans[last], projections(s, last), layer, sparse=last and s >= SPARSE)

            with e.Fori(0, LAYERS) as layer:
                g0 = layer * BLOCKS
                for u in PROLOGUE:
                    project(u, first_plan, g0, layer)
                pe_block(g0, True, False, layer)
                with e.Fori(1, BLOCKS - 1) as b:
                    pe_block(b + g0, False, False)
                gl = g0 + (BLOCKS - 1)
                pe_block(gl, False, True)
                pe_slot(gl, SLOTS, False, plans[True], [[EARLY[SLOTS]], [], []], next_layer=layer + 1, work=False, sparse=True)
                e.wait_ge(S.pt_ev, gl * SLOTS + SLOTS)
                transpose_rows(layer + 1)
                pe_slot(gl, SLOTS + 1, False, plans[True], [[EARLY[SLOTS + 1]], [], []], next_layer=layer + 1, work=False, sparse=True)

            def m_fc1(b, j):
                if j < 2:
                    e.wait_ge(S.m_xlo, b * 2)
                else:
                    e.wait_ge(S.m_gelu, b * FT + (j - 1))
                three(ps_pr[j % 2][:], [(cols("q", c, j), (h_hi[:, c, :], h_lo[:, c, :])) for c in range(DC)], S.m_fc1)

            def m_transposes(b, i):
                if i == 0:
                    e.wait_ge(S.m_xh, b)
                e.wait_ge(S.m_gelu, b * FT + (i - 1))
                for c in range(DC):
                    for j in range(2):
                        o = 256 * c + P * j
                        ins = e.transpose(ps_pr[i][:, o:o + P], kv_st[:, 2 * i + j, P * c:P * c + P], ident[:])
                ins.then_inc(S.m_x, 1)

            def m_fc2(b, p, tiles):
                t = slice(P * p, P * p + P)
                for j in tiles:
                    w2 = [w["q"][:, 2 + j // HG, D * (j % HG):D * (j % HG) + D] for w in (w_hi, w_lo)]
                    for n, (g, w) in enumerate(((g_hi, w2[0]), (g_hi, w2[1]), (g_lo, w2[0]))):
                        ins = e.matmul(ps_o[p // 2][:, D * (p % 2):D * (p % 2) + D], g[:, j, t], w,
                                       start=(j == 0 and n == 0), stop=(j == FT - 1 and n == 2))
                if p % 2 and tiles[-1] == FT - 1:
                    ins.then_inc(S.m_fc2, 1)

            def m_block(b, first, last):
                for j in range(2 if first else 0, FT):
                    m_fc1(b, j)
                if first:
                    e.wait_ge(S.xout_done, LAYERS * BLOCKS)
                else:
                    e.wait_ge(S.m_out, b * 2)
                e.wait_ge(S.m_glo, b * FT + (FT - 2))
                m_fc2(b, 0, range(FT - 2))
                for j in (FT - 2, FT - 1):
                    e.wait_ge(S.m_glo, b * FT + (j + 1))
                    m_fc2(b, 0, range(j, j + 1))
                for p in range(1, PAIRS):
                    if p == (2 if first else 1) and not last:
                        m_transposes(b + 1, 0)
                        m_transposes(b + 1, 1)
                    m_fc2(b, p, range(FT))

            e.wait_ge(S.wq_ok, (LAYERS + 1) * GROUPS)
            m_block(0, True, False)
            with e.Fori(1, BLOCKS - 1) as b:
                m_block(b, False, False)
            m_block(BLOCKS - 1, False, True)


def kernel(**inputs):
    import numpy as np
    import concourse.bacc as bacc
    from concourse.bass_utils import run_bass_kernel_spmd

    a = {k: np.asarray(v) for k, v in inputs.items()}
    z = lambda n: a["L0_xattn_" + n]
    w = lambda n: a["L1_xattn_" + n]
    heads = lambda n: w(n).reshape(H, K)
    grouped = lambda m: m.reshape(DC, P, -1, HG * K).transpose(1, 2, 0, 3).reshape(P, -1)
    by_rows = lambda m: m.reshape(-1, P, D).transpose(1, 0, 2).reshape(P, -1)
    arrays = {
        "x": a["x"].reshape(BATCH * Q, D),
        "ctx": a["ctx_2048"].reshape(BATCH * Q, D),
        "zw": np.stack([z("Wn"), z("Wm"), z("Wl"), z("Wo")]),
        "zb": np.stack([z("bn"), z("bm"), z("bl"), z("bo")], axis=1),
        "weights": np.stack([part for i in (1, 2) for part in (grouped(w(f"wq{i}")), grouped(w(f"wk{i}")), grouped(w(f"wv{i}")),
                                                               by_rows(w(f"wo{i}")))]
                            + [np.concatenate([grouped(w("w_fc1")), by_rows(w("w_fc2"))], axis=1)]),
        "rows": np.stack([np.concatenate([heads(f"{n}{i}") for n in ("bq", "bk", "bias_k", "bias_v", "bv")]) for i in (1, 2)]
                         + [np.concatenate([w("b_fc1").reshape(FT, P), np.zeros((5 * H - FT, P), np.float32)])]),
        "ln": np.stack([np.stack([w(f"{n}_scale"), w(f"{n}_offset")]) for n in ("ln1", "ln2", "ln_mlp")]),
        "bo": np.stack([w("bo1"), w("bo2")]),
        "b2": w("b_fc2"),
    }
    arrays = {k: np.ascontiguousarray(v) for k, v in arrays.items()}
    nc = bacc.Bacc("TRN2", target_bir_lowering=False, num_devices=1)
    args = {k: nc.dram_tensor(k, v.shape, mybir.dt.from_np(v.dtype), kind="ExternalInput").ap() for k, v in arrays.items()}
    out = nc.dram_tensor("out", (BATCH * Q, D), F32, kind="ExternalOutput").ap()
    build(nc, out=out, **args)
    r = run_bass_kernel_spmd(nc, [arrays], core_ids=[0])
    return r.results[0]["out"].reshape(BATCH, Q, D)
```
